# Optimizing a Trainium2 kernel written in Bass

```python
import numpy as np
import jax
import jax.numpy as jnp

def _softmax(x, axis=-1):
    return jax.nn.softmax(x, axis=axis)

def _gelu(x):
    return jax.nn.gelu(x, approximate=True)

def _silu(x):
    return jax.nn.silu(x)

def _sigmoid(x):
    return jax.nn.sigmoid(x)

def _layernorm(x, axis=-1, eps=1e-05):
    m = jnp.mean(x, axis=axis, keepdims=True)
    v = jnp.var(x, axis=axis, keepdims=True)
    return (x - m) / jnp.sqrt(v + eps)

def _scatter_add(tgt, idx, src, axis=0):
    return tgt.at[idx].add(src)

def _segment_sum(src, seg, n):
    return jax.ops.segment_sum(src, seg, n)
kernel_name = 'mk_gps_d2_gnn_r8_07d691'

def setup_inputs(seed: int=0):
    np.random.seed(seed)
    _w = jnp.asarray

    def _rec_inputs():
        import jax
        import jax.numpy as jnp
        _gk = jax.random.key(seed)
        x = -0.0003542 + 1 * jax.random.normal(jax.random.fold_in(_gk, 1), (2000, 256), jnp.float32)
        src = jax.random.randint(jax.random.fold_in(_gk, 2), (64000,), 0, 2000, jnp.int32)
        dst = jax.random.randint(jax.random.fold_in(_gk, 3), (64000,), 0, 2000, jnp.int32)
        _o = jnp.argsort(dst, stable=True)
        src = src[_o]
        dst = dst[_o]
        edge_attr_128 = 4.82035e-05 + 0.999966 * jax.random.normal(jax.random.fold_in(_gk, 11), (64000, 128), jnp.float32)
        edge_attr_16 = -0.000153872 + 1.00011 * jax.random.normal(jax.random.fold_in(_gk, 12), (64000, 16), jnp.float32)
        edge_attr_4 = 0.0007022 + 0.999661 * jax.random.normal(jax.random.fold_in(_gk, 13), (64000, 4), jnp.float32)
        edge_weight = jax.random.uniform(jax.random.fold_in(_gk, 16), (64000,), jnp.float32, 0.0, 0.999951)
        return (x, src, dst, edge_attr_128, edge_attr_16, edge_attr_4, edge_weight)
    x, src, dst, edge_attr_128, edge_attr_16, edge_attr_4, edge_weight = _rec_inputs()

    def _L0_gnn_setup():
        import jax, jax.numpy as jnp
        import numpy as np
        BN_EPS = 1e-05

        def _bn(x, gamma, beta, mean, var):
            return (x - mean) / jnp.sqrt(var + BN_EPS) * gamma + beta
        key = jax.random.key(seed)
        ks = jax.random.split(key, 24)
        N, E = (2000, 8000)
        D_IN, H, D_OUT, D_E, KH = (256, 64, 256, 128, 32)
        s = 0.05
        inp = {}
        inp['x'] = jax.random.normal(ks[0], (N, D_IN), jnp.float32)
        inp['edge_input'] = jax.random.normal(ks[1], (E, D_E), jnp.float32)
        inp['edge_list'] = jax.random.randint(ks[2], (E, 2), 0, N, jnp.int32)
        inp['edge_weight'] = jax.random.uniform(ks[3], (E,), jnp.float32)
        inp['w1'] = jax.random.normal(ks[4], (D_IN, H), jnp.float32) * s
        inp['b1'] = jax.random.normal(ks[5], (H,), jnp.float32) * s
        inp['kw1'] = jax.random.normal(ks[6], (D_E, KH), jnp.float32) * s
        inp['kb1'] = jax.random.normal(ks[7], (KH,), jnp.float32) * s
        inp['kw2'] = jax.random.normal(ks[8], (KH, (H + 1) * H), jnp.float32) * s
        inp['kb2'] = jax.random.normal(ks[9], ((H + 1) * H,), jnp.float32) * s
        inp['w2'] = jax.random.normal(ks[10], (H, D_OUT), jnp.float32) * s
        inp['b2'] = jax.random.normal(ks[11], (D_OUT,), jnp.float32) * s

        def bn_params(k, d):
            k1, k2, k3, k4 = jax.random.split(k, 4)
            g = 1.0 + jax.random.normal(k1, (d,), jnp.float32) * s
            b = jax.random.normal(k2, (d,), jnp.float32) * s
            m = jax.random.normal(k3, (d,), jnp.float32) * s
            v = 0.5 + jax.random.uniform(k4, (d,), jnp.float32)
            return (g, b, m, v)
        inp['g_in'], inp['be_in'], inp['m_in'], inp['v_in'] = bn_params(ks[12], D_IN)
        inp['g_msg'], inp['be_msg'], inp['m_msg'], inp['v_msg'] = bn_params(ks[13], H)
        inp['g_upd'], inp['be_upd'], inp['m_upd'], inp['v_upd'] = bn_params(ks[14], H)
        inp['g_out'], inp['be_out'], inp['m_out'], inp['v_out'] = bn_params(ks[15], D_OUT)
        return inp
    _L0_gnn_all = _L0_gnn_setup()
    _L0_gnn_in = {k: v for k, v in _L0_gnn_all.items() if k in ('w1', 'b1', 'kw1', 'kb1', 'kw2', 'kb2', 'w2', 'b2', 'g_in', 'be_in', 'm_in', 'v_in', 'g_msg', 'be_msg', 'm_msg', 'v_msg', 'g_upd', 'be_upd', 'm_upd', 'v_upd', 'g_out', 'be_out', 'm_out', 'v_out')}
    del _L0_gnn_all

    def _L0_mix_setup():
        import jax, jax.numpy as jnp
        import numpy as np
        MIDC = 256
        HEADS = 8
        HEADC = MIDC // HEADS
        EPS = 1e-05

        def _ln(x, gamma, beta):
            mu = jnp.mean(x, axis=-1, keepdims=True)
            var = jnp.var(x, axis=-1, keepdims=True)
            return (x - mu) * jax.lax.rsqrt(var + EPS) * gamma + beta
        key = jax.random.key(seed)
        ks = jax.random.split(key, 8)
        B, HW, C = (8, 512, MIDC)
        s = 1.0 / np.sqrt(C)
        return {'x': jax.random.normal(ks[0], (B, HW, C), jnp.float32), 'w_qkv': jax.random.normal(ks[1], (C, 3 * C), jnp.float32) * s, 'b_qkv': jnp.zeros((3 * C,), jnp.float32), 'kln_g': jnp.ones((HEADC,), jnp.float32), 'kln_b': jnp.zeros((HEADC,), jnp.float32), 'vln_g': jnp.ones((HEADC,), jnp.float32), 'vln_b': jnp.zeros((HEADC,), jnp.float32), 'w1': jax.random.normal(ks[2], (C, C), jnp.float32) * s, 'b1': jnp.zeros((C,), jnp.float32), 'w2': jax.random.normal(ks[3], (C, C), jnp.float32) * s, 'b2': jnp.zeros((C,), jnp.float32)}
    _L0_mix_all = _L0_mix_setup()
    _L0_mix_in = {k: v for k, v in _L0_mix_all.items() if k in ('w_qkv', 'b_qkv', 'kln_g', 'kln_b', 'vln_g', 'vln_b', 'w1', 'b1', 'w2', 'b2')}
    del _L0_mix_all

    def _L0_ffn_setup():
        import jax, jax.numpy as jnp
        import numpy as np
        IN_CH = 256
        OUT_CH = 256
        key = jax.random.key(seed)
        kx, kw, kb = jax.random.split(key, 3)
        x = jax.random.normal(kx, (8, 512, IN_CH), dtype=jnp.float32)
        bound = 1.0 / np.sqrt(IN_CH)
        weight = jax.random.uniform(kw, (OUT_CH, IN_CH), dtype=jnp.float32, minval=-bound, maxval=bound)
        bias = jax.random.uniform(kb, (OUT_CH,), dtype=jnp.float32, minval=-bound, maxval=bound)
        return {'x': x, 'weight': weight, 'bias': bias}
    _L0_ffn_all = _L0_ffn_setup()
    _L0_ffn_in = {k: v for k, v in _L0_ffn_all.items() if k in ('weight', 'bias')}
    del _L0_ffn_all

    def _L1_gnn_setup():
        import jax, jax.numpy as jnp
        import numpy as np
        N, E, C, R, HID = (6250, 62500, 64, 16, 64)
        key = jax.random.key(seed)
        ks = jax.random.split(key, 24)
        g = lambda k, shape, s=1.0: jax.random.normal(k, shape, dtype=jnp.float32) * s
        cs = C ** (-0.5)
        inp = {'h': g(ks[0], (N, 4 * C)), 'edge_index': jax.random.randint(ks[1], (2, E), 0, N), 'edge_sh': g(ks[2], (E, 4)), 'edge_rbf': g(ks[3], (E, R)), 'W_up0': g(ks[4], (C, C), cs), 'W_up1': g(ks[5], (C, C), cs), 'M1': g(ks[6], (R, HID), R ** (-0.5)), 'M2': g(ks[7], (HID, HID), HID ** (-0.5)), 'M3': g(ks[8], (HID, HID), HID ** (-0.5)), 'M4': g(ks[9], (HID, 4 * C), HID ** (-0.5)), 'W_lin0': g(ks[10], (C, C), cs), 'W_lin1': g(ks[11], (C, C), cs), 'Wsc0': g(ks[12], (C, C), cs), 'Wsc1': g(ks[13], (C, C), cs), 'Wc0': g(ks[14], (C, 5)), 'Wc1': g(ks[15], (C, 4)), 'WB0': g(ks[16], (C, C), cs), 'WB1': g(ks[17], (C, C), cs), 'gamma0': jnp.ones((C,), jnp.float32), 'beta0': jnp.zeros((C,), jnp.float32), 'gamma1': jnp.ones((C,), jnp.float32)}
        return inp
    _L1_gnn_all = _L1_gnn_setup()
    _L1_gnn_in = {k: v for k, v in _L1_gnn_all.items() if k in ('W_up0', 'W_up1', 'M1', 'M2', 'M3', 'M4', 'W_lin0', 'W_lin1', 'Wsc0', 'Wsc1', 'Wc0', 'Wc1', 'WB0', 'WB1', 'gamma0', 'beta0', 'gamma1')}
    del _L1_gnn_all

    def _L1_mix_setup():
        import jax, jax.numpy as jnp
        import numpy as np
        HEADS = 8
        DIM_HEAD = 64
        EPS = 1e-05

        def _inst_norm_lastdim(t):
            mu = jnp.mean(t, axis=-1, keepdims=True)
            var = jnp.mean(jnp.square(t - mu), axis=-1, keepdims=True)
            return (t - mu) * jax.lax.rsqrt(var + EPS)
        key = jax.random.key(seed)
        k1, k2, k3, k4 = jax.random.split(key, 4)
        b, n, dim = (4, 1024, 256)
        inner = HEADS * DIM_HEAD
        x = jax.random.normal(k1, (b, n, dim), dtype=jnp.float32)
        Wqkv = jax.random.normal(k2, (3 * inner, dim), dtype=jnp.float32) * (1.0 / np.sqrt(dim))
        Wout = jax.random.normal(k3, (dim, inner), dtype=jnp.float32) * (1.0 / np.sqrt(inner))
        bout = jax.random.normal(k4, (dim,), dtype=jnp.float32) * 0.01
        return {'x': x, 'Wqkv': Wqkv, 'Wout': Wout, 'bout': bout}
    _L1_mix_all = _L1_mix_setup()
    _L1_mix_in = {k: v for k, v in _L1_mix_all.items() if k in ('Wqkv', 'Wout', 'bout')}
    del _L1_mix_all

    def _L1_ffn_setup():
        import jax, jax.numpy as jnp
        import numpy as np
        B, S, D = (8, 512, 256)
        H = 4 * D
        CAPACITY = 0.5
        key = jax.random.key(seed)
        ks = jax.random.split(key, 6)
        x = jax.random.normal(ks[0], (B, S, D), dtype=jnp.float32)
        attention_mask = jnp.zeros((B, 1, 1, S), dtype=jnp.float32)
        wr = jax.random.normal(ks[1], (D, 1), dtype=jnp.float32) * 0.02
        br = jnp.zeros((1,), dtype=jnp.float32)
        w1 = jax.random.normal(ks[2], (D, H), dtype=jnp.float32) * 0.02
        b1 = jnp.zeros((H,), dtype=jnp.float32)
        w2 = jax.random.normal(ks[3], (H, D), dtype=jnp.float32) * 0.02
        b2 = jnp.zeros((D,), dtype=jnp.float32)
        return {'x': x, 'attention_mask': attention_mask, 'wr': wr, 'br': br, 'w1': w1, 'b1': b1, 'w2': w2, 'b2': b2}
    _L1_ffn_all = _L1_ffn_setup()
    _L1_ffn_in = {k: v for k, v in _L1_ffn_all.items() if k in ('attention_mask', 'wr', 'br', 'w1', 'b1', 'w2', 'b2')}
    del _L1_ffn_all
    return {'x': x, 'src': src, 'dst': dst, 'edge_attr_128': edge_attr_128, 'edge_attr_16': edge_attr_16, 'edge_attr_4': edge_attr_4, 'edge_weight': edge_weight, 'L0_gnn_w1': _L0_gnn_in['w1'], 'L0_gnn_b1': _L0_gnn_in['b1'], 'L0_gnn_kw1': _L0_gnn_in['kw1'], 'L0_gnn_kb1': _L0_gnn_in['kb1'], 'L0_gnn_kw2': _L0_gnn_in['kw2'], 'L0_gnn_kb2': _L0_gnn_in['kb2'], 'L0_gnn_w2': _L0_gnn_in['w2'], 'L0_gnn_b2': _L0_gnn_in['b2'], 'L0_gnn_g_in': _L0_gnn_in['g_in'], 'L0_gnn_be_in': _L0_gnn_in['be_in'], 'L0_gnn_m_in': _L0_gnn_in['m_in'], 'L0_gnn_v_in': _L0_gnn_in['v_in'], 'L0_gnn_g_msg': _L0_gnn_in['g_msg'], 'L0_gnn_be_msg': _L0_gnn_in['be_msg'], 'L0_gnn_m_msg': _L0_gnn_in['m_msg'], 'L0_gnn_v_msg': _L0_gnn_in['v_msg'], 'L0_gnn_g_upd': _L0_gnn_in['g_upd'], 'L0_gnn_be_upd': _L0_gnn_in['be_upd'], 'L0_gnn_m_upd': _L0_gnn_in['m_upd'], 'L0_gnn_v_upd': _L0_gnn_in['v_upd'], 'L0_gnn_g_out': _L0_gnn_in['g_out'], 'L0_gnn_be_out': _L0_gnn_in['be_out'], 'L0_gnn_m_out': _L0_gnn_in['m_out'], 'L0_gnn_v_out': _L0_gnn_in['v_out'], 'L0_mix_w_qkv': _L0_mix_in['w_qkv'], 'L0_mix_b_qkv': _L0_mix_in['b_qkv'], 'L0_mix_kln_g': _L0_mix_in['kln_g'], 'L0_mix_kln_b': _L0_mix_in['kln_b'], 'L0_mix_vln_g': _L0_mix_in['vln_g'], 'L0_mix_vln_b': _L0_mix_in['vln_b'], 'L0_mix_w1': _L0_mix_in['w1'], 'L0_mix_b1': _L0_mix_in['b1'], 'L0_mix_w2': _L0_mix_in['w2'], 'L0_mix_b2': _L0_mix_in['b2'], 'L0_ffn_weight': _L0_ffn_in['weight'], 'L0_ffn_bias': _L0_ffn_in['bias'], 'L1_gnn_W_up0': _L1_gnn_in['W_up0'], 'L1_gnn_W_up1': _L1_gnn_in['W_up1'], 'L1_gnn_M1': _L1_gnn_in['M1'], 'L1_gnn_M2': _L1_gnn_in['M2'], 'L1_gnn_M3': _L1_gnn_in['M3'], 'L1_gnn_M4': _L1_gnn_in['M4'], 'L1_gnn_W_lin0': _L1_gnn_in['W_lin0'], 'L1_gnn_W_lin1': _L1_gnn_in['W_lin1'], 'L1_gnn_Wsc0': _L1_gnn_in['Wsc0'], 'L1_gnn_Wsc1': _L1_gnn_in['Wsc1'], 'L1_gnn_Wc0': _L1_gnn_in['Wc0'], 'L1_gnn_Wc1': _L1_gnn_in['Wc1'], 'L1_gnn_WB0': _L1_gnn_in['WB0'], 'L1_gnn_WB1': _L1_gnn_in['WB1'], 'L1_gnn_gamma0': _L1_gnn_in['gamma0'], 'L1_gnn_beta0': _L1_gnn_in['beta0'], 'L1_gnn_gamma1': _L1_gnn_in['gamma1'], 'L1_mix_Wqkv': _L1_mix_in['Wqkv'], 'L1_mix_Wout': _L1_mix_in['Wout'], 'L1_mix_bout': _L1_mix_in['bout'], 'L1_ffn_attention_mask': _L1_ffn_in['attention_mask'], 'L1_ffn_wr': _L1_ffn_in['wr'], 'L1_ffn_br': _L1_ffn_in['br'], 'L1_ffn_w1': _L1_ffn_in['w1'], 'L1_ffn_b1': _L1_ffn_in['b1'], 'L1_ffn_w2': _L1_ffn_in['w2'], 'L1_ffn_b2': _L1_ffn_in['b2']}

def reference(x, src, dst, edge_attr_128, edge_attr_16, edge_attr_4, edge_weight, L0_gnn_w1, L0_gnn_b1, L0_gnn_kw1, L0_gnn_kb1, L0_gnn_kw2, L0_gnn_kb2, L0_gnn_w2, L0_gnn_b2, L0_gnn_g_in, L0_gnn_be_in, L0_gnn_m_in, L0_gnn_v_in, L0_gnn_g_msg, L0_gnn_be_msg, L0_gnn_m_msg, L0_gnn_v_msg, L0_gnn_g_upd, L0_gnn_be_upd, L0_gnn_m_upd, L0_gnn_v_upd, L0_gnn_g_out, L0_gnn_be_out, L0_gnn_m_out, L0_gnn_v_out, L0_mix_w_qkv, L0_mix_b_qkv, L0_mix_kln_g, L0_mix_kln_b, L0_mix_vln_g, L0_mix_vln_b, L0_mix_w1, L0_mix_b1, L0_mix_w2, L0_mix_b2, L0_ffn_weight, L0_ffn_bias, L1_gnn_W_up0, L1_gnn_W_up1, L1_gnn_M1, L1_gnn_M2, L1_gnn_M3, L1_gnn_M4, L1_gnn_W_lin0, L1_gnn_W_lin1, L1_gnn_Wsc0, L1_gnn_Wsc1, L1_gnn_Wc0, L1_gnn_Wc1, L1_gnn_WB0, L1_gnn_WB1, L1_gnn_gamma0, L1_gnn_beta0, L1_gnn_gamma1, L1_mix_Wqkv, L1_mix_Wout, L1_mix_bout, L1_ffn_attention_mask, L1_ffn_wr, L1_ffn_br, L1_ffn_w1, L1_ffn_b1, L1_ffn_w2, L1_ffn_b2):
    import jax
    import jax.numpy as jnp

    def _L0_gnn_ref(x, edge_input, edge_list, edge_weight, w1, b1, kw1, kb1, kw2, kb2, w2, b2, g_in, be_in, m_in, v_in, g_msg, be_msg, m_msg, v_msg, g_upd, be_upd, m_upd, v_upd, g_out, be_out, m_out, v_out):
        import jax, jax.numpy as jnp
        import numpy as np
        BN_EPS = 1e-05

        def _bn(x, gamma, beta, mean, var):
            return (x - mean) / jnp.sqrt(var + BN_EPS) * gamma + beta
        N = x.shape[0]
        H = w1.shape[1]
        node_in = edge_list[:, 0]
        node_out = edge_list[:, 1]
        xn = _bn(x, g_in, be_in, m_in, v_in)
        layer_input = jax.nn.relu(xn)
        msg = layer_input[node_in] @ w1 + b1
        msg = jax.nn.relu(_bn(msg, g_msg, be_msg, m_msg, v_msg))
        kern = jax.nn.relu(edge_input @ kw1 + kb1) @ kw2 + kb2
        kern = kern.reshape(-1, H + 1, H)
        msg = jnp.einsum('ejk,ek->ej', kern[:, 1:, :], msg) + kern[:, 0, :]
        update = jax.ops.segment_sum(msg * edge_weight[:, None], node_out, num_segments=N)
        update = jax.nn.relu(_bn(update, g_upd, be_upd, m_upd, v_upd))
        out = update @ w2 + b2
        out = _bn(out, g_out, be_out, m_out, v_out)
        return out

    def _L0_mix_ref(x, w_qkv, b_qkv, kln_g, kln_b, vln_g, vln_b, w1, b1, w2, b2):
        import jax, jax.numpy as jnp
        import numpy as np
        MIDC = 256
        HEADS = 8
        HEADC = MIDC // HEADS
        EPS = 1e-05

        def _ln(x, gamma, beta):
            mu = jnp.mean(x, axis=-1, keepdims=True)
            var = jnp.var(x, axis=-1, keepdims=True)
            return (x - mu) * jax.lax.rsqrt(var + EPS) * gamma + beta
        B, HW, C = x.shape
        bias = x
        qkv = (x @ w_qkv + b_qkv).reshape(B, HW, HEADS, 3 * HEADC)
        qkv = qkv.transpose(0, 2, 1, 3)
        q, k, v = jnp.split(qkv, 3, axis=-1)
        k = _ln(k, kln_g, kln_b)
        v = _ln(v, vln_g, vln_b)
        kv = jnp.einsum('bhnd,bhne->bhde', k, v) / HW
        out = jnp.einsum('bhnd,bhde->bhne', q, kv)
        out = out.transpose(0, 2, 1, 3).reshape(B, HW, C)
        ret = out + bias
        h = jax.nn.gelu(ret @ w1 + b1, approximate=False)
        return h @ w2 + b2 + bias

    def _L0_ffn_ref(x, weight, bias):
        import jax, jax.numpy as jnp
        import numpy as np
        IN_CH = 256
        OUT_CH = 256
        return jnp.einsum('bsi,oi->bso', x, weight) + bias

    def _L1_gnn_ref(h, edge_index, edge_sh, edge_rbf, W_up0, W_up1, M1, M2, M3, M4, W_lin0, W_lin1, Wsc0, Wsc1, Wc0, Wc1, WB0, WB1, gamma0, beta0, gamma1):
        import jax, jax.numpy as jnp
        import numpy as np
        N, E, C, R, HID = (6250, 62500, 64, 16, 64)
        n = h.shape[0]
        h0 = h[:, :C]
        h1 = h[:, C:].reshape(n, C, 3)
        up0 = h0 @ W_up0
        up1 = jnp.einsum('ncx,cd->ndx', h1, W_up1)
        r = jax.nn.silu(edge_rbf @ M1)
        r = jax.nn.silu(r @ M2)
        r = jax.nn.silu(r @ M3)
        tpw = (r @ M4).reshape(-1, 4, C)
        snd, rcv = (edge_index[0], edge_index[1])
        x0 = up0[snd]
        x1 = up1[snd]
        sh0 = edge_sh[:, 0]
        sh1 = edge_sh[:, 1:]
        inv3 = 1.0 / jnp.sqrt(jnp.float32(3.0))
        m0e = tpw[:, 0] * x0 * sh0[:, None] + tpw[:, 3] * jnp.einsum('ecx,ex->ec', x1, sh1) * inv3
        m1e = tpw[:, 1][:, :, None] * x0[:, :, None] * sh1[:, None, :] + tpw[:, 2][:, :, None] * x1 * sh0[:, None, None]
        msg0 = jax.ops.segment_sum(m0e, rcv, num_segments=n)
        msg1 = jax.ops.segment_sum(m1e, rcv, num_segments=n)
        A0 = msg0 @ W_lin0
        A1 = jnp.einsum('ncx,cd->ndx', msg1, W_lin1)
        sc0 = h0 @ Wsc0
        sc1 = jnp.einsum('ncx,cd->ndx', h1, Wsc1)
        vv = jnp.sum(A1 * A1, -1)
        B0 = Wc0[:, 0] * A0 + Wc0[:, 1] * A0 * A0 + Wc0[:, 2] * vv + Wc0[:, 3] * A0 ** 3 + Wc0[:, 4] * A0 * vv
        B1 = (Wc1[:, 0] + Wc1[:, 1] * A0 + Wc1[:, 2] * A0 * A0 + Wc1[:, 3] * vv)[..., None] * A1
        o0 = B0 @ WB0 + sc0
        o1 = jnp.einsum('ncx,cd->ndx', B1, WB1) + sc1
        eps = jnp.float32(1e-05)
        mu = jnp.mean(o0, 0)
        xc = o0 - mu
        var = jnp.mean(xc * xc, 0)
        n0 = xc * jax.lax.rsqrt(var + eps) * gamma0 + beta0
        nrm1 = jnp.mean(jnp.sum(o1 * o1, -1) / 3.0, 0)
        n1 = o1 * (jax.lax.rsqrt(nrm1 + eps) * gamma1)[None, :, None]
        return jnp.concatenate([n0, n1.reshape(n, 3 * C)], -1)

    def _L1_mix_ref(x, Wqkv, Wout, bout):
        import jax, jax.numpy as jnp
        import numpy as np
        HEADS = 8
        DIM_HEAD = 64
        EPS = 1e-05

        def _inst_norm_lastdim(t):
            mu = jnp.mean(t, axis=-1, keepdims=True)
            var = jnp.mean(jnp.square(t - mu), axis=-1, keepdims=True)
            return (t - mu) * jax.lax.rsqrt(var + EPS)
        b, n, dim = x.shape
        qkv = jnp.einsum('bnc,fc->bnf', x, Wqkv)
        q, k, v = jnp.split(qkv, 3, axis=-1)

        def to_heads(t):
            return t.reshape(b, n, HEADS, DIM_HEAD).transpose(0, 2, 1, 3)
        q, k, v = (to_heads(q), to_heads(k), to_heads(v))
        k = _inst_norm_lastdim(k)
        v = _inst_norm_lastdim(v)
        dots = jnp.einsum('bhnd,bhne->bhde', k, v)
        out = jnp.einsum('bhnd,bhde->bhne', q, dots) / n
        out = out.transpose(0, 2, 1, 3).reshape(b, n, HEADS * DIM_HEAD)
        return jnp.einsum('bnf,cf->bnc', out, Wout) + bout

    def _L1_ffn_ref(x, attention_mask, wr, br, w1, b1, w2, b2):
        import jax, jax.numpy as jnp
        import numpy as np
        B, S, D = (8, 512, 256)
        H = 4 * D
        CAPACITY = 0.5
        b, s, d = x.shape
        weights = (jnp.einsum('bsd,do->bso', x, wr) + br)[..., 0]
        k = max(1, int(CAPACITY * s))
        kk = k - 1 if k > 1 else 1
        _, idx = jax.lax.top_k(weights, k)
        sel_idx = idx[:, :kk]
        sel = jnp.take_along_axis(x, sel_idx[:, :, None], axis=1)
        h = jax.nn.gelu(jnp.einsum('bkd,dh->bkh', sel, w1) + b1)
        y = jnp.einsum('bkh,hd->bkd', h, w2) + b2
        w_sel = jnp.take_along_axis(weights, sel_idx, axis=1)
        y = y * w_sel[..., None]
        batch_idx = jnp.arange(b)[:, None]
        processed = jnp.zeros_like(x).at[batch_idx, sel_idx].set(y)
        return processed + x
    edge_index = jnp.stack([src, dst])
    edge_index_t = jnp.stack([src, dst], axis=1)
    xn = _layernorm(x, axis=-1)
    x = x + _L0_gnn_ref(xn, edge_attr_128, edge_index_t, edge_weight, L0_gnn_w1, L0_gnn_b1, L0_gnn_kw1, L0_gnn_kb1, L0_gnn_kw2, L0_gnn_kb2, L0_gnn_w2, L0_gnn_b2, L0_gnn_g_in, L0_gnn_be_in, L0_gnn_m_in, L0_gnn_v_in, L0_gnn_g_msg, L0_gnn_be_msg, L0_gnn_m_msg, L0_gnn_v_msg, L0_gnn_g_upd, L0_gnn_be_upd, L0_gnn_m_upd, L0_gnn_v_upd, L0_gnn_g_out, L0_gnn_be_out, L0_gnn_m_out, L0_gnn_v_out) + _L0_mix_ref(xn[None], L0_mix_w_qkv, L0_mix_b_qkv, L0_mix_kln_g, L0_mix_kln_b, L0_mix_vln_g, L0_mix_vln_b, L0_mix_w1, L0_mix_b1, L0_mix_w2, L0_mix_b2)[0]
    x = x + _L0_ffn_ref(_layernorm(x, axis=-1)[None], L0_ffn_weight, L0_ffn_bias)[0]
    xn = _layernorm(x, axis=-1)
    x = x + _L1_gnn_ref(xn, edge_index, edge_attr_4, edge_attr_16, L1_gnn_W_up0, L1_gnn_W_up1, L1_gnn_M1, L1_gnn_M2, L1_gnn_M3, L1_gnn_M4, L1_gnn_W_lin0, L1_gnn_W_lin1, L1_gnn_Wsc0, L1_gnn_Wsc1, L1_gnn_Wc0, L1_gnn_Wc1, L1_gnn_WB0, L1_gnn_WB1, L1_gnn_gamma0, L1_gnn_beta0, L1_gnn_gamma1) + _L1_mix_ref(xn[None], L1_mix_Wqkv, L1_mix_Wout, L1_mix_bout)[0]
    x = x + _L1_ffn_ref(_layernorm(x, axis=-1)[None], L1_ffn_attention_mask, L1_ffn_wr, L1_ffn_br, L1_ffn_w1, L1_ffn_b1, L1_ffn_w2, L1_ffn_b2)[0]
    return x

_drawn_inputs = setup_inputs


def setup_inputs(seed=0):
    import zlib

    import numpy as np

    out = dict(_drawn_inputs(seed))
    spreads = {'L0_mix_b_qkv': (0.0, 0.1),
     'L0_mix_kln_g': (1.0, 0.6),
     'L0_mix_kln_b': (0.0, 0.485),
     'L0_mix_vln_g': (1.0, 0.6),
     'L0_mix_vln_b': (0.0, 0.43),
     'L0_mix_b1': (0.0, 0.1),
     'L0_mix_b2': (0.0, 0.1),
     'L1_gnn_gamma0': (1.0, 0.592),
     'L1_gnn_beta0': (0.0, 0.466),
     'L1_gnn_gamma1': (1.0, 0.2),
     'L1_ffn_b1': (0.0, 0.8),
     'L1_ffn_b2': (0.0, 0.8)}
    factors = {'L0_gnn_be_upd': 5.106,
     'L0_gnn_m_upd': 4.439,
     'L1_gnn_Wsc0': 8.0,
     'L1_gnn_Wsc1': 4.978,
     'L1_mix_bout': 8.0,
     'L1_ffn_wr': 8.0,
     'L1_ffn_w1': 8.0,
     'L1_ffn_w2': 8.0}
    for name, (base, spread) in spreads.items():
        noise = np.random.default_rng([zlib.crc32(name.encode()), seed]).standard_normal(out[name].shape)
        drawn = base * np.exp(spread * noise) if base else spread * noise
        out[name] = jnp.asarray(drawn.astype(out[name].dtype))
    for name, factor in factors.items():
        out[name] = (out[name] * factor).astype(out[name].dtype)
    return out
```

```python
from contextlib import ExitStack

import concourse.bass as bass
from concourse import mybir

F32 = mybir.dt.float32
I32 = mybir.dt.int32
ALU = mybir.AluOpType
ACT = mybir.ActivationFunctionType
AX = mybir.AxisListType

P = 128
N, D, E = 2000, 256, 64000
NT = (N + P - 1) // P
NPAD = NT * P
LAST = N - (NT - 1) * P
ET = E // P
WIN = 8
NW = N + WIN
H = 64
KH = 32
GR = 5
BODY = 2 * GR
ITERS = ET // BODY
NG = 2 * ITERS + 1
MP = 3 * (ITERS + 1)
GE = GR * P
NCH = 500
EPS = 1e-5
SMALL = 1720
NA = 7
ARENA = 32352
RING = 7744
SEL = N // 2 - 1


class Area:

    def __init__(self, tensor, start, end):
        self.tensor, self.at, self.end = tensor, start, end

    def take(self, n):
        a = self.at
        self.at += n
        assert self.at <= self.end, (self.at, self.end)
        return self.tensor[:, a:a + n]


def build(nc, A, out):
    ctx = ExitStack()
    with ctx:
        def sb(name, cols, dt=F32, parts=P):
            return ctx.enter_context(nc.sbuf_tensor(name, [parts, cols], dt))

        def sem(name):
            return ctx.enter_context(nc.semaphore(name))

        arena = sb("arena", ARENA)
        ring = sb("ring", RING)
        XT = sb("XT", 2 * NPAD)[:, :].rearrange("p (k n) -> p k n", k=2)
        src = sb("src", ET, I32)
        dstF = sb("dstF", ET)
        ewt = sb("ewt", ET + GR)
        LO = sb("LO", ET)
        base = sb("base", ET)
        dloc = sb("dloc", ET + GR)
        baseI = sb("baseI", ET, I32, 1)
        vacc = sb("vacc", NW)
        curI = sb("curI", 2 * GR, I32)
        small = sb("small", SMALL)
        npassI = sb("npassI", 2, I32, 1)
        ps = ctx.enter_context(nc.psum_tensor("ps", [P, 8, 512], F32))

        sm = Area(small, 0, SMALL)
        ident = sm.take(P)
        iota8 = sm.take(WIN)
        st = sm.take(NT * 6).rearrange("p (t s) -> p t s", s=6)
        mv = sm.take(NT * 2).rearrange("p (t s) -> p t s", s=2)
        var = sm.take(NT)
        std = sm.take(NT)
        rs = sm.take(NT)
        bnv = sm.take(30).rearrange("p (v c) -> p v c", v=5)
        bns = sm.take(6)
        bnb = sm.take(6)
        bnt = sm.take(6)
        ones = sm.take(P)
        w1g = sm.take(2 * H).rearrange("p (k h) -> p k h", k=2)
        kw1 = sm.take(KH)
        kb1r = sm.take(GR * KH)
        w2g = sm.take(D)
        wV = sm.take(H)
        bq = sm.take(2)
        b1c = sm.take(2)
        b2c = sm.take(2)
        bfc = sm.take(2)
        boc = sm.take(2)
        bvec = sm.take(2)
        l1v = sm.take(6).rearrange("p (v c) -> p v c", v=3)
        mvo = sm.take(4).rearrange("p (k s) -> p k s", k=2)
        sto = sm.take(2 * 4 * 6).rearrange("p (k c s) -> p k c s", k=2, c=4)
        ss = sm.take(2)
        nrm = sm.take(2)
        osc = sm.take(2)
        obi = sm.take(2)
        brc = sm.take(1)
        fb1 = sm.take(8)
        wcol = sm.take(NT)
        cnt3 = sm.take(3 * NT).rearrange("p (c t) -> p c t", c=3)
        mw = sm.take(NT)
        wr = sm.take(2)
        wmean = sm.take(32)

        def rows(off):
            return arena[:, off:off + NT * D].rearrange("p (t d) -> p t d", d=D)

        def cols(off, k=2):
            return arena[:, off:off + k * NPAD].rearrange("p (k n) -> p k n", k=k)

        YT = cols(0)
        ROW = rows(4096)
        YROW = rows(8192)
        LT = cols(12288)
        H1T = LT
        MT = arena[0:H, 16384:16384 + NPAD]
        KC = arena[:, 18432:18432 + NT * 512].rearrange("p (t g c) -> p t g c", t=NT, c=32)
        MROW = arena[:, 26624:26624 + NT * H].rearrange("p (t h) -> p t h", h=H)
        SQ = arena[:, 27648:28672].rearrange("p (b c) -> p b c", b=2)
        a1 = Area(arena, 28672, 32256)
        wkv = a1.take(1024).rearrange("p (k c) -> p k c", k=2)
        wqT = a1.take(512).rearrange("p (k c) -> p k c", k=2)
        w1m = a1.take(512).rearrange("p (k c) -> p k c", k=2)
        w1p = a1.take(512).rearrange("p (k c) -> p k c", k=2)
        w2m = a1.take(512).rearrange("p (k c) -> p k c", k=2)
        mask32 = a1.take(P)
        VS = a1.take(NT * 16)
        r0 = Area(ring, 0, RING)
        MR = r0.take(BODY * (H + 1 + KH)).rearrange("p (s c) -> p s c", s=BODY)
        RM = r0.take(2 * GR * WIN * KH).rearrange("p (g t w q) -> p g t w q", g=2, t=GR, w=WIN)
        EA = r0.take(2 * GE).rearrange("p (g e) -> p g e", g=2)
        SW = r0.take(2 * GR * WIN).rearrange("p (g t w) -> p g t w", g=2, t=GR)
        W2S = sb("W2S", 16 * H)[:, :].rearrange("p (q j) -> p q j", q=16)
        wfT = sb("wfT", 512)[:, :].rearrange("p (k c) -> p k c", k=2)
        ru = r0.at
        U = ring[0:H, ru:ru + NPAD]
        gkv = r0.take(512)
        bkvr = r0.take(512)[0:1, :]
        bkv = r0.take(512)
        KVM = r0.take(2 * P).rearrange("p (g c) -> p g c", g=2)
        AM = r0.take(512).rearrange("p (g c) -> p g c", g=2)
        GM = r0.take(512).rearrange("p (g c) -> p g c", g=2)
        dr = arena[0:125, 0:512]
        drI = ring[0:125, 0:512].bitcast(I32)
        dstI = ring[:, 512:512 + ET].bitcast(I32)
        lohi = sm.take(8)
        span = sm.take(2)

        acc = arena[:, 0:NW * 16].rearrange("p (n q) -> p n q", q=16)

        KV1 = arena[:, 4096:4096 + NT * 1024].rearrange("p (t g c) -> p t g c", t=NT, c=64)
        a2 = Area(arena, 20480, 26752)
        wkv1 = a2.take(2048).rearrange("p (k c) -> p k c", k=2)
        wq1 = a2.take(1024).rearrange("p (k c) -> p k c", k=4)
        woT = a2.take(1024).rearrange("p (k c) -> p k c", k=4)
        bu = a2.take(256).rearrange("p (k c) -> p k c", k=2)
        mask64 = a2.take(P)
        a2.at = 26112
        m1 = a2.take(P)
        m2 = a2.take(P)
        m3 = a2.take(P)
        m4 = a2.take(D)
        UPR = rows(26752)
        SQ1 = arena[:, 30848:31872]
        r1a = Area(ring, 0, RING)
        KVM1 = r1a.take(4 * P).rearrange("p (g c) -> p g c", g=4)
        AM1 = r1a.take(1024).rearrange("p (g c) -> p g c", g=4)
        GM1 = r1a.take(512).rearrange("p (g c) -> p g c", g=2)
        VS1 = r1a.take(NT * 16)
        RK1 = r1a.take(NT * 8)

        acc1 = arena[:, 4096:4096 + NA * NPAD].rearrange("p (h n) -> p h n", h=NA)
        a3 = Area(arena, 4096 + NA * NPAD, 26112)
        G1 = a3.take(BODY * D).rearrange("p (s c) -> p s c", s=BODY)
        PP = a3.take(BODY * 8 * H).rearrange("p (s b c) -> p s b c", s=BODY, b=8)
        a3b = Area(arena, 26752, ARENA)
        R1 = a3b.take(GE)
        R2 = a3b.take(GE)
        R3 = a3b.take(GE)
        RBF = a3b.take(GE * 2).rearrange("p (g e) -> p g e", g=2)
        S4 = a3b.take(2 * GR * 4 * WIN).rearrange("p (g t k w) -> p g t k w", g=2, t=GR, k=4)
        OH = a3b.take(2 * GR * WIN).rearrange("p (g t w) -> p g t w", g=2, t=GR)
        shv = a3b.take(ET * 4).rearrange("p (t k) -> p t k", k=4)

        AR = arena[:, 18432:22528].rearrange("p (t b c) -> p t b c", b=4, c=64)
        BR = arena[:, 4096:8192].rearrange("p (t b c) -> p t b c", b=4, c=64)
        TMP = [arena[:, 8192 + 1024 * i:9216 + 1024 * i].rearrange("p (t c) -> p t c", c=64) for i in range(4)]
        BT = cols(12320)
        OT = cols(18432)
        HT = cols(12320, 8)
        WB = arena[:, 28704:28704 + NPAD]
        r4 = Area(ring, 2432, RING)
        wl = vacc[:, 0:NA * D].rearrange("p (h c) -> p h c", h=NA)
        bdb = r4.take(256).rearrange("p (k c) -> p k c", k=2)
        bds = r4.take(256).rearrange("p (k c) -> p k c", k=2)
        wc = r4.take(9 * 64).rearrange("p (v c) -> p v c", v=9)
        pat = r4.take(512).rearrange("p (a b c) -> p a b c", a=2, b=2)
        wrb = r4.take(256).rearrange("p (k c) -> p k c", k=2)
        ltm = r4.take(P)
        fb2 = r4.take(256)
        fw1 = ring[:, 0:2048].rearrange("p (k c) -> p k c", k=2)
        fw2 = r4.take(2048).rearrange("p (m c) -> p m c", m=8)
        OUTR = XT.rearrange("p k n -> p (k n)").rearrange("p (t d) -> p t d", d=D)
        junk = XT[:, 0, 0:N]

        mtab = nc.dram_tensor("mtab", [NPAD, H], F32, kind="Internal").ap()
        utab = nc.dram_tensor("utab", [NPAD, D], F32, kind="Internal").ap()
        lod = nc.dram_tensor("lod", [ET], F32, kind="Internal").ap()

        S = {n: sem(n) for n in (
            "s_zero", "s_idx", "s_const", "s_x", "s_w0", "s_lod", "s_lo", "s_npass", "s_dve", "s_act", "s_span",
            "s_bnvar", "s_bnstd", "s_bn", "s_lt", "s_msg", "s_mt", "s_mtr", "s_mrow", "s_mtab",
            "s_wc", "s_kv", "s_kvc", "s_kvr", "s_vs", "s_vstd", "s_kvn", "s_kvt", "s_kvm", "s_A", "s_Am",
            "s_G", "s_Gm", "s_bv", "s_bvm", "s_h1", "s_h1e", "s_mo", "s_xt0",
            "s_acc0p",
            "s_er", "s_rready", "s_mask", "s_seg", "s_rmw", "s_curI", "s_step", "s_base",
            "s_u", "s_ue", "s_o0", "s_w1", "s_ff", "s_up", "s_upr", "s_utab", "s_w4",
            "s_kv1", "s_k1c", "s_k1s", "s_v1r", "s_v1std", "s_v1n", "s_kvt1", "s_kvm1", "s_A1", "s_Am1", "s_G1", "s_Gm1",
            "s_y1", "s_xt3", "s_acc1", "s_mlp", "s_silu", "s_T", "s_prod", "s_seg1", "s_rmw1", "s_curI1", "s_oh",
            "s_ar", "s_are", "s_b", "s_bt", "s_bte", "s_o", "s_oe", "s_nr", "s_nre", "s_nvar", "s_nstd",
            "s_wb", "s_wbe", "s_wct", "s_wcol", "s_hh", "s_he", "s_yy", "s_out", "s_store", "s_base1")}
        lnr = [[sem(f"{w}{n}") for n in range(4)] for w in ("rowT", "row", "lnvar", "lnstd", "lny", "colT", "col", "xt")]
        rowT, row, lnvar, lnstd, lny, colT, col, xtd = lnr
        gath = [sem(f"gath{k}") for k in range(BODY)]
        eal = [sem(f"eal{k}") for k in range(2)]
        rbl = [sem(f"rbl{k}") for k in range(2)]

        block = ctx.enter_context(nc.Block())
        bcast = lambda ap, shape: ap.broadcast_to(shape)
        NLOAD = {}

        def outer(slot):
            return ps[:, 2 + slot % GR, 0:P]

        def affine(slot):
            return ps[0:H + 1 + KH, 2 + slot % GR, P:P + WIN]

        def sums(T):
            return ps[:, 6 + T % 2, 0:NA * WIN].rearrange("p (h w) -> p h w", h=NA)

        def weights_of(T):
            return ps[:, 2 + T % 4, 0:D]

        def vload(eng):
            eng.wait_ge(S["s_npass"], 1)
            return eng.value_load(npassI[0:1, 0:1], min_val=1, max_val=N // WIN + 1)

        @block.sync
        def _(sp):
            def ld(dst, a, s):
                NLOAD[s] = NLOAD.get(s, 0) + 1
                return sp.dma_start(dst, a).then_inc(S[s], 16)

            ld(drI, A["dst_r"], "s_idx")
            ld(dstI, A["dst_l"], "s_idx")
            sp.wait_ge(S["s_zero"], 2)
            ld(ROW[:, 0:NT - 1, :], A["x"][0:(NT - 1) * P, :].rearrange("(t p) d -> p t d", p=P), "s_x")
            ld(ROW[0:LAST, NT - 1, :], A["x"][(NT - 1) * P:N, :], "s_x")
            ld(ident, A["ident"], "s_const")
            ld(iota8, A["iota8"], "s_const")
            ld(bnv.rearrange("p v c -> p (v c)"), A["bnv"], "s_const")
            ld(ones, A["ones"], "s_const")
            ld(src[:, :], A["src_l"], "s_const")
            ld(ewt[:, 0:ET], A["ew"], "s_const")
            ld(mask32, A["mask32"], "s_const")
            ld(w1g.rearrange("p k h -> p (k h)"), A["w1g"], "s_const")
            for d_, n_ in ((kw1, "kw1"), (kb1r[0:1, :], "kb1r"), (w2g[0:H, :], "w2g"), (wV[0:H + 1 + KH, :], "wV"),
                           (bq, "bq"), (b1c, "b1c"), (b2c, "b2c"), (bfc, "bfc"), (boc, "boc"),
                           (l1v.rearrange("p v c -> p (v c)"), "l1v"), (brc, "brc"), (fb1, "fb1"), (wr, "wr"),
                           (bkvr, "bkvr"), (gkv, "gkv"), (bkv, "bkv"),
                           (wkv.rearrange("p k c -> p (k c)"), "wkv"), (wqT.rearrange("p k c -> p (k c)"), "wqT"),
                           (w1m.rearrange("p k c -> p (k c)"), "w1m"), (w1p.rearrange("p k c -> p (k c)"), "w1p"),
                           (w2m.rearrange("p k c -> p (k c)"), "w2m"), (W2S.rearrange("p q j -> p (q j)"), "W2S"),
                           (wfT.rearrange("p k c -> p (k c)"), "wfT")):
                ld(d_, A[n_], "s_w0")
            for k in range(2):
                ld(XT[:, k, 0:N], A["xT"][k * P:(k + 1) * P, :], "s_w0")
            sp.wait_ge(S["s_span"], 1)
            sp.dma_start(lod.rearrange("(p q) -> p q", q=4), lohi[0:125, 0:4]).then_inc(S["s_lod"], 16)
            sp.wait_ge(S["s_lod"], 16)
            sp.dma_start(LO[:, :], lod.rearrange("(a n) -> a n", a=1).broadcast_to([P, ET])).then_inc(S["s_lo"], 16)
            sp.wait_ge(S["s_mrow"], 2)
            sp.dma_start(mtab.rearrange("(t p) h -> p t h", p=P), MROW).then_inc(S["s_mtab"], 16)

            npass = vload(sp)

            def load_ea(count, group, par):
                sp.wait_ge(S["s_er"], count)
                sp.dma_start(EA[:, par, :], A["eaT"][:, bass.ds(group * GE, GE)]).then_inc(eal[par], 16)

            with sp.Fori(0, npass) as j:
                sp.wait_ge(S["s_er"], j * NG + 2)
                sp.sem_inc(S["s_step"], 1)
                with sp.Fori(0, ITERS + 1) as i:
                    for g in range(2):
                        load_ea(j * NG + 2 * i + g + 1, 2 * i + g, g)
                sp.wait_ge(eal[1], (j + 1) * (ITERS + 1) * 16)
                sp.sem_inc(S["s_step"], 1)
            sp.wait_ge(S["s_ue"], 4)
            for d_, n_ in ((wkv1.rearrange("p k c -> p (k c)"), "wkv1"), (wq1.rearrange("p k c -> p (k c)"), "wq1"),
                           (woT.rearrange("p k c -> p (k c)"), "woT"), (bu.rearrange("p k c -> p (k c)"), "bu"),
                           (m1[0:32, :], "m1"), (m2, "m2"), (m3, "m3"), (m4, "m4"), (mask64, "mask64")):
                ld(d_, A[n_], "s_w1")
            sp.wait_ge(S["s_o0"], 8)
            for d_, n_ in ((wl.rearrange("p k c -> p (k c)"), "wl"), (bdb.rearrange("p k c -> p (k c)"), "bdb"),
                           (bds.rearrange("p k c -> p (k c)"), "bds"), (wc.rearrange("p k c -> p (k c)"), "wc"),
                           (pat.rearrange("p a b c -> p (a b c)"), "pat"), (ltm, "ltm"), (fb2, "fb2"),
                           (fw2.rearrange("p m c -> p (m c)"), "fw2")):
                ld(d_, A[n_], "s_w4")
            sp.wait_ge(S["s_upr"], 8)
            sp.dma_start(utab.rearrange("(t p) h -> p t h", p=P), UPR).then_inc(S["s_utab"], 16)
            sp.wait_ge(S["s_xt3"], 8)
            sp.wait_ge(S["s_utab"], 16)
            sp.dma_start(shv.rearrange("p t k -> p (t k)"), A["sh"]).then_inc(S["s_utab"], 16)
            ld(fw1.rearrange("p k c -> p (k c)"), A["fw1"], "s_w4")
            with sp.Fori(0, npass) as j:
                sp.wait_ge(S["s_mlp"], j * MP + 6)
                sp.sem_inc(S["s_step"], 1)
                with sp.Fori(0, (ITERS + 2) // 2) as i:
                    for g in range(2):
                        sp.wait_ge(S["s_mlp"], j * MP + 3 * (2 * i + g) + 1)
                        sp.dma_start(RBF[0:32, g, :],
                                     A["rbf"][bass.ds((2 * i + g) * 32, 32), :]).then_inc(rbl[g], 16)
                sp.wait_ge(rbl[1], (j + 1) * ((ITERS + 2) // 2) * 16)
                sp.sem_inc(S["s_step"], 1)
            for t in range(NT):
                sp.wait_ge(S["s_out"], t + 1)
                n = P if t < NT - 1 else LAST
                sp.dma_start(out[t * P:t * P + n, :], OUTR[0:n, t, :]).then_inc(S["s_store"], 16)
            sp.wait_ge(S["s_store"], 16 * NT)

        @block.gpsimd
        def _(pool):
            npass = vload(pool)

            def gathers(j, i, table, width, ring_, done, used, copied):
                for h in range(2):
                    t0 = i * BODY + h * GR
                    pool.wait_ge(used, j * ET + t0 + GR)
                    pool.sem_inc(S["s_step"], 1)
                    pool.tensor_copy(curI[:, h * GR:(h + 1) * GR], src[:, bass.ds(t0, GR)]).then_inc(copied, 1)
                    pool.wait_ge(copied, j * 2 * ITERS + 2 * i + h + 1)
                    pool.sem_inc(S["s_step"], 1)
                    for k in range(GR):
                        slot = h * GR + k
                        pool.indirect_dma_start(ring_[:, slot, 0:width], None, table,
                                                bass.IndirectOffsetOnAxis(ap=curI[:, slot:slot + 1], axis=0)
                                                ).then_inc(done[slot], 16)

            pool.wait_ge(S["s_mtab"], 16)
            with pool.Fori(0, npass) as j:
                with pool.Fori(0, ITERS) as i:
                    gathers(j, i, mtab, H, MR, gath, S["s_seg"], S["s_curI"])
            pool.wait_ge(S["s_utab"], 32)
            pool.wait_ge(S["s_xt3"], 8)
            with pool.Fori(0, npass) as j:
                with pool.Fori(0, ITERS) as i:
                    gathers(j, i, utab, D, G1, gath, S["s_prod"], S["s_curI1"])

        @block.scalar
        def _(act):
            n = [0]

            def link(ins):
                n[0] += 1
                ins.then_inc(S["s_act"], 1)
                act.wait_ge(S["s_act"], n[0])

            def rows_and_std(v):
                if v:
                    for i in range(NT // 2):
                        act.wait_ge(rowT[v], i + 1)
                        act.activation(ROW[:, 2 * i:2 * i + 2, :].rearrange("p t d -> p (t d)"),
                                       ps[:, 4 + i % 4, :], ACT.Copy).then_inc(row[v], 1)
                act.wait_ge(lnvar[v], 1)
                act.activation(std, var, ACT.Sqrt).then_inc(lnstd[v], 1)

            def cols_out(v):
                for i in range(NT // 2):
                    c, k = divmod(i, 2)
                    act.wait_ge(colT[v], i + 1)
                    act.activation(YT[:, k, 512 * c:512 * c + 512], ps[:, i % 4, :], ACT.Copy).then_inc(col[v], 1)

            act.wait_ge(S["s_bnvar"], 1)
            act.activation(bns, bnt, ACT.Sqrt).then_inc(S["s_bnstd"], 1)
            rows_and_std(0)
            cols_out(0)
            act.wait_ge(col[0], 8)
            act.wait_ge(S["s_bn"], 1)
            for k in range(2):
                act.activation(LT[:, k, :], YT[:, k, :], ACT.Relu, bias=bnb[:, k:k + 1],
                               scale=bns[:, k:k + 1]).then_inc(S["s_lt"], 1)
            for c in range(4):
                act.wait_ge(S["s_msg"], c + 1)
                act.activation(MT[:, 512 * c:512 * c + 512], ps[0:H, c, :], ACT.Relu, bias=bnb[0:H, 2:3],
                               scale=bns[0:H, 2:3]).then_inc(S["s_mt"], 1)
            for t in range(NT):
                act.wait_ge(S["s_kv"], t + 1)
                act.activation(KC[:, t, :, :].rearrange("p g c -> p (g c)"), ps[:, t % 4, :],
                               ACT.Copy).then_inc(S["s_kvc"], 1)
                if t >= 2:
                    act.wait_ge(S["s_vs"], t - 1)
                act.activation(SQ[:, t % 2, :], ps[:, t % 4, :], ACT.Square).then_inc(S["s_kvr"], 1)
            act.wait_ge(S["s_vs"], NT + 1)
            act.activation(VS, VS, ACT.Sqrt).then_inc(S["s_vstd"], 1)
            for i in range(8):
                c, o = divmod(i, 2)
                act.wait_ge(S["s_h1"], i + 1)
                if i == 0:
                    act.wait_ge(S["s_bvm"], 1)
                act.activation(H1T[:, o, 512 * c:512 * c + 512], ps[:, i % 4, :], ACT.Gelu,
                               bias=bvec[:, o:o + 1]).then_inc(S["s_h1e"], 1)
            act.wait_ge(S["s_xt0"], 16)
            act.wait_ge(S["s_mtab"], 16)
            act.memzero(arena[:, 20000:NW * 16]).then_inc(S["s_acc0p"], 1)

            npass = vload(act)
            def relu(par, lead, free):
                act.wait_ge(S["s_er"], lead)
                act.wait_ge(S["s_seg"], free)
                act.activation(MR[:, par * GR:(par + 1) * GR, H + 1:],
                               ps[:, par, 0:GR * KH].rearrange("p (t q) -> p t q", t=GR),
                               ACT.Relu).then_inc(S["s_rready"], 1)

            with act.Fori(0, npass) as j:
                relu(0, j * NG + 3, j * ET + GR)
                with act.Fori(0, ITERS) as i:
                    for g in range(2):
                        relu(1 - g, j * NG + 2 * i + g + 4, j * ET + (2 * i + g + 2) * GR)
            for c in range(4):
                act.wait_ge(S["s_u"], c + 1)
                act.activation(U[:, NCH * c:NCH * (c + 1)], ps[0:H, c, 0:NCH], ACT.Relu, bias=bnb[0:H, 3:4],
                               scale=bns[0:H, 3:4]).then_inc(S["s_ue"], 1)
            rows_and_std(1)
            cols_out(1)
            rows_and_std(2)
            cols_out(2)
            for i in range(NT // 2):
                act.wait_ge(S["s_up"], i + 1)
                act.activation(UPR[:, 2 * i:2 * i + 2, :].rearrange("p t d -> p (t d)"), ps[:, 4 + i % 4, :],
                               ACT.Copy).then_inc(S["s_upr"], 1)
            for t in range(NT):
                act.wait_ge(S["s_kv1"], t + 1)
                b = 2 * (t % 2)
                act.activation(KV1[:, t, :, :].rearrange("p g c -> p (g c)"),
                               ps[:, b:b + 2, :].rearrange("p b c -> p (b c)"), ACT.Copy).then_inc(S["s_k1c"], 1)
                if t >= 1:
                    act.wait_ge(S["s_v1r"], t)
                act.activation(SQ1, ps[:, b:b + 2, :].rearrange("p b c -> p (b c)"),
                               ACT.Square).then_inc(S["s_k1s"], 1)
            act.wait_ge(S["s_v1r"], NT + 1)
            act.activation(VS1, VS1, ACT.Sqrt).then_inc(S["s_v1std"], 1)
            def silu(count, dst, free=None):
                act.wait_ge(S["s_mlp"], count + 6)
                if free is not None:
                    act.wait_ge(*free)
                act.activation(dst.rearrange("p (b e) -> p b e", b=2), ps[:, 0:2, 0:GE // 2],
                               ACT.Silu).then_inc(S["s_silu"], 1)

            mp = MP
            with act.Fori(0, npass) as j:
                silu(j * mp + 1, R1)
                silu(j * mp + 2, R2)
                silu(j * mp + 3, R3, (S["s_T"], j * ET + 1))
                with act.Fori(0, ITERS) as i:
                    silu(j * mp + 3 * i + 4, R1)
                    silu(j * mp + 3 * i + 5, R2)
                    silu(j * mp + 3 * i + 6, R3, (S["s_T"], j * ET + BODY * i + BODY + 1))
            for i in range(NT // 2):
                act.wait_ge(S["s_ar"], i + 1)
                act.activation(AR[:, 2 * i:2 * i + 2, :, :].rearrange("p t b c -> p (t b c)"), ps[:, 4 + i % 4, :],
                               ACT.Copy).then_inc(S["s_are"], 1)
            for i in range(NT // 2):
                c, k = divmod(i, 2)
                act.wait_ge(S["s_bt"], i + 1)
                act.activation(BT[:, k, 512 * c:512 * c + 512], ps[:, i % 4, :], ACT.Copy).then_inc(S["s_bte"], 1)
            for i in range(8):
                c, k = divmod(i, 2)
                act.wait_ge(S["s_o"], i + 1)
                act.activation(OT[:, k, 512 * c:512 * c + 512], ps[:, 4 + i % 4, :], ACT.Copy).then_inc(S["s_oe"], 1)
            act.wait_ge(S["s_nvar"], 1)
            act.activation(nrm, nrm, ACT.Sqrt).then_inc(S["s_nstd"], 1)
            rows_and_std(3)
            cols_out(3)
            for c in range(4):
                act.wait_ge(S["s_wb"], c + 1)
                act.activation(WB[:, 512 * c:512 * c + 512], ps[:, 4 + c, :], ACT.Identity,
                               bias=brc[:, 0:1]).then_inc(S["s_wbe"], 1)
            for i in range(32):
                c, m = divmod(i, 8)
                act.wait_ge(S["s_hh"], i + 1)
                act.activation(HT[:, m, 512 * c:512 * c + 512], ps[:, i % 4, :], ACT.Gelu_apprx_tanh,
                               bias=fb1[:, m:m + 1]).then_inc(S["s_he"], 1)

        @block.tensor
        def _(pe):
            def to_rows(v):
                pe.wait_ge(xtd[v], 1)
                for i in range(NT // 2):
                    if i >= 4:
                        pe.wait_ge(row[v], i - 3)
                    for t in range(2):
                        for k in range(2):
                            tr = pe.transpose(ps[:, 4 + i % 4, t * D + k * P:t * D + (k + 1) * P],
                                              XT[:, k, (2 * i + t) * P:(2 * i + t + 1) * P], ident)
                    tr.then_inc(rowT[v], 1)

            def to_cols(v):
                for i in range(NT // 2):
                    c, k = divmod(i, 2)
                    pe.wait_ge(lny[v], 4 * c + 4)
                    if i >= 4:
                        pe.wait_ge(col[v], i - 3)
                    for t in range(4):
                        tr = pe.transpose(ps[:, i % 4, t * P:(t + 1) * P], YROW[:, 4 * c + t, k * P:(k + 1) * P], ident)
                    tr.then_inc(colT[v], 1)

            pe.wait_ge(S["s_const"], 16 * NLOAD["s_const"])
            pe.wait_ge(S["s_idx"], 32)
            pe.wait_ge(S["s_span"], 1)
            pe.transpose(ps[0:1, 7, 0:125], span[0:125, 0:1], ident[0:125, 0:125]).then_inc(S["s_span"], 1)
            to_cols(0)
            for c in range(4):
                pe.wait_ge(S["s_lt"], 2)
                for k in range(2):
                    mm = pe.matmul(ps[0:H, c, :], w1g[:, k, :], LT[:, k, 512 * c:512 * c + 512],
                                   start=(k == 0), stop=(k == 1))
                mm.then_inc(S["s_msg"], 1)
            for i in range(2):
                pe.wait_ge(S["s_mt"], 2 * i + 2)
                for t in range(8):
                    n = 8 * i + t
                    tr = pe.transpose(ps[:, 4 + i, t * H:(t + 1) * H], MT[:, n * P:(n + 1) * P], ident[0:H, 0:H])
                tr.then_inc(S["s_mtr"], 1)
            pe.wait_ge(S["s_w0"], 16 * NLOAD["s_w0"])
            pe.wait_ge(S["s_wc"], 1)
            pe.wait_ge(S["s_mt"], 4)
            for t in range(NT):
                if t >= 4:
                    pe.wait_ge(S["s_kvr"], t - 3)
                b = ps[:, t % 4, :]
                for k in range(2):
                    pe.matmul(b, YT[:, k, t * P:(t + 1) * P], wkv[:, k, :], start=(k == 0), stop=False)
                pe.matmul(b, ones[0:1, :], bkvr, start=False, stop=True).then_inc(S["s_kv"], 1)
            for g in range(2):
                for t in range(NT):
                    pe.wait_ge(S["s_kvn"], t + 1)
                    r = P if t < NT - 1 else LAST
                    KCf = KC[0:r, t, :, :].rearrange("p g c -> p (g c)")
                    mm = pe.matmul(ps[:, 6, g * P:(g + 1) * P], KCf[:, 256 + g * P:256 + (g + 1) * P],
                                   KCf[:, g * P:(g + 1) * P], start=(t == 0), stop=(t == NT - 1))
            mm.then_inc(S["s_kvt"], 1)
            pe.wait_ge(S["s_kvm"], 1)
            for g in range(2):
                mm = pe.matmul(ps[:, 4, g * D:(g + 1) * D], KVM[:, g, :], w1m[:, g, :], start=True, stop=True)
            mm.then_inc(S["s_A"], 1)
            pe.wait_ge(S["s_Am"], 1)
            for c in range(2):
                for g in range(2):
                    mm = pe.matmul(ps[:, 5, c * D:(c + 1) * D], wqT[:, g, c * P:(c + 1) * P], AM[:, g, :],
                                   start=(g == 0), stop=(g == 1))
            mm.then_inc(S["s_G"], 1)
            for o in range(2):
                for g in range(2):
                    mm = pe.matmul(ps[:, 7, o:o + 1], AM[:, g, o * P:(o + 1) * P], bq[:, g:g + 1],
                                   start=(g == 0), stop=(g == 1))
            mm.then_inc(S["s_bv"], 1)
            pe.wait_ge(S["s_Gm"], 1)
            pe.wait_ge(S["s_bvm"], 1)
            for i in range(8):
                c, o = divmod(i, 2)
                if i >= 4:
                    pe.wait_ge(S["s_h1e"], i - 3)
                for k in range(2):
                    mm = pe.matmul(ps[:, i % 4, :], GM[:, k, o * P:(o + 1) * P], YT[:, k, 512 * c:512 * c + 512],
                                   start=(k == 0), stop=(k == 1))
                mm.then_inc(S["s_h1"], 1)
            for i in range(8):
                c, o = divmod(i, 2)
                pe.wait_ge(S["s_h1e"], 2 * c + 2)
                if i >= 4:
                    pe.wait_ge(S["s_xt0"], i - 3)
                for k in range(2):
                    mm = pe.matmul(ps[:, 4 + i % 4, :], w2m[:, k, o * P:(o + 1) * P], H1T[:, k, 512 * c:512 * c + 512],
                                   start=(k == 0), stop=(k == 1))
                mm.then_inc(S["s_mo"], 1)

            npass = vload(pe)
            pe.wait_ge(S["s_xt0"], 16)
            pe.sem_inc(S["s_er"], 2)
            pe.sem_inc(S["s_seg"], BODY)

            def edge_net(par, loaded, free):
                pe.wait_ge(eal[par], loaded)
                pe.wait_ge(S["s_rready"], free) if free is not None else None
                for t in range(GR):
                    r = ps[:, par, t * KH:(t + 1) * KH]
                    pe.matmul(r, ones[0:1, :], kb1r[0:1, 0:KH], start=True, stop=False)
                    mm = pe.matmul(r, EA[:, par, t * P:(t + 1) * P], kw1, start=False, stop=True)
                mm.then_inc(S["s_er"], 1)

            def segments(j, i, g):
                T = j * ET + i * BODY + g * GR
                pe.wait_ge(S["s_mask"], j * NG + 2 * i + g + 1)
                for t in range(GR):
                    slot = g * GR + t
                    pe.wait_ge(gath[slot], (j * ITERS + i + 1) * 16)
                    pe.wait_ge(S["s_rmw"], T + t + 1)
                    for h in range(2):
                        pe.matmul(outer(slot)[h * H:(h + 1) * H, :], MR[:, slot, 0:H],
                                  RM[:, g, t, :, h * 16:(h + 1) * 16], start=True, stop=True)
                    pe.matmul(affine(slot), MR[:, slot, :],
                              SW[:, g, t, :], start=True, stop=True).then_inc(S["s_seg"], 1)

            with pe.Fori(0, npass) as j:
                edge_net(0, j * (ITERS + 1) * 16 + 16, None)
                with pe.Fori(0, ITERS) as i:
                    edge_net(1, (j * (ITERS + 1) + i + 1) * 16, j * (2 * ITERS + 1) + 2 * i + 1)
                    segments(j, i, 0)
                    edge_net(0, (j * (ITERS + 1) + i + 2) * 16, j * (2 * ITERS + 1) + 2 * i + 2)
                    segments(j, i, 1)
                pe.wait_ge(S["s_rready"], (j + 1) * NG)
            pe.wait_ge(S["s_base"], 1)
            for c in range(4):
                pe.matmul(ps[0:H, c, 0:NCH], wV[0:H + 1 + KH, :], vacc[0:H + 1 + KH, c * NCH:(c + 1) * NCH],
                          start=True, stop=False)
                for q in range(16):
                    mm = pe.matmul(ps[0:H, c, 0:NCH], W2S[:, q, :], acc[:, c * NCH:(c + 1) * NCH, q],
                                   start=False, stop=(q == 15))
                mm.then_inc(S["s_u"], 1)
            for i in range(8):
                c, o = divmod(i, 2)
                pe.wait_ge(S["s_ue"], c + 1)
                if i >= 4:
                    pe.wait_ge(S["s_o0"], i - 3)
                pe.matmul(ps[:, 4 + i % 4, 0:NCH], w2g[0:H, o * P:(o + 1) * P], U[:, c * NCH:(c + 1) * NCH],
                          start=True, stop=True).then_inc(S["s_mo"], 1)
            to_rows(1)
            to_cols(1)
            for i in range(8):
                c, o = divmod(i, 2)
                pe.wait_ge(col[1], 2 * c + 2)
                pe.wait_ge(S["s_ff"], i - 3) if i >= 4 else pe.wait_ge(row[1], 8)
                for k in range(2):
                    mm = pe.matmul(ps[:, 4 + i % 4, :], wfT[:, k, o * P:(o + 1) * P], YT[:, k, 512 * c:512 * c + 512],
                                   start=(k == 0), stop=(k == 1))
                mm.then_inc(S["s_mo"], 1)
            to_rows(2)
            to_cols(2)
            pe.wait_ge(S["s_w1"], 16 * NLOAD["s_w1"])
            pe.wait_ge(row[2], 8)
            for i in range(NT // 2):
                pe.wait_ge(col[2], 2 * (i // 2) + 2)
                if i >= 4:
                    pe.wait_ge(S["s_upr"], i - 3)
                for t in range(2):
                    for k in range(2):
                        mm = pe.matmul(ps[:, 4 + i % 4, t * D + k * P:t * D + (k + 1) * P],
                                       YT[:, k, (2 * i + t) * P:(2 * i + t + 1) * P], bu[:, k, :], start=True, stop=True)
                mm.then_inc(S["s_up"], 1)
            pe.wait_ge(S["s_wc"], 2)
            pe.wait_ge(col[2], 8)
            for t in range(NT):
                if t >= 2:
                    pe.wait_ge(S["s_k1s"], t - 1)
                for h in range(2):
                    for k in range(2):
                        mm = pe.matmul(ps[:, 2 * (t % 2) + h, :], YT[:, k, t * P:(t + 1) * P],
                                       wkv1[:, k, h * 512:(h + 1) * 512], start=(k == 0), stop=(k == 1))
                mm.then_inc(S["s_kv1"], 1)
            pe.wait_ge(S["s_upr"], 8)
            for g in range(4):
                for t in range(NT):
                    pe.wait_ge(S["s_v1n"], t + 1)
                    r = P if t < NT - 1 else LAST
                    KVf = KV1[0:r, t, :, :].rearrange("p g c -> p (g c)")
                    mm = pe.matmul(ps[:, 4, g * P:(g + 1) * P], KVf[:, 512 + g * P:512 + (g + 1) * P],
                                   KVf[:, g * P:(g + 1) * P], start=(t == 0), stop=(t == NT - 1))
            mm.then_inc(S["s_kvt1"], 1)
            pe.wait_ge(S["s_kvm1"], 1)
            for g in range(4):
                mm = pe.matmul(ps[:, 5 + g // 2, (g % 2) * D:(g % 2 + 1) * D], KVM1[:, g, :], woT[:, g, :],
                               start=True, stop=True)
            mm.then_inc(S["s_A1"], 1)
            pe.wait_ge(S["s_Am1"], 2)
            for c in range(2):
                for g in range(4):
                    mm = pe.matmul(ps[:, 7, c * D:(c + 1) * D], wq1[:, g, c * P:(c + 1) * P], AM1[:, g, :],
                                   start=(g == 0), stop=(g == 3))
            mm.then_inc(S["s_G1"], 1)
            pe.wait_ge(S["s_Gm1"], 1)
            for i in range(8):
                c, o = divmod(i, 2)
                if i >= 4:
                    pe.wait_ge(S["s_xt3"], i - 3)
                for k in range(2):
                    mm = pe.matmul(ps[:, i % 4, :], GM1[:, k, o * P:(o + 1) * P], YT[:, k, 512 * c:512 * c + 512],
                                   start=(k == 0), stop=(k == 1))
                mm.then_inc(S["s_y1"], 1)

            pe.wait_ge(S["s_xt3"], 8)
            pe.wait_ge(S["s_utab"], 32)
            pe.wait_ge(S["s_acc1"], 1)
            pe.sem_inc(S["s_mlp"], 6)
            pe.sem_inc(S["s_T"], 1)
            pe.sem_inc(S["s_seg1"], BODY)

            def layer(w, src_, rows_, after):
                pe.wait_ge(*after)
                for b in range(2):
                    mm = pe.matmul(ps[:, b, 0:GE // 2], w[0:rows_, :], src_[0:rows_, b * (GE // 2):(b + 1) * (GE // 2)],
                                   start=True, stop=True)
                mm.then_inc(S["s_mlp"], 1)

            mp = MP

            def weights(j, i, u, k):
                if k == 0:
                    pe.wait_ge(S["s_silu"], j * mp + 3 * i + 3)
                pe.wait_ge(S["s_prod"], j * ET + i * BODY + k + BODY - 3)
                h = k // GR
                pe.matmul(weights_of(u * BODY + k), R3[h * H:(h + 1) * H, (k % GR) * P:(k % GR + 1) * P], m4[h * H:(h + 1) * H, :],
                          start=True, stop=True).then_inc(S["s_T"], 1)

            def segment(j, i, u, k):
                T = j * ET + i * BODY + k
                pe.wait_ge(S["s_prod"], T + BODY + 1)
                pe.wait_ge(S["s_rmw1"], T + 1)
                o = sums(u * BODY + k)
                S4k = S4[:, k // GR, k % GR, :, :]
                for pair, (a, y0, y1) in enumerate(((0, 0, 1), (1, 0, 1), (2, 1, 3), (4, 1, 4))):
                    mm = pe.matmul(o[:, a:a + y1 - y0, :], PP[:, k, 2 * pair:2 * pair + 2, :], S4k[:, y0:y1, :],
                                   start=True, stop=True)
                mm.then_inc(S["s_seg1"], 1)

            with pe.Fori(0, npass) as j:
                def first(par, n_loaded, c):
                    pe.wait_ge(rbl[par], n_loaded)
                    layer(m1, RBF[:, par, :], 32, (S["s_silu"], c))

                pe.wait_ge(rbl[0], (j * ((ITERS + 2) // 2) + 1) * 16)
                for b in range(2):
                    mm = pe.matmul(ps[:, b, 0:GE // 2], m1[0:32, :], RBF[0:32, 0, b * (GE // 2):(b + 1) * (GE // 2)],
                                   start=True, stop=True)
                mm.then_inc(S["s_mlp"], 1)
                layer(m2, R1, P, (S["s_silu"], j * mp + 1))
                layer(m3, R2, P, (S["s_silu"], j * mp + 2))
                with pe.Fori(0, ITERS // 2) as i2:
                    for u in range(2):
                        i = 2 * i2 + u
                        for k in range(BODY):
                            weights(j, i, u, k)
                            if k == 1:
                                first(1 - u, (j * ((ITERS + 2) // 2) + i2 + 1 + u) * 16, j * mp + 3 * i + 3)
                            if k == 4:
                                layer(m2, R1, P, (S["s_silu"], j * mp + 3 * i + 4))
                            if k == BODY - 1:
                                layer(m3, R2, P, (S["s_silu"], j * mp + 3 * i + 5))
                            if k >= 2:
                                segment(j, i, u, k - 2)
                        segment(j, i, u, BODY - 2)
                        segment(j, i, u, BODY - 1)
                pe.wait_ge(S["s_silu"], (j + 1) * mp)
                pe.wait_ge(rbl[1], (j + 1) * ((ITERS + 2) // 2) * 16)
            pe.wait_ge(S["s_base1"], 1)
            pe.wait_ge(S["s_w4"], 16 * NLOAD["s_w4"])
            for i in range(NT // 2):
                if i >= 4:
                    pe.wait_ge(S["s_are"], i - 3)
                for t in range(2):
                    for h in range(NA):
                        mm = pe.matmul(ps[:, 4 + i % 4, t * D:(t + 1) * D], acc1[:, h, (2 * i + t) * P:(2 * i + t + 1) * P],
                                       wl[:, h, :], start=(h == 0), stop=(h == NA - 1))
                mm.then_inc(S["s_ar"], 1)
            pe.wait_ge(S["s_b"], 1)
            for i in range(NT // 2):
                c, k = divmod(i, 2)
                if i >= 4:
                    pe.wait_ge(S["s_bte"], i - 3)
                for t in range(4):
                    tr = pe.transpose(ps[:, i % 4, t * P:(t + 1) * P],
                                      BR[:, 4 * c + t, 2 * k:2 * k + 2, :].rearrange("p b c -> p (b c)"), ident)
                tr.then_inc(S["s_bt"], 1)
            pe.wait_ge(S["s_are"], 8)
            for i in range(8):
                c, k = divmod(i, 2)
                pe.wait_ge(S["s_bte"], i + 1)
                if i >= 4:
                    pe.wait_ge(S["s_oe"], i - 3)
                pe.matmul(ps[:, 4 + i % 4, :], bdb[:, k, :], BT[:, k, 512 * c:512 * c + 512], start=True, stop=False)
                pe.matmul(ps[:, 4 + i % 4, :], bds[:, k, :], YT[:, k, 512 * c:512 * c + 512], start=False,
                          stop=True).then_inc(S["s_o"], 1)
            pe.wait_ge(S["s_nr"], 1)
            for o in range(2):
                for k in range(2):
                    mm = pe.matmul(ps[:, 0, o:o + 1], pat[:, k, o, :], ss[:, k:k + 1], start=(k == 0), stop=(k == 1))
            mm.then_inc(S["s_nre"], 1)
            to_rows(3)
            to_cols(3)
            pe.wait_ge(row[3], 8)
            for c in range(4):
                pe.wait_ge(col[3], 2 * c + 2)
                for k in range(2):
                    mm = pe.matmul(ps[:, 4 + c, :], wrb[:, k, :], YT[:, k, 512 * c:512 * c + 512],
                                   start=(k == 0), stop=(k == 1))
                mm.then_inc(S["s_wb"], 1)
            for i in range(4):
                pe.wait_ge(S["s_wbe"], 4)
                for t in range(4):
                    tr = pe.transpose(ps[:, 4 + i, t * P:(t + 1) * P], WB[:, (4 * i + t) * P:(4 * i + t + 1) * P], ident)
                tr.then_inc(S["s_wct"], 1)
            for i in range(32):
                c, m = divmod(i, 8)
                if i >= 4:
                    pe.wait_ge(S["s_he"], i - 3)
                for k in range(2):
                    mm = pe.matmul(ps[:, i % 4, :], fw1[:, k, m * P:(m + 1) * P], YT[:, k, 512 * c:512 * c + 512],
                                   start=(k == 0), stop=(k == 1))
                mm.then_inc(S["s_hh"], 1)
            pe.wait_ge(S["s_wcol"], 4)
            for t in range(NT):
                pe.wait_ge(S["s_he"], 8 * (t // 4) + 8)
                if t >= 4:
                    pe.wait_ge(S["s_out"], t - 3)
                for m in range(8):
                    mm = pe.matmul(ps[:, 4 + t % 4, 0:D], HT[:, m, t * P:(t + 1) * P], fw2[:, m, :],
                                   start=(m == 0), stop=(m == 7))
                mm.then_inc(S["s_yy"], 1)

        @block.vector
        def _(dve):
            n = [0]

            def link(ins):
                n[0] += 1
                ins.then_inc(S["s_dve"], 1)
                dve.wait_ge(S["s_dve"], n[0])

            def layer_norm(v):
                for t in range(NT):
                    if v:
                        dve.wait_ge(row[v], t // 2 + 1)
                    ins = dve.bn_stats(st[:, t, :], ROW[:, t, :])
                link(ins)
                for t in range(NT):
                    ins = dve.bn_aggr(mv[:, t, :], st[:, t, :])
                link(ins)
                dve.tensor_scalar(var, mv[:, :, 1], EPS, None, ALU.add).then_inc(lnvar[v], 1)
                dve.wait_ge(lnstd[v], 1)
                link(dve.reciprocal(rs, std))
                for t in range(NT):
                    dve.tensor_scalar(YROW[:, t, :], ROW[:, t, :], mv[:, t, 0:1], rs[:, t:t + 1],
                                      ALU.subtract, ALU.mult).then_inc(lny[v], 1)

            dve.memset(ROW[:, NT - 1, :], 0.0).then_inc(S["s_zero"], 1)
            dve.memset(XT[:, :, N:NPAD], 0.0).then_inc(S["s_zero"], 1)
            dve.memset(vacc[:, :], 0.0)
            dve.memset(ewt[:, ET:], 0.0)
            dve.memset(dloc[:, ET:], -1.0)
            dve.wait_ge(S["s_idx"], 32)
            dve.tensor_copy(dstF[:, :], dstI)
            link(dve.tensor_copy(dr, drI))
            dve.memset(MR[:, :, H:H + 1], 1.0)
            drv = dr.rearrange("p (q e) -> p q e", q=4)
            dve.tensor_reduce(lohi[0:125, 0:4], drv, AX.X, ALU.min)
            link(dve.tensor_reduce(lohi[0:125, 4:8], drv, AX.X, ALU.max))
            link(dve.tensor_tensor(cnt3[0:125, 0, 0:4], lohi[0:125, 4:8], lohi[0:125, 0:4], ALU.subtract))
            dve.tensor_reduce(span[0:125, 0:1], cnt3[0:125, 0, 0:4], AX.X, ALU.max).then_inc(S["s_span"], 1)
            dve.wait_ge(S["s_span"], 2)
            link(dve.tensor_reduce(span[0:1, 1:2], ps[0:1, 7, 0:125], AX.X, ALU.max))
            link(dve.tensor_copy(npassI[0:1, 1:2], span[0:1, 1:2]))
            link(dve.tensor_scalar(npassI[0:1, 1:2], npassI[0:1, 1:2], 3, None, ALU.arith_shift_right))
            dve.tensor_scalar(npassI[0:1, 0:1], npassI[0:1, 1:2], 1, None, ALU.add).then_inc(S["s_npass"], 1)
            dve.wait_ge(S["s_const"], 16 * NLOAD["s_const"])
            dve.tensor_scalar(bnt, bnv[:, 3, :], EPS, None, ALU.add).then_inc(S["s_bnvar"], 1)
            dve.wait_ge(S["s_bnstd"], 1)
            link(dve.reciprocal(bns, bns))
            link(dve.tensor_tensor(bns, bns, bnv[:, 0, :], ALU.mult))
            link(dve.tensor_tensor(bnb, bnv[:, 4, :], bnv[:, 2, :], ALU.subtract))
            link(dve.tensor_tensor(bnb, bnb, bns, ALU.mult))
            dve.tensor_tensor(bnb, bnb, bnv[:, 1, :], ALU.add).then_inc(S["s_bn"], 1)
            dve.wait_ge(S["s_x"], 32)
            layer_norm(0)
            for i in range(2):
                dve.wait_ge(S["s_mtr"], i + 1)
                dve.tensor_copy(MROW[:, 8 * i:8 * i + 8, :].rearrange("p t h -> p (t h)"),
                                ps[:, 4 + i, :]).then_inc(S["s_mrow"], 1)

            def centre(w, g, c):
                wv = w.rearrange("p (g c) -> p g c", c=c)
                m = wmean[0:w.shape[0], 0:g]
                link(dve.tensor_reduce(m, wv, AX.X, ALU.add))
                link(dve.tensor_scalar(m, m, 1.0 / c, None, ALU.mult))
                link(dve.tensor_tensor(wv, wv, m.unsqueeze(2).broadcast_to([w.shape[0], g, c]), ALU.subtract))

            dve.wait_ge(S["s_w0"], 16 * NLOAD["s_w0"])
            for k in range(2):
                centre(wkv[:, k, :], 16, 32)
            centre(bkvr, 16, 32)
            dve.sem_inc(S["s_wc"], 1)
            for t in range(NT):
                dve.wait_ge(S["s_kvr"], t + 1)
                dve.tensor_reduce(VS[:, t * 16:(t + 1) * 16], SQ[:, t % 2, :].rearrange("p (g c) -> p g c", c=32),
                                  AX.X, ALU.add).then_inc(S["s_vs"], 1)
            dve.wait_ge(S["s_vs"], NT)
            dve.tensor_scalar(VS, VS, 1.0 / 32, EPS, ALU.mult, ALU.add).then_inc(S["s_vs"], 1)
            dve.wait_ge(S["s_vstd"], 1)
            link(dve.reciprocal(VS, VS))
            for t in range(NT):
                dve.wait_ge(S["s_kvc"], t + 1)
                ins = dve.tensor_tensor(KC[:, t, :, :], KC[:, t, :, :],
                                        VS[:, t * 16:(t + 1) * 16].unsqueeze(2).broadcast_to([P, 16, 32]), ALU.mult)
            link(ins)
            for t in range(NT):
                ins = dve.tensor_tensor(KC[:, t, :, :], KC[:, t, :, :], gkv.rearrange("p (g c) -> p g c", c=32), ALU.mult)
            link(ins)
            for t in range(NT):
                dve.tensor_tensor(KC[:, t, :, :], KC[:, t, :, :], bkv.rearrange("p (g c) -> p g c", c=32),
                                  ALU.add).then_inc(S["s_kvn"], 1)
            dve.wait_ge(S["s_kvt"], 1)
            dve.tensor_tensor(KVM, ps[:, 6, 0:256].rearrange("p (g c) -> p g c", g=2),
                              mask32.unsqueeze(1).broadcast_to([P, 2, P]), ALU.mult).then_inc(S["s_kvm"], 1)
            dve.wait_ge(S["s_A"], 1)
            dve.tensor_copy(AM.rearrange("p g c -> p (g c)"), ps[:, 4, :]).then_inc(S["s_Am"], 1)
            dve.wait_ge(S["s_G"], 1)
            dve.tensor_tensor(GM.rearrange("p g c -> p (g c)"), ps[:, 5, :], w1p.rearrange("p g c -> p (g c)"),
                              ALU.add).then_inc(S["s_Gm"], 1)
            dve.wait_ge(S["s_bv"], 1)
            dve.tensor_tensor(bvec, ps[:, 7, 0:2], b1c, ALU.add).then_inc(S["s_bvm"], 1)
            for i in range(8):
                c, o = divmod(i, 2)
                dve.wait_ge(S["s_mo"], i + 1)
                xc = XT[:, o, 512 * c:512 * c + 512]
                dve.scalar_tensor_tensor(xc, ps[:, 4 + i % 4, :], b2c[:, o:o + 1], xc, ALU.add,
                                         ALU.add).then_inc(S["s_xt0"], 1)
            dve.wait_ge(S["s_xt0"], 8)
            for i in range(8):
                c, o = divmod(i, 2)
                xc = XT[:, o, 512 * c:512 * c + 512]
                dve.tensor_tensor(xc, xc, YT[:, o, 512 * c:512 * c + 512], ALU.add).then_inc(S["s_xt0"], 1)
            dve.wait_ge(S["s_xt0"], 16)
            dve.memset(arena[:, 0:20000], 0.0)
            dve.wait_ge(S["s_lo"], 16)
            link(dve.tensor_copy(base[:, :], LO[:, :]))
            dve.wait_ge(S["s_acc0p"], 1)
            npass = vload(dve)

            def windows(done):
                dve.tensor_tensor(dloc[:, 0:ET], dstF[:, :], base[:, :], ALU.subtract)
                dve.tensor_copy(baseI[:, :], base[0:1, :]).then_inc(S["s_oh"], 1)
                dve.wait_ge(S["s_oh"], done)

            def next_windows(done):
                dve.tensor_scalar(base[:, :], base[:, :], float(WIN), float(N), ALU.add,
                                  ALU.min).then_inc(S["s_oh"], 1)
                dve.wait_ge(S["s_oh"], done)

            def onehot(out_, t0, count, sem_):
                dve.tensor_tensor(out_, iota8.unsqueeze(1).broadcast_to([P, GR, WIN]),
                                  dloc[:, bass.ds(t0, GR)].unsqueeze(2).broadcast_to([P, GR, WIN]),
                                  ALU.is_equal).then_inc(sem_, 1)
                dve.wait_ge(sem_, count)

            dve.sem_inc(S["s_rmw"], GR)
            with dve.Fori(0, npass) as j:
                per = 2 + 2 * NG
                windows(j * per + 1)

                def masks(i, g):
                    c = j * per + 1 + 2 * (2 * i + g)
                    t0 = i * BODY + g * GR
                    ready = j * NG + 2 * i + g + 1
                    g = g % 2
                    dve.wait_ge(S["s_seg"], j * ET + t0 + GR)
                    onehot(SW[:, g, :, :], t0, c + 1, S["s_oh"])
                    dve.tensor_tensor(SW[:, g, :, :], SW[:, g, :, :],
                                      ewt[:, bass.ds(t0, GR)].unsqueeze(2).broadcast_to([P, GR, WIN]),
                                      ALU.mult).then_inc(S["s_oh"], 1)
                    dve.wait_ge(S["s_oh"], c + 2)
                    dve.wait_ge(S["s_rready"], ready)
                    dve.tensor_tensor(
                        RM[:, g, :, :, :],
                        MR[:, g * GR:(g + 1) * GR, H + 1:].unsqueeze(2).broadcast_to([P, GR, WIN, KH]),
                        SW[:, g, :, :].unsqueeze(3).broadcast_to([P, GR, WIN, KH]),
                        ALU.mult).then_inc(S["s_mask"], 1)

                def add(i, g):
                    for t in range(GR):
                        slot = g * GR + t
                        T = j * ET + i * BODY + slot
                        b = dve.value_load(baseI[0:1, bass.ds(i * BODY + slot, 1)], min_val=0, max_val=N)
                        dve.wait_ge(S["s_seg"], T + BODY + 1)
                        dve.wait_ge(S["s_rmw"], T + GR)
                        a = acc[:, bass.ds(b, WIN), :]
                        dve.tensor_tensor(a, a, outer(slot).rearrange("p (n q) -> p n q", q=16), ALU.add)
                        v = vacc[0:H + 1 + KH, bass.ds(b, WIN)]
                        dve.tensor_tensor(v, v, affine(slot), ALU.add).then_inc(S["s_rmw"], 1)

                masks(0, 0)
                with dve.Fori(0, ITERS) as i:
                    for g in range(2):
                        masks(i, g + 1)
                        add(i, g)
                next_windows(j * per + per)
            dve.drain().then_inc(S["s_base"], 1)
            for i in range(8):
                c, o = divmod(i, 2)
                dve.wait_ge(S["s_mo"], 8 + i + 1)
                xc = XT[:, o, NCH * c:NCH * (c + 1)]
                dve.scalar_tensor_tensor(xc, ps[:, 4 + i % 4, 0:NCH], bns[:, 4 + o:5 + o], xc, ALU.mult,
                                         ALU.add).then_inc(S["s_o0"], 1)
            dve.wait_ge(S["s_o0"], 8)
            for o in range(2):
                ins = dve.tensor_scalar(XT[:, o, 0:N], XT[:, o, 0:N], bnb[:, 4 + o:5 + o], None, ALU.add)
            ins.then_inc(xtd[1], 1)
            layer_norm(1)
            for i in range(8):
                c, o = divmod(i, 2)
                dve.wait_ge(S["s_mo"], 16 + i + 1)
                xc = XT[:, o, 512 * c:512 * c + 512]
                ins = dve.scalar_tensor_tensor(xc, ps[:, 4 + i % 4, :], bfc[:, o:o + 1], xc, ALU.add, ALU.add)
                ins.then_inc(S["s_ff"], 1)
            dve.wait_ge(S["s_ff"], 8)
            dve.sem_inc(xtd[2], 1)
            layer_norm(2)
            dve.wait_ge(S["s_w1"], 16 * NLOAD["s_w1"])
            for k in range(2):
                centre(wkv1[:, k, :], 16, 64)
            dve.sem_inc(S["s_wc"], 1)
            link(dve.tensor_scalar(m4[:, 192:256], m4[:, 192:256], 3.0 ** -0.5, None, ALU.mult))
            for t in range(NT):
                dve.wait_ge(S["s_k1s"], t + 1)
                dve.tensor_reduce(VS1[:, t * 16:(t + 1) * 16], SQ1.rearrange("p (g c) -> p g c", c=64),
                                  AX.X, ALU.add).then_inc(S["s_v1r"], 1)
            dve.wait_ge(S["s_v1r"], NT)
            dve.tensor_scalar(VS1, VS1, 1.0 / 64, EPS, ALU.mult, ALU.add).then_inc(S["s_v1r"], 1)
            dve.wait_ge(S["s_v1std"], 1)
            link(dve.reciprocal(VS1, VS1))
            vsv = VS1.rearrange("p (t u h) -> p t u h", t=NT, u=2)
            link(dve.tensor_tensor(RK1.rearrange("p (t h) -> p t h", h=8), vsv[:, :, 0, :], vsv[:, :, 1, :], ALU.mult))
            for t in range(NT):
                dve.tensor_tensor(KV1[:, t, 8:16, :], KV1[:, t, 8:16, :],
                                  RK1[:, t * 8:(t + 1) * 8].unsqueeze(2).broadcast_to([P, 8, 64]),
                                  ALU.mult).then_inc(S["s_v1n"], 1)
            dve.wait_ge(S["s_kvt1"], 1)
            dve.tensor_tensor(KVM1, ps[:, 4, :].rearrange("p (g c) -> p g c", g=4),
                              mask64.unsqueeze(1).broadcast_to([P, 4, P]), ALU.mult).then_inc(S["s_kvm1"], 1)
            dve.wait_ge(S["s_A1"], 1)
            for h in range(2):
                dve.tensor_copy(AM1[:, 2 * h:2 * h + 2, :].rearrange("p g c -> p (g c)"),
                                ps[:, 5 + h, :]).then_inc(S["s_Am1"], 1)
            dve.wait_ge(S["s_G1"], 1)
            dve.tensor_copy(GM1.rearrange("p g c -> p (g c)"), ps[:, 7, :]).then_inc(S["s_Gm1"], 1)
            for i in range(8):
                c, o = divmod(i, 2)
                dve.wait_ge(S["s_y1"], i + 1)
                xc = XT[:, o, 512 * c:512 * c + 512]
                dve.scalar_tensor_tensor(xc, ps[:, i % 4, :], boc[:, o:o + 1], xc, ALU.add,
                                         ALU.add).then_inc(S["s_xt3"], 1)
            dve.wait_ge(S["s_kvt1"], 1)
            dve.memset(acc1, 0.0).then_inc(S["s_acc1"], 1)
            dve.wait_ge(S["s_acc1"], 1)
            link(dve.tensor_copy(base[:, :], LO[:, :]))
            dve.wait_ge(S["s_utab"], 32)
            dve.sem_inc(S["s_prod"], BODY)
            dve.sem_inc(S["s_rmw1"], 2)
            OHB = None
            with dve.Fori(0, npass) as j:
                per = 2 + 4 * ITERS
                b0 = npass * (2 + 2 * NG)
                windows(b0 + j * per + 1)
                dve.sem_inc(S["s_step"], 1)

                def scaled(i, g):
                    c = b0 + j * per + 1 + 2 * (2 * i + g)
                    t0 = i * BODY + g * GR
                    dve.wait_ge(S["s_seg1"], j * ET + (2 * i + g) * GR + GR)
                    onehot(OH[:, g, :, :], t0, c + 1, S["s_oh"])
                    dve.tensor_tensor(
                        S4[:, g, :, :, :], OH[:, g, :, :].unsqueeze(2).broadcast_to([P, GR, 4, WIN]),
                        shv[:, bass.ds(t0, GR), :].unsqueeze(3).broadcast_to([P, GR, 4, WIN]),
                        ALU.mult).then_inc(S["s_oh"], 1)
                    dve.wait_ge(S["s_oh"], c + 2)

                def products(i, u, slot):
                    T = j * ET + i * BODY + slot
                    dve.wait_ge(S["s_T"], T + 2)
                    dve.wait_ge(gath[slot], ((npass + j) * ITERS + i + 1) * 16)
                    dve.wait_ge(S["s_seg1"], T + 1)
                    tp = weights_of(u * BODY + slot).rearrange("p (b c) -> p b c", b=4)
                    x = G1[:, slot, :].rearrange("p (b c) -> p b c", b=4)
                    dve.tensor_tensor(PP[:, slot, 0:8:7, :], tp[:, 0:2, :], x[:, 0:1, :].broadcast_to([P, 2, H]), ALU.mult)
                    dve.tensor_tensor(PP[:, slot, 1:7, :].rearrange("p (a x) c -> p a x c", a=2),
                                      tp[:, 2:4, :].unsqueeze(2).broadcast_to([P, 2, 3, H]),
                                      x[:, 1:4, :].unsqueeze(1).broadcast_to([P, 2, 3, H]),
                                      ALU.mult).then_inc(S["s_prod"], 1)

                def add1(i, u, slot):
                    T = j * ET + i * BODY + slot
                    b = dve.value_load(baseI[0:1, bass.ds(i * BODY + slot, 1)], min_val=0, max_val=N)
                    dve.wait_ge(S["s_seg1"], T + BODY + 1)
                    dve.wait_ge(S["s_rmw1"], T + 2)
                    a = acc1[:, :, bass.ds(b, WIN)]
                    dve.tensor_tensor(a, a, sums(u * BODY + slot), ALU.add).then_inc(S["s_rmw1"], 1)

                with dve.Fori(0, ITERS // 2) as i2:
                    for T in range(2 * BODY):
                        u, slot = divmod(T, BODY)
                        i = 2 * i2 + u
                        if slot % GR == 0:
                            scaled(i, slot // GR)
                        products(i, u, slot)
                        if T >= 2:
                            add1(2 * i2 + (T - 2) // BODY, (T - 2) // BODY, (T - 2) % BODY)
                    for slot in range(BODY - 2, BODY):
                        add1(2 * i2 + 1, 1, slot)
                next_windows(b0 + j * per + per)
            dve.drain().then_inc(S["s_base1"], 1)
            dve.wait_ge(S["s_are"], 8)
            dve.wait_ge(S["s_w4"], 16 * NLOAD["s_w4"])
            A0 = AR[:, :, 0, :]
            t0, t1, t2, t3 = TMP

            def W(v):
                return wc[:, v, :].unsqueeze(1).broadcast_to([P, NT, 64])

            def tt(o, a, b, op):
                link(dve.tensor_tensor(o, a, b, op))
            tt(t0, AR[:, :, 1, :], AR[:, :, 1, :], ALU.mult)
            tt(t1, AR[:, :, 2, :], AR[:, :, 2, :], ALU.mult)
            tt(t0, t0, t1, ALU.add)
            tt(t1, AR[:, :, 3, :], AR[:, :, 3, :], ALU.mult)
            tt(t0, t0, t1, ALU.add)
            tt(t1, A0, A0, ALU.mult)
            tt(t2, A0, W(1), ALU.mult)
            tt(t2, t2, W(0), ALU.add)
            tt(t3, t1, W(3), ALU.mult)
            tt(t2, t2, t3, ALU.add)
            tt(t3, t0, W(4), ALU.mult)
            tt(t2, t2, t3, ALU.add)
            tt(t2, t2, A0, ALU.mult)
            tt(t3, t0, W(2), ALU.mult)
            tt(BR[:, :, 0, :], t2, t3, ALU.add)
            tt(t2, A0, W(6), ALU.mult)
            tt(t2, t2, W(5), ALU.add)
            tt(t3, t1, W(7), ALU.mult)
            tt(t2, t2, t3, ALU.add)
            tt(t3, t0, W(8), ALU.mult)
            tt(t2, t2, t3, ALU.add)
            for x in range(3):
                ins = dve.tensor_tensor(BR[:, :, 1 + x, :], AR[:, :, 1 + x, :], t2, ALU.mult)
            ins.then_inc(S["s_b"], 1)
            dve.wait_ge(S["s_oe"], 8)
            for k in range(2):
                for c in range(4):
                    ins = dve.bn_stats(sto[:, k, c, :], OT[:, k, c * NCH:(c + 1) * NCH])
            link(ins)
            for k in range(2):
                ins = dve.bn_aggr(mvo[:, k, :], sto[:, k, :, :].rearrange("p c s -> p (c s)"))
            link(ins)
            link(dve.tensor_tensor(ss, mvo[:, :, 0], mvo[:, :, 0], ALU.mult))
            dve.tensor_tensor(ss, ss, mvo[:, :, 1], ALU.add).then_inc(S["s_nr"], 1)
            dve.wait_ge(S["s_nre"], 1)
            link(dve.tensor_copy(nrm, ps[:, 0, 0:2]))
            link(dve.tensor_copy(nrm[0:H, 0:1], mvo[0:H, 0, 1:2]))
            dve.tensor_scalar(nrm, nrm, EPS, None, ALU.add).then_inc(S["s_nvar"], 1)
            dve.wait_ge(S["s_nstd"], 1)
            link(dve.reciprocal(osc, nrm))
            link(dve.tensor_tensor(osc, osc, l1v[:, 0, :], ALU.mult))
            link(dve.tensor_tensor(obi, mvo[:, :, 0], osc, ALU.mult))
            link(dve.tensor_tensor(obi, obi, l1v[:, 2, :], ALU.mult))
            link(dve.tensor_tensor(obi, l1v[:, 1, :], obi, ALU.subtract))
            for k in range(2):
                ins = dve.scalar_tensor_tensor(XT[:, k, :], OT[:, k, :], osc[:, k:k + 1], XT[:, k, :], ALU.mult, ALU.add)
            link(ins)
            for k in range(2):
                ins = dve.tensor_scalar(XT[:, k, :], XT[:, k, :], obi[:, k:k + 1], None, ALU.add)
            link(ins)
            link(dve.tensor_copy(wrb, wr.unsqueeze(2).broadcast_to([P, 2, P])))
            dve.sem_inc(xtd[3], 1)
            layer_norm(3)
            for i in range(4):
                dve.wait_ge(S["s_wct"], i + 1)
                dve.tensor_copy(wcol[:, 4 * i:4 * i + 4],
                                ps[:, 4 + i, :].rearrange("p (t c) -> p t c", c=P)[:, :, 0]).then_inc(S["s_wcol"], 1)
            dve.wait_ge(S["s_wcol"], 4)
            link(dve.memset(cnt3[:, 0, 0:1], 0.0))
            for t in range(NT):
                w = wcol[:, t:t + 1]
                if t:
                    link(dve.tensor_scalar(junk[:, 0:t * P], WB[:, 0:t * P], w, 0.0, ALU.is_ge, ALU.add,
                                           accum_out=cnt3[:, 0, t:t + 1]))
                link(dve.tensor_scalar(junk[:, t * P:N], WB[:, t * P:N], w, 0.0, ALU.is_gt, ALU.add,
                                       accum_out=cnt3[:, 1, t:t + 1]))
                link(dve.scalar_tensor_tensor(junk[:, 0:P], WB[:, t * P:(t + 1) * P], w, ltm, ALU.is_equal, ALU.mult,
                                              accum_out=cnt3[:, 2, t:t + 1]))
            link(dve.tensor_tensor(mw, cnt3[:, 0, :], cnt3[:, 1, :], ALU.add))
            link(dve.tensor_tensor(mw, mw, cnt3[:, 2, :], ALU.add))
            link(dve.tensor_scalar(mw, mw, float(SEL), None, ALU.is_lt))
            link(dve.tensor_tensor(mw, mw, wcol, ALU.mult))
            for t in range(NT):
                dve.wait_ge(S["s_yy"], t + 1)
                o = OUTR[:, t, :]
                link(dve.tensor_tensor(o, ps[:, 4 + t % 4, 0:D], fb2, ALU.add))
                link(dve.scalar_tensor_tensor(o, o, mw[:, t:t + 1], ROW[:, t, :], ALU.mult, ALU.add))
                dve.tensor_tensor(o, o, YROW[:, t, :], ALU.add).then_inc(S["s_out"], 1)


def kernel(**inputs):
    import numpy as np
    import concourse.bacc as _bacc
    from concourse.bass_utils import run_bass_kernel_spmd as _run

    I = {k: np.asarray(v) for k, v in inputs.items()}
    perm = np.concatenate([np.arange(64)] + [64 + 3 * np.arange(64) + x for x in range(3)])

    def kt(a):
        k = a.shape[0] // 128
        return np.ascontiguousarray(a.reshape(k, 128, -1).transpose(1, 0, 2).reshape(128, -1))

    def colv(v):
        return np.ascontiguousarray(v.reshape(-1, 128).T)

    def pad64(v):
        return np.concatenate([v, np.zeros(64, np.float32)])

    def blocks(parts):
        a = np.zeros((128, 2, 128), np.float32)
        for n, b in enumerate(parts):
            r = 64 * (n % 2)
            a[r:r + 64, n // 2, r:r + 64] = b
        return a.reshape(128, 256)

    A = {}
    x = I["x"][:, perm]
    A["x"] = np.ascontiguousarray(x)
    A["xT"] = np.ascontiguousarray(x.T)
    A["src_l"] = np.ascontiguousarray(I["src"].reshape(ET, P).T)
    A["dst_l"] = np.ascontiguousarray(I["dst"].reshape(ET, P).T)
    A["dst_r"] = np.ascontiguousarray(I["dst"].reshape(125, 4 * P))
    A["ew"] = np.ascontiguousarray(I["edge_weight"].reshape(ET, P).T)
    A["sh"] = np.ascontiguousarray(I["edge_attr_4"].reshape(ET, P, 4).transpose(1, 0, 2).reshape(P, ET * 4))
    ea = np.zeros((P, (2 * ITERS + 2) * GE), np.float32)
    ea[:, :E] = I["edge_attr_128"].T
    A["eaT"] = ea
    rb = np.zeros(((ITERS + 2) * 2 * GE, 16), np.float32)
    rb[:E] = I["edge_attr_16"]
    A["rbf"] = np.ascontiguousarray(rb.reshape(ITERS + 2, 2, GE, 16).transpose(0, 1, 3, 2).reshape(-1, GE))
    A["ident"] = np.eye(128, dtype=np.float32)
    A["iota8"] = np.tile(np.arange(WIN, dtype=np.float32), (128, 1))
    A["ones"] = np.ones((128, 128), np.float32)
    A["mask32"] = np.kron(np.eye(4), np.ones((32, 32))).astype(np.float32) / np.float32(N)
    A["mask64"] = np.kron(np.eye(2), np.ones((64, 64))).astype(np.float32) / np.float32(N)
    A["ltm"] = np.tril(np.ones((128, 128), np.float32), -1)
    pat = np.zeros((2, 128, 2, 128), np.float32)
    for k in range(2):
        for o in range(2):
            for a in range(2):
                for b in range(2):
                    if (k, a) != (0, 0) and (o, b) != (0, 0):
                        pat[k, 64 * a:64 * a + 64, o, 64 * b:64 * b + 64] = np.eye(64) / 3
    A["pat"] = np.ascontiguousarray(pat.transpose(1, 0, 2, 3).reshape(128, 512))
    g = lambda n: I["L0_gnn_" + n]
    vec = []
    for a in ("g", "be", "m", "v"):
        vec.append(np.concatenate([colv(g(a + "_in")[perm]), colv(pad64(g(a + "_msg"))), colv(pad64(g(a + "_upd"))),
                                   colv(g(a + "_out")[perm])], 1))
    z2 = np.zeros((128, 2), np.float32)
    vec.append(np.concatenate([z2, colv(pad64(g("b1"))), z2[:, :1], colv(g("b2")[perm])], 1))
    A["bnv"] = np.concatenate(vec, 1)
    A["w1g"] = kt(g("w1")[perm])
    A["kw1"] = g("kw1")
    A["kb1r"] = np.tile(g("kb1"), GR)[None]
    A["w2g"] = np.ascontiguousarray(g("w2")[:, perm])
    kw2 = g("kw2").reshape(KH, H + 1, H)
    kb2 = g("kb2").reshape(H + 1, H)
    A["W2S"] = np.ascontiguousarray(kw2[:, 1:, :].reshape(2, 16, H, H).transpose(0, 3, 1, 2).reshape(128, 16 * H))
    A["wV"] = np.concatenate([kb2[1:].T, kb2[:1], kw2[:, 0, :]], 0)
    m = lambda n: I["L0_mix_" + n]
    wq = m("w_qkv")[perm].reshape(D, 8, 3, 32)
    bq = m("b_qkv").reshape(8, 3, 32)
    A["wqT"] = kt(np.ascontiguousarray(wq[:, :, 0].reshape(D, D).T))
    A["bq"] = colv(bq[:, 0].reshape(-1))
    A["wkv"] = kt(np.concatenate([wq[:, :, 1].reshape(D, D), wq[:, :, 2].reshape(D, D)], 1))
    A["bkvr"] = np.concatenate([bq[:, 1].reshape(-1), bq[:, 2].reshape(-1)])[None]
    A["gkv"] = np.tile(np.concatenate([np.tile(m("kln_g"), 8), np.tile(m("vln_g"), 8)]), (128, 1))
    A["bkv"] = np.tile(np.concatenate([np.tile(m("kln_b"), 8), np.tile(m("vln_b"), 8)]), (128, 1))
    A["w1m"] = kt(m("w1"))
    A["w1p"] = kt(m("w1")[perm])
    A["w2m"] = kt(np.ascontiguousarray(m("w2")[:, perm]))
    A["b1c"] = colv(m("b1"))
    A["b2c"] = colv(m("b2")[perm])
    A["wfT"] = kt(np.ascontiguousarray(I["L0_ffn_weight"].T[perm][:, perm]))
    A["bfc"] = colv(I["L0_ffn_bias"][perm])
    g1 = lambda n: I["L1_gnn_" + n]
    A["bu"] = blocks([g1("W_up0")] + [g1("W_up1")] * 3)
    A["bdb"] = blocks([g1("WB0")] + [g1("WB1")] * 3)
    A["bds"] = blocks([g1("Wsc0")] + [g1("Wsc1")] * 3)

    def two(w):
        a = np.zeros((2 * w.shape[0], 128), np.float32)
        a[:w.shape[0], :64] = w
        a[w.shape[0]:, 64:] = w
        return a
    A["m1"], A["m2"], A["m3"] = two(g1("M1")), two(g1("M2")), two(g1("M3"))
    A["m4"] = np.tile(g1("M4"), (2, 1))
    wl = np.zeros((2, 64, NA, 4, 64), np.float32)
    w0, w1 = g1("W_lin0"), g1("W_lin1")
    for half, h in ((0, 0), (0, 2), (1, 3), (0, 6)):
        wl[half, :, h, 0] = w0
    for half, h, c in ((1, 0, 1), (0, 1, 2), (1, 1, 3), (1, 4, 1), (1, 5, 2), (1, 6, 3)):
        wl[half, :, h, c] = w1
    A["wl"] = wl.reshape(128, NA * D)
    A["wc"] = np.tile(np.concatenate([g1("Wc0").T.reshape(-1), g1("Wc1").T.reshape(-1)]), (128, 1))
    gam = np.concatenate([g1("gamma0")] + [g1("gamma1")] * 3)
    bet = np.concatenate([g1("beta0"), np.zeros(192, np.float32)])
    is0 = np.concatenate([np.ones(64, np.float32), np.zeros(192, np.float32)])
    A["l1v"] = np.concatenate([colv(gam), colv(bet), colv(is0)], 1)
    Wqkv = I["L1_mix_Wqkv"][:, perm]
    A["wq1"] = kt(Wqkv[0:512])
    A["wkv1"] = kt(np.ascontiguousarray(Wqkv[512:].T))
    A["woT"] = kt(np.ascontiguousarray(I["L1_mix_Wout"][perm].T))
    A["boc"] = colv(I["L1_mix_bout"][perm])
    f = lambda n: I["L1_ffn_" + n]
    A["wr"] = colv(f("wr")[perm, 0])
    A["brc"] = np.tile(f("br"), (128, 1))
    A["fw1"] = kt(f("w1")[perm])
    A["fb1"] = colv(f("b1"))
    A["fw2"] = kt(np.ascontiguousarray(f("w2")[:, perm]))
    A["fb2"] = np.tile(f("b2")[perm], (128, 1))

    nc = _bacc.Bacc("TRN2", target_bir_lowering=False, num_devices=1)
    arrays, aps = {}, {}
    for name, a in A.items():
        a = np.ascontiguousarray(a)
        assert a.dtype in (np.float32, np.int32), (name, a.dtype)
        arrays["in_" + name] = a
        aps[name] = nc.dram_tensor("in_" + name, a.shape, mybir.dt.from_np(a.dtype), kind="ExternalInput").ap()
    out = nc.dram_tensor("out_0", (N, D), F32, kind="ExternalOutput").ap()
    build(nc, aps, out)
    r = _run(nc, [arrays], core_ids=[0])
    got = r.results[0]["out_0"]
    inv = np.argsort(perm)
    return np.ascontiguousarray(got[:, inv])
```

```python
from contextlib import ExitStack

import concourse.bass as bass
from concourse import mybir

F32 = mybir.dt.float32
I32 = mybir.dt.int32
F32R = mybir.dt.float32r
BF16 = mybir.dt.bfloat16
ALU = mybir.AluOpType
ACT = mybir.ActivationFunctionType
AX = mybir.AxisListType

P = 128
N, D, E = 2000, 256, 64000
NT = (N + P - 1) // P
NPAD = NT * P
LAST = N - (NT - 1) * P
ET = E // P
WIN = 8
NW = N + WIN
H = 64
KH = 32
GR = 5
BODY = 2 * GR
ITERS = ET // BODY
NG = 2 * ITERS + 1
MP = 3 * (ITERS + 1)
SPL = 2 * ITERS + 1
ET2 = ET + 2
AHEAD = 2
HIGH = -4096
GE = GR * P
NCH = 500
EPS = 1e-5
SMALL = 1720
NA = 7
ARENA = 32256
RING = 7744
SEL = N // 2 - 1


class Area:

    def __init__(self, tensor, start, end):
        self.tensor, self.at, self.end = tensor, start, end

    def take(self, n):
        a = self.at
        self.at += n
        assert self.at <= self.end, (self.at, self.end)
        return self.tensor[:, a:a + n]


def build(nc, A, out):
    ctx = ExitStack()
    with ctx:
        def sb(name, cols, dt=F32, parts=P):
            return ctx.enter_context(nc.sbuf_tensor(name, [parts, cols], dt))

        def sem(name):
            return ctx.enter_context(nc.semaphore(name))

        arena = sb("arena", ARENA)
        ring = sb("ring", RING)
        XT = sb("XT", 2 * NPAD)[:, :].rearrange("p (k n) -> p k n", k=2)
        src = sb("src", ET + GR, I32)
        dstF = sb("dstF", ET)
        ewt = sb("ewt", ET + GR)
        LO = sb("LO", ET)
        base = sb("base", ET)
        dloc = sb("dloc", ET + GR)
        baseI = sb("baseI", GR + ET, I32, 1)
        vacc = sb("vacc", NW)
        curI = sb("curI", 2 * GR, I32)
        small = sb("small", SMALL)
        npassI = sb("npassI", 2, I32, 1)
        with ExitStack() as first:
            W2S = first.enter_context(nc.sbuf_tensor("W2S", [P, 16 * H], F32))[:, :].rearrange("p (q j) -> p q j", q=16)
            wfT = first.enter_context(nc.sbuf_tensor("wfT", [P, 512], F32))[:, :].rearrange("p (k c) -> p k c", k=2)
        RS = sb("RS", 2 * GE, F32R)[:, :].rearrange("p (h e) -> p h e", h=2)
        m4s = sb("m4s", 2 * D, F32R)[:, :].rearrange("p (h c) -> p h c", h=2)
        ps = ctx.enter_context(nc.psum_tensor("ps", [P, 8, 512], F32))

        sm = Area(small, 0, SMALL)
        ident = sm.take(P)
        iota8 = sm.take(WIN)
        st = sm.take(NT * 6).rearrange("p (t s) -> p t s", s=6)
        mv = sm.take(NT * 2).rearrange("p (t s) -> p t s", s=2)
        var = sm.take(NT)
        std = sm.take(NT)
        rs = sm.take(NT)
        bnv = sm.take(30).rearrange("p (v c) -> p v c", v=5)
        bns = sm.take(6)
        bnb = sm.take(6)
        bnt = sm.take(6)
        ones = sm.take(P)
        w1g = sm.take(2 * H).rearrange("p (k h) -> p k h", k=2)
        kw1 = sm.take(KH)
        kb1r = sm.take(KH)
        k2 = sm.take(KH)
        kb2 = sm.take(KH)
        k3 = sm.take(KH // 2).bitcast(BF16)
        kb3 = sm.take(KH // 2).bitcast(BF16)
        w2g = sm.take(D)
        wV = sm.take(H)
        bq = sm.take(2)
        b1c = sm.take(2)
        b2c = sm.take(2)
        bfc = sm.take(2)
        boc = sm.take(2)
        bvec = sm.take(2)
        l1v = sm.take(6).rearrange("p (v c) -> p v c", v=3)
        mvo = sm.take(4).rearrange("p (k s) -> p k s", k=2)
        sto = sm.take(2 * 4 * 6).rearrange("p (k c s) -> p k c s", k=2, c=4)
        ss = sm.take(2)
        nrm = sm.take(2)
        osc = sm.take(2)
        obi = sm.take(2)
        brc = sm.take(1)
        fb1 = sm.take(8)
        wcol = sm.take(NT)
        cnt3 = sm.take(3 * NT).rearrange("p (c t) -> p c t", c=3)
        mw = sm.take(NT)
        wr = sm.take(2)
        wmean = sm.take(32)

        def rows(off):
            return arena[:, off:off + NT * D].rearrange("p (t d) -> p t d", d=D)

        def cols(off, k=2):
            return arena[:, off:off + k * NPAD].rearrange("p (k n) -> p k n", k=k)

        YT = cols(0)
        ROW = rows(4096)
        YROW = rows(8192)
        LT = cols(12288)
        H1T = LT
        MT = arena[0:H, 16384:16384 + NPAD]
        KC = arena[:, 18432:18432 + NT * 512].rearrange("p (t g c) -> p t g c", t=NT, c=32)
        MROW = arena[:, 26624:26624 + NT * H].rearrange("p (t h) -> p t h", h=H)
        SQ = arena[:, 27648:28672].rearrange("p (b c) -> p b c", b=2)
        a1 = Area(arena, 28672, 32256)
        wkv = a1.take(1024).rearrange("p (k c) -> p k c", k=2)
        wqT = a1.take(512).rearrange("p (k c) -> p k c", k=2)
        w1m = a1.take(512).rearrange("p (k c) -> p k c", k=2)
        w1p = a1.take(512).rearrange("p (k c) -> p k c", k=2)
        w2m = a1.take(512).rearrange("p (k c) -> p k c", k=2)
        mask32 = a1.take(P)
        VS = a1.take(NT * 16)
        r0 = Area(ring, 0, RING)
        MR = r0.take(BODY * (H + 1 + KH)).rearrange("p (s c) -> p s c", s=BODY)
        RM = r0.take(2 * GR * WIN * (KH + 1)).rearrange("p (g t c) -> p g t c", g=2, t=GR)
        SW = RM[:, :, :, WIN * KH:]
        EA = r0.take(2 * GE).rearrange("p (g e) -> p g e", g=2)
        ru = r0.at
        U = ring[0:H, ru:ru + NPAD]
        re = Area(ring, ru, RING)
        EA2 = re.take(2 * GE).rearrange("p (g e) -> p g e", g=2)
        EA3 = re.take(GE).bitcast(BF16).rearrange("p (g e) -> p g e", g=2)
        gkv = r0.take(512)
        bkvr = r0.take(512)[0:1, :]
        bkv = r0.take(512)
        KVM = r0.take(2 * P).rearrange("p (g c) -> p g c", g=2)
        AM = r0.take(512).rearrange("p (g c) -> p g c", g=2)
        GM = r0.take(512).rearrange("p (g c) -> p g c", g=2)
        dr = arena[0:125, 0:512]
        drI = ring[0:125, 0:512].bitcast(I32)
        dstI = ring[:, 512:512 + ET].bitcast(I32)
        lohi = sm.take(8)
        span = sm.take(2)

        acc = arena[:, 0:NW * 16].rearrange("p (n q) -> p n q", q=16)

        KV1 = arena[:, 4096:4096 + NT * 1024].rearrange("p (t g c) -> p t g c", t=NT, c=64)
        a2 = Area(arena, 20480, 26752)
        wkv1 = a2.take(2048).rearrange("p (k c) -> p k c", k=2)
        wq1 = a2.take(1024).rearrange("p (k c) -> p k c", k=4)
        woT = a2.take(1024).rearrange("p (k c) -> p k c", k=4)
        bu = a2.take(256).rearrange("p (k c) -> p k c", k=2)
        mask64 = a2.take(P)
        a2.at = 26112
        m1 = a2.take(P)
        m2 = a2.take(P)
        m3 = a2.take(P)
        m4 = a2.take(D)
        UPR = rows(26752)
        SQ1 = arena[:, 30848:31872]
        r1a = Area(ring, 0, RING)
        KVM1 = r1a.take(4 * P).rearrange("p (g c) -> p g c", g=4)
        AM1 = r1a.take(1024).rearrange("p (g c) -> p g c", g=4)
        GM1 = r1a.take(512).rearrange("p (g c) -> p g c", g=2)
        VS1 = r1a.take(NT * 16)
        RK1 = r1a.take(NT * 8)

        acc1 = arena[:, 4096:4096 + NA * NPAD].rearrange("p (h n) -> p h n", h=NA)
        a3 = Area(arena, 4096 + NA * NPAD, 26112)
        G1 = a3.take(BODY * D).rearrange("p (s c) -> p s c", s=BODY)
        PP = a3.take(BODY * 6 * H).rearrange("p (s b c) -> p s b c", s=BODY, b=6)
        a3b = Area(arena, 26752, ARENA)
        R1 = a3b.take(GE)
        R2 = a3b.take(GE)
        R3 = a3b.take(GE)
        RBF = a3b.take(GE * 2).rearrange("p (g e) -> p g e", g=2)
        S5 = a3b.take(2 * GR * 5 * WIN).rearrange("p (g t k w) -> p g t k w", g=2, t=GR, k=5)
        XS = a3b.take(GR * 3 * H).rearrange("p (t x c) -> p t x c", t=GR, x=3)
        XU = a3b.take(2 * GR * H).rearrange("p (g t c) -> p g t c", g=2, t=GR)
        r3 = Area(ring, 0, 2432)
        shv = r3.take((ET + GR) * 4).rearrange("p (t k) -> p t k", k=4)
        UP12 = ring[:, RING - GE:]

        AR = arena[:, 18432:22528].rearrange("p (t b c) -> p t b c", b=4, c=64)
        BR = arena[:, 4096:8192].rearrange("p (t b c) -> p t b c", b=4, c=64)
        TMP = [arena[:, 8192 + 1024 * i:9216 + 1024 * i].rearrange("p (t c) -> p t c", c=64) for i in range(4)]
        BT = cols(12320)
        OT = cols(18432)
        HT = cols(12320, 8)
        WB = arena[:, 28704:28704 + NPAD]
        r4 = Area(ring, 2432, RING)
        wl = vacc[:, 0:NA * D].rearrange("p (h c) -> p h c", h=NA)
        bdb = r4.take(256).rearrange("p (k c) -> p k c", k=2)
        bds = r4.take(256).rearrange("p (k c) -> p k c", k=2)
        wc = r4.take(9 * 64).rearrange("p (v c) -> p v c", v=9)
        pat = r4.take(512).rearrange("p (a b c) -> p a b c", a=2, b=2)
        wrb = r4.take(256).rearrange("p (k c) -> p k c", k=2)
        ltm = r4.take(P)
        fb2 = r4.take(256)
        fw1 = ring[:, 0:2048].rearrange("p (k c) -> p k c", k=2)
        fw2 = r4.take(2048).rearrange("p (m c) -> p m c", m=8)
        OUTR = XT.rearrange("p k n -> p (k n)").rearrange("p (t d) -> p t d", d=D)
        junk = XT[:, 0, 0:N]

        mtab = nc.dram_tensor("mtab", [NPAD, H], F32, kind="Internal").ap()
        utab = nc.dram_tensor("utab", [NPAD, D], F32, kind="Internal").ap()
        lod = nc.dram_tensor("lod", [ET], F32, kind="Internal").ap()

        S = {n: sem(n) for n in (
            "s_zero", "s_idx", "s_const", "s_x", "s_w0", "s_lod", "s_lo", "s_npass", "s_dve", "s_act", "s_span",
            "s_bnvar", "s_bnstd", "s_bn", "s_lt", "s_msg", "s_mt", "s_mtr", "s_mrow", "s_mtab",
            "s_wc", "s_kv", "s_kvc", "s_kvr", "s_vs", "s_vstd", "s_kvn", "s_kvt", "s_kvm", "s_A", "s_Am",
            "s_G", "s_Gm", "s_bv", "s_bvm", "s_h1", "s_h1e", "s_mo", "s_xt0",
            "s_acc0p",
            "s_er", "s_ea", "s_rest", "s_k", "s_rready", "s_mask", "s_seg", "s_rmw", "s_curI", "s_step", "s_base",
            "s_u", "s_ue", "s_o0", "s_w1", "s_ff", "s_up", "s_upr", "s_utab", "s_w4", "s_fw1",
            "s_kv1", "s_k1c", "s_k1s", "s_v1r", "s_v1std", "s_v1n", "s_kvt1", "s_kvm1", "s_A1", "s_Am1", "s_G1", "s_Gm1",
            "s_y1", "s_xt3", "s_acc1", "s_mlp", "s_silu", "s_T", "s_prod", "s_seg1", "s_rmw1", "s_curI1", "s_oh", "s_pass1", "s_split", "s_half",
            "s_ar", "s_are", "s_b", "s_bt", "s_bte", "s_o", "s_oe", "s_nr", "s_nre", "s_nvar", "s_nstd",
            "s_wb", "s_wbe", "s_wct", "s_wcol", "s_hh", "s_he", "s_yy", "s_out", "s_store", "s_base1")}
        lnr = [[sem(f"{w}{n}") for n in range(4)] for w in ("rowT", "row", "lnvar", "lnstd", "lny", "colT", "col", "xt")]
        rowT, row, lnvar, lnstd, lny, colT, col, xtd = lnr
        gath = [sem(f"gath{k}") for k in range(BODY)]
        eal = [sem(f"eal{k}") for k in range(2)]
        rbl = [sem(f"rbl{k}") for k in range(2)]

        block = ctx.enter_context(nc.Block())
        bcast = lambda ap, shape: ap.broadcast_to(shape)
        NLOAD = {}

        def top(a):
            return a.bitcast(BF16).rearrange("p (n b) -> p n b", b=2)[:, :, 1]

        def place(slot):
            g, pos = divmod(slot, GR)
            return 2 + 2 * g + pos // 3, pos % 3 * (P + WIN)

        def outer(slot):
            b, c = place(slot)
            return ps[:, b, c:c + P]

        def affine(slot):
            b, c = place(slot)
            return ps[:, b, c + P:c + P + WIN]

        def sums(T):
            return ps[:, 6 + T % 2, 0:NA * WIN].rearrange("p (h w) -> p h w", h=NA)

        def weights_of(T):
            return ps[:, 2 + T % 4, 0:D]

        def vload(eng):
            eng.wait_ge(S["s_npass"], 1)
            return eng.value_load(npassI[0:1, 0:1], min_val=1, max_val=N // WIN + 1)

        @block.sync
        def _(sp):
            def ld(dst, a, s):
                NLOAD[s] = NLOAD.get(s, 0) + 1
                return sp.dma_start(dst, a).then_inc(S[s], 16)

            ld(drI, A["dst_r"], "s_idx")
            ld(dstI, A["dst_l"], "s_idx")
            sp.wait_ge(S["s_zero"], 2)
            ld(ROW[:, 0:NT - 1, :], A["x"][0:(NT - 1) * P, :].rearrange("(t p) d -> p t d", p=P), "s_x")
            ld(ROW[0:LAST, NT - 1, :], A["x"][(NT - 1) * P:N, :], "s_x")
            ld(ident, A["ident"], "s_const")
            ld(iota8, A["iota8"], "s_const")
            ld(bnv.rearrange("p v c -> p (v c)"), A["bnv"], "s_const")
            ld(ones, A["ones"], "s_const")
            ld(src[:, :], A["src_l"], "s_const")
            ld(ewt[:, 0:ET], A["ew"], "s_const")
            ld(mask32, A["mask32"], "s_const")
            ld(w1g.rearrange("p k h -> p (k h)"), A["w1g"], "s_const")
            for d_, n_ in ((kw1, "kw1"), (kb1r[0:1, :], "kb1r"), (w2g[0:H, :], "w2g"), (wV, "wV"),
                           (bq, "bq"), (b1c, "b1c"), (b2c, "b2c"), (bfc, "bfc"), (boc, "boc"),
                           (l1v.rearrange("p v c -> p (v c)"), "l1v"), (brc, "brc"), (fb1, "fb1"), (wr, "wr"),
                           (bkvr, "bkvr"), (gkv, "gkv"), (bkv, "bkv"),
                           (wkv.rearrange("p k c -> p (k c)"), "wkv"), (wqT.rearrange("p k c -> p (k c)"), "wqT"),
                           (w1m.rearrange("p k c -> p (k c)"), "w1m"), (w1p.rearrange("p k c -> p (k c)"), "w1p"),
                           (w2m.rearrange("p k c -> p (k c)"), "w2m"), (W2S.rearrange("p q j -> p (q j)"), "W2S"),
                           (wfT.rearrange("p k c -> p (k c)"), "wfT")):
                ld(d_, A[n_], "s_w0")
            for k in range(2):
                ld(XT[:, k, 0:N], A["xT"][k * P:(k + 1) * P, :], "s_w0")
            sp.wait_ge(S["s_span"], 1)
            sp.dma_start(lod.rearrange("(p q) -> p q", q=4), lohi[0:125, 0:4]).then_inc(S["s_lod"], 16)
            sp.wait_ge(S["s_lod"], 16)
            sp.dma_start(LO[:, :], lod.rearrange("(a n) -> a n", a=1).broadcast_to([P, ET])).then_inc(S["s_lo"], 16)
            sp.wait_ge(S["s_mrow"], 2)
            sp.dma_start(mtab.rearrange("(t p) h -> p t h", p=P), MROW).then_inc(S["s_mtab"], 16)

            npass = vload(sp)

            def load_ea(count, group, par):
                sp.wait_ge(S["s_er"], count)
                sp.dma_start(EA[:, par, :], A["eaT"][:, bass.ds(group * GE, GE)]).then_inc(eal[par], 16)

            with sp.Fori(0, npass) as j:
                sp.wait_ge(S["s_er"], j * NG + 2)
                sp.sem_inc(S["s_step"], 1)
                sp.wait_ge(S["s_ea"], j * (NG + 1) + 1)
                sp.sem_inc(S["s_step"], 1)
                with sp.Fori(0, ITERS + 1) as i:
                    for g in range(2):
                        load_ea(j * NG + 2 * i + g + 1, 2 * i + g, g)
                sp.wait_ge(eal[1], (j + 1) * (ITERS + 1) * 16)
                sp.sem_inc(S["s_step"], 1)
            sp.wait_ge(S["s_ue"], 4)
            for d_, n_ in ((wkv1.rearrange("p k c -> p (k c)"), "wkv1"), (wq1.rearrange("p k c -> p (k c)"), "wq1"),
                           (woT.rearrange("p k c -> p (k c)"), "woT"), (bu.rearrange("p k c -> p (k c)"), "bu"),
                           (m1[0:32, :], "m1"), (m2, "m2"), (m3, "m3"), (m4, "m4"), (mask64, "mask64")):
                ld(d_, A[n_], "s_w1")
            sp.wait_ge(S["s_o0"], 8)
            for d_, n_ in ((wl.rearrange("p k c -> p (k c)"), "wl"), (bdb.rearrange("p k c -> p (k c)"), "bdb"),
                           (bds.rearrange("p k c -> p (k c)"), "bds"), (wc.rearrange("p k c -> p (k c)"), "wc"),
                           (pat.rearrange("p a b c -> p (a b c)"), "pat"), (ltm, "ltm"), (fb2, "fb2"),
                           (fw2.rearrange("p m c -> p (m c)"), "fw2")):
                ld(d_, A[n_], "s_w4")
            sp.wait_ge(S["s_upr"], 8)
            sp.dma_start(utab.rearrange("(t p) h -> p t h", p=P), UPR).then_inc(S["s_utab"], 16)
            sp.wait_ge(S["s_xt3"], 8)
            sp.wait_ge(S["s_utab"], 16)
            sp.dma_start(shv.rearrange("p t k -> p (t k)"), A["sh"]).then_inc(S["s_utab"], 16)
            with sp.Fori(0, npass) as j:
                sp.wait_ge(S["s_mlp"], j * MP + 6)
                sp.sem_inc(S["s_step"], 1)
                with sp.Fori(0, (ITERS + 2) // 2) as i:
                    for g in range(2):
                        sp.wait_ge(S["s_mlp"], j * MP + 3 * (2 * i + g) + 1)
                        sp.dma_start(RBF[0:32, g, :],
                                     A["rbf"][bass.ds((2 * i + g) * 32, 32), :]).then_inc(rbl[g], 16)
                sp.wait_ge(rbl[1], (j + 1) * ((ITERS + 2) // 2) * 16)
                sp.sem_inc(S["s_step"], 1)
            sp.wait_ge(S["s_base1"], 1)
            ld(fw1.rearrange("p k c -> p (k c)"), A["fw1"], "s_fw1")
            for t in range(NT):
                sp.wait_ge(S["s_out"], t + 1)
                n = P if t < NT - 1 else LAST
                sp.dma_start(out[t * P:t * P + n, :], OUTR[0:n, t, :]).then_inc(S["s_store"], 16)
            sp.wait_ge(S["s_store"], 16 * NT)

        @block.gpsimd
        def _(pool):
            npass = vload(pool)

            def gather_group(free, n, t0, h, table, width, ring_, used, copied):
                pool.wait_ge(used, free)
                pool.sem_inc(S["s_step"], 1)
                pool.tensor_copy(curI[:, h * GR:(h + 1) * GR], src[:, bass.ds(t0, GR)]).then_inc(copied, 1)
                pool.wait_ge(copied, n)
                pool.sem_inc(S["s_step"], 1)
                for slot in range(h * GR, (h + 1) * GR):
                    pool.indirect_dma_start(ring_[:, slot, 0:width], None, table,
                                            bass.IndirectOffsetOnAxis(ap=curI[:, slot:slot + 1], axis=0)
                                            ).then_inc(gath[slot], 16)

            pool.wait_ge(S["s_mtab"], 16)
            with pool.Fori(0, npass) as j:
                with pool.Fori(0, ITERS) as i:
                    for h in range(2):
                        gather_group(j * 2 * ITERS + 2 * i + h + 1, j * 2 * ITERS + 2 * i + h + 1,
                                     i * BODY + h * GR, h, mtab, H, MR, S["s_seg"], S["s_curI"])
            pool.wait_ge(S["s_utab"], 32)
            pool.wait_ge(S["s_xt3"], 8)
            with pool.Fori(0, npass) as j:
                pool.wait_ge(S["s_pass1"], j + 1)
                pool.sem_inc(S["s_step"], 1)
                with pool.Fori(0, ITERS) as i:
                    for h in range(2):
                        gather_group(j * ET + i * BODY + (h + 1) * GR, j * NG + 2 * i + h + 1, i * BODY + h * GR, h,
                                     utab, D, G1, S["s_prod"], S["s_curI1"])
                gather_group((j + 1) * ET + GR, (j + 1) * NG, ET, 0, utab, D, G1, S["s_prod"], S["s_curI1"])

        @block.scalar
        def _(act):
            n = [0]

            def link(ins):
                n[0] += 1
                ins.then_inc(S["s_act"], 1)
                act.wait_ge(S["s_act"], n[0])

            def rows_and_std(v):
                if v:
                    for i in range(NT // 2):
                        act.wait_ge(rowT[v], i + 1)
                        act.activation(ROW[:, 2 * i:2 * i + 2, :].rearrange("p t d -> p (t d)"),
                                       ps[:, 4 + i % 4, :], ACT.Copy).then_inc(row[v], 1)
                act.wait_ge(lnvar[v], 1)
                act.activation(std, var, ACT.Sqrt).then_inc(lnstd[v], 1)

            def cols_out(v):
                for i in range(NT // 2):
                    c, k = divmod(i, 2)
                    act.wait_ge(colT[v], i + 1)
                    act.activation(YT[:, k, 512 * c:512 * c + 512], ps[:, i % 4, :], ACT.Copy).then_inc(col[v], 1)

            act.wait_ge(S["s_bnvar"], 1)
            act.activation(bns, bnt, ACT.Sqrt).then_inc(S["s_bnstd"], 1)
            rows_and_std(0)
            cols_out(0)
            act.wait_ge(col[0], 8)
            act.wait_ge(S["s_bn"], 1)
            for k in range(2):
                act.activation(LT[:, k, :], YT[:, k, :], ACT.Relu, bias=bnb[:, k:k + 1],
                               scale=bns[:, k:k + 1]).then_inc(S["s_lt"], 1)
            for c in range(4):
                act.wait_ge(S["s_msg"], c + 1)
                act.activation(MT[:, 512 * c:512 * c + 512], ps[0:H, c, :], ACT.Relu, bias=bnb[0:H, 2:3],
                               scale=bns[0:H, 2:3]).then_inc(S["s_mt"], 1)
            for t in range(NT):
                act.wait_ge(S["s_kv"], t + 1)
                act.activation(KC[:, t, :, :].rearrange("p g c -> p (g c)"), ps[:, t % 4, :],
                               ACT.Copy).then_inc(S["s_kvc"], 1)
                if t >= 2:
                    act.wait_ge(S["s_vs"], t - 1)
                act.activation(SQ[:, t % 2, :], ps[:, t % 4, :], ACT.Square).then_inc(S["s_kvr"], 1)
            act.wait_ge(S["s_vs"], NT + 1)
            act.activation(VS, VS, ACT.Sqrt).then_inc(S["s_vstd"], 1)
            for i in range(8):
                c, o = divmod(i, 2)
                act.wait_ge(S["s_h1"], i + 1)
                if i == 0:
                    act.wait_ge(S["s_bvm"], 1)
                act.activation(H1T[:, o, 512 * c:512 * c + 512], ps[:, i % 4, :], ACT.Gelu,
                               bias=bvec[:, o:o + 1]).then_inc(S["s_h1e"], 1)
            act.wait_ge(S["s_xt0"], 16)
            act.wait_ge(S["s_mtab"], 16)
            act.memzero(arena[:, 20000:NW * 16]).then_inc(S["s_acc0p"], 1)

            npass = vload(act)
            def relu(par, lead, free):
                act.wait_ge(S["s_er"], lead)
                act.wait_ge(S["s_seg"], free)
                act.activation(MR[:, par * GR:(par + 1) * GR, H + 1:],
                               ps[:, par, 0:GR * KH].rearrange("p (t q) -> p t q", t=GR),
                               ACT.Relu).then_inc(S["s_rready"], 1)

            with act.Fori(0, npass) as j:
                relu(0, j * NG + 3, j * 2 * ITERS + 1)
                with act.Fori(0, ITERS) as i:
                    for g in range(2):
                        relu(1 - g, j * NG + 2 * i + g + 4, (j * ITERS + i) * 2 + g + 2)
            for c in range(4):
                act.wait_ge(S["s_u"], c + 1)
                act.activation(U[:, NCH * c:NCH * (c + 1)], ps[0:H, c, 0:NCH], ACT.Relu, bias=bnb[0:H, 3:4],
                               scale=bns[0:H, 3:4]).then_inc(S["s_ue"], 1)
            rows_and_std(1)
            cols_out(1)
            rows_and_std(2)
            cols_out(2)
            for i in range(NT // 2):
                act.wait_ge(S["s_up"], i + 1)
                act.activation(UPR[:, 2 * i:2 * i + 2, :].rearrange("p t d -> p (t d)"), ps[:, 4 + i % 4, :],
                               ACT.Copy).then_inc(S["s_upr"], 1)
            for t in range(NT):
                act.wait_ge(S["s_kv1"], t + 1)
                b = 2 * (t % 2)
                act.activation(KV1[:, t, :, :].rearrange("p g c -> p (g c)"),
                               ps[:, b:b + 2, :].rearrange("p b c -> p (b c)"), ACT.Copy).then_inc(S["s_k1c"], 1)
                if t >= 1:
                    act.wait_ge(S["s_v1r"], t)
                act.activation(SQ1, ps[:, b:b + 2, :].rearrange("p b c -> p (b c)"),
                               ACT.Square).then_inc(S["s_k1s"], 1)
            act.wait_ge(S["s_v1r"], NT + 1)
            act.activation(VS1, VS1, ACT.Sqrt).then_inc(S["s_v1std"], 1)
            def silu(count, dst, free=None):
                act.wait_ge(S["s_mlp"], count + 6)
                if free is not None:
                    act.wait_ge(*free)
                act.activation(dst.rearrange("p (b e) -> p b e", b=2), ps[:, 0:2, 0:GE // 2],
                               ACT.Silu).then_inc(S["s_silu"], 1)

            mp = MP
            with act.Fori(0, npass) as j:
                silu(j * mp + 1, R1)
                silu(j * mp + 2, R2)
                silu(j * mp + 3, R3, (S["s_split"], j * SPL + 1))
                with act.Fori(0, ITERS) as i:
                    silu(j * mp + 3 * i + 4, R1)
                    silu(j * mp + 3 * i + 5, R2)
                    silu(j * mp + 3 * i + 6, R3, (S["s_split"], j * SPL + 2 * i + 3))
            for i in range(NT // 2):
                act.wait_ge(S["s_ar"], i + 1)
                act.activation(AR[:, 2 * i:2 * i + 2, :, :].rearrange("p t b c -> p (t b c)"), ps[:, 4 + i % 4, :],
                               ACT.Copy).then_inc(S["s_are"], 1)
            for i in range(NT // 2):
                c, k = divmod(i, 2)
                act.wait_ge(S["s_bt"], i + 1)
                act.activation(BT[:, k, 512 * c:512 * c + 512], ps[:, i % 4, :], ACT.Copy).then_inc(S["s_bte"], 1)
            for i in range(8):
                c, k = divmod(i, 2)
                act.wait_ge(S["s_o"], i + 1)
                act.activation(OT[:, k, 512 * c:512 * c + 512], ps[:, 4 + i % 4, :], ACT.Copy).then_inc(S["s_oe"], 1)
            act.wait_ge(S["s_nvar"], 1)
            act.activation(nrm, nrm, ACT.Sqrt).then_inc(S["s_nstd"], 1)
            rows_and_std(3)
            cols_out(3)
            for c in range(4):
                act.wait_ge(S["s_wb"], c + 1)
                act.activation(WB[:, 512 * c:512 * c + 512], ps[:, 4 + c, :], ACT.Identity,
                               bias=brc[:, 0:1]).then_inc(S["s_wbe"], 1)
            for i in range(32):
                c, m = divmod(i, 8)
                act.wait_ge(S["s_hh"], i + 1)
                act.activation(HT[:, m, 512 * c:512 * c + 512], ps[:, i % 4, :], ACT.Gelu_apprx_tanh,
                               bias=fb1[:, m:m + 1]).then_inc(S["s_he"], 1)

        @block.tensor
        def _(pe):
            def to_rows(v):
                pe.wait_ge(xtd[v], 1)
                for i in range(NT // 2):
                    if i >= 4:
                        pe.wait_ge(row[v], i - 3)
                    for t in range(2):
                        for k in range(2):
                            tr = pe.transpose(ps[:, 4 + i % 4, t * D + k * P:t * D + (k + 1) * P],
                                              XT[:, k, (2 * i + t) * P:(2 * i + t + 1) * P], ident)
                    tr.then_inc(rowT[v], 1)

            def to_cols(v):
                for i in range(NT // 2):
                    c, k = divmod(i, 2)
                    pe.wait_ge(lny[v], 4 * c + 4)
                    if i >= 4:
                        pe.wait_ge(col[v], i - 3)
                    for t in range(4):
                        tr = pe.transpose(ps[:, i % 4, t * P:(t + 1) * P], YROW[:, 4 * c + t, k * P:(k + 1) * P], ident)
                    tr.then_inc(colT[v], 1)

            pe.wait_ge(S["s_const"], 16 * NLOAD["s_const"])
            pe.wait_ge(S["s_idx"], 32)
            pe.wait_ge(S["s_span"], 1)
            pe.transpose(ps[0:1, 7, 0:125], span[0:125, 0:1], ident[0:125, 0:125]).then_inc(S["s_span"], 1)
            to_cols(0)
            for c in range(4):
                pe.wait_ge(S["s_lt"], 2)
                for k in range(2):
                    mm = pe.matmul(ps[0:H, c, :], w1g[:, k, :], LT[:, k, 512 * c:512 * c + 512],
                                   start=(k == 0), stop=(k == 1))
                mm.then_inc(S["s_msg"], 1)
            for i in range(2):
                pe.wait_ge(S["s_mt"], 2 * i + 2)
                for t in range(8):
                    n = 8 * i + t
                    tr = pe.transpose(ps[:, 4 + i, t * H:(t + 1) * H], MT[:, n * P:(n + 1) * P], ident[0:H, 0:H])
                tr.then_inc(S["s_mtr"], 1)
            pe.wait_ge(S["s_w0"], 16 * NLOAD["s_w0"])
            pe.wait_ge(S["s_wc"], 1)
            pe.wait_ge(S["s_mt"], 4)
            for t in range(NT):
                if t >= 4:
                    pe.wait_ge(S["s_kvr"], t - 3)
                b = ps[:, t % 4, :]
                for k in range(2):
                    pe.matmul(b, YT[:, k, t * P:(t + 1) * P], wkv[:, k, :], start=(k == 0), stop=False)
                pe.matmul(b, ones[0:1, :], bkvr, start=False, stop=True).then_inc(S["s_kv"], 1)
            for g in range(2):
                for t in range(NT):
                    pe.wait_ge(S["s_kvn"], t + 1)
                    r = P if t < NT - 1 else LAST
                    KCf = KC[0:r, t, :, :].rearrange("p g c -> p (g c)")
                    mm = pe.matmul(ps[:, 6, g * P:(g + 1) * P], KCf[:, 256 + g * P:256 + (g + 1) * P],
                                   KCf[:, g * P:(g + 1) * P], start=(t == 0), stop=(t == NT - 1))
            mm.then_inc(S["s_kvt"], 1)
            pe.wait_ge(S["s_kvm"], 1)
            for g in range(2):
                mm = pe.matmul(ps[:, 4, g * D:(g + 1) * D], KVM[:, g, :], w1m[:, g, :], start=True, stop=True)
            mm.then_inc(S["s_A"], 1)
            pe.wait_ge(S["s_Am"], 1)
            for c in range(2):
                for g in range(2):
                    mm = pe.matmul(ps[:, 5, c * D:(c + 1) * D], wqT[:, g, c * P:(c + 1) * P], AM[:, g, :],
                                   start=(g == 0), stop=(g == 1))
            mm.then_inc(S["s_G"], 1)
            for o in range(2):
                for g in range(2):
                    mm = pe.matmul(ps[:, 7, o:o + 1], AM[:, g, o * P:(o + 1) * P], bq[:, g:g + 1],
                                   start=(g == 0), stop=(g == 1))
            mm.then_inc(S["s_bv"], 1)
            pe.wait_ge(S["s_Gm"], 1)
            pe.wait_ge(S["s_bvm"], 1)
            for i in range(8):
                c, o = divmod(i, 2)
                if i >= 4:
                    pe.wait_ge(S["s_h1e"], i - 3)
                for k in range(2):
                    mm = pe.matmul(ps[:, i % 4, :], GM[:, k, o * P:(o + 1) * P], YT[:, k, 512 * c:512 * c + 512],
                                   start=(k == 0), stop=(k == 1))
                mm.then_inc(S["s_h1"], 1)
            for i in range(8):
                c, o = divmod(i, 2)
                pe.wait_ge(S["s_h1e"], 2 * c + 2)
                if i >= 4:
                    pe.wait_ge(S["s_xt0"], i - 3)
                for k in range(2):
                    mm = pe.matmul(ps[:, 4 + i % 4, :], w2m[:, k, o * P:(o + 1) * P], H1T[:, k, 512 * c:512 * c + 512],
                                   start=(k == 0), stop=(k == 1))
                mm.then_inc(S["s_mo"], 1)

            npass = vload(pe)
            pe.wait_ge(S["s_xt0"], 16)
            pe.sem_inc(S["s_er"], 2)
            pe.sem_inc(S["s_seg"], 2)

            def edge_net(par, ready, free):
                pe.wait_ge(S["s_ea"], ready)
                pe.wait_ge(S["s_rready"], free) if free is not None else None
                for t in range(GR):
                    r = ps[:, par, t * KH:(t + 1) * KH]
                    e = slice(t * P, (t + 1) * P)
                    for n, b in enumerate((top(kb1r[0:1, :]), top(kb2[0:1, :]), kb3[0:1, :])):
                        pe.matmul(r, top(ones[0:1, :]), b, start=(n == 0), stop=False)
                    e1, e2, e3 = top(EA[:, par, e]), top(EA2[:, par, e]), EA3[:, par, e]
                    for a_, b in ((e1, top(kw1)), (e1, top(k2)), (e1, k3), (e2, top(kw1)), (e2, top(k2)), (e3, top(kw1))):
                        mm = pe.matmul(r, a_, b, start=False, stop=(a_ is e3))
                mm.then_inc(S["s_er"], 1)

            def segments(j, i, g):
                pe.wait_ge(S["s_mask"], j * NG + 2 * i + g + 1)
                pe.wait_ge(S["s_rmw"], j * (ET + GR) + i * BODY + g * GR + 1)
                for t in range(GR):
                    slot = g * GR + t
                    pe.wait_ge(gath[slot], (j * ITERS + i + 1) * 16)
                    b, c = place(slot)
                    pe.matmul(ps[0:H, b, c:c + P], MR[:, slot, 0:H], RM[:, g, t, 0:P], start=True, stop=True)
                    pe.matmul(ps[H:P, b, c:c + P + WIN], MR[:, slot, 0:H], RM[:, g, t, P:], start=True, stop=True)
                    mm = pe.matmul(affine(slot)[0:H, :], MR[:, slot, KH + 1:], SW[:, g, t, :], start=True, stop=True)
                mm.then_inc(S["s_seg"], 1)

            with pe.Fori(0, npass) as j:
                edge_net(0, j * (NG + 1) + 2, None)
                with pe.Fori(0, ITERS) as i:
                    edge_net(1, j * (NG + 1) + 2 * i + 3, j * (2 * ITERS + 1) + 2 * i + 1)
                    segments(j, i, 0)
                    edge_net(0, j * (NG + 1) + 2 * i + 4, j * (2 * ITERS + 1) + 2 * i + 2)
                    segments(j, i, 1)
                pe.wait_ge(S["s_rready"], (j + 1) * NG)
            pe.wait_ge(S["s_base"], 1)
            for c in range(4):
                pe.matmul(ps[0:H, c, 0:NCH], wV, vacc[:, c * NCH:(c + 1) * NCH],
                          start=True, stop=False)
                for q in range(16):
                    mm = pe.matmul(ps[0:H, c, 0:NCH], W2S[:, q, :], acc[:, c * NCH:(c + 1) * NCH, q],
                                   start=False, stop=(q == 15))
                mm.then_inc(S["s_u"], 1)
            for i in range(8):
                c, o = divmod(i, 2)
                pe.wait_ge(S["s_ue"], c + 1)
                if i >= 4:
                    pe.wait_ge(S["s_o0"], i - 3)
                pe.matmul(ps[:, 4 + i % 4, 0:NCH], w2g[0:H, o * P:(o + 1) * P], U[:, c * NCH:(c + 1) * NCH],
                          start=True, stop=True).then_inc(S["s_mo"], 1)
            to_rows(1)
            to_cols(1)
            for i in range(8):
                c, o = divmod(i, 2)
                pe.wait_ge(col[1], 2 * c + 2)
                pe.wait_ge(S["s_ff"], i - 3) if i >= 4 else pe.wait_ge(row[1], 8)
                for k in range(2):
                    mm = pe.matmul(ps[:, 4 + i % 4, :], wfT[:, k, o * P:(o + 1) * P], YT[:, k, 512 * c:512 * c + 512],
                                   start=(k == 0), stop=(k == 1))
                mm.then_inc(S["s_mo"], 1)
            to_rows(2)
            to_cols(2)
            pe.wait_ge(S["s_w1"], 16 * NLOAD["s_w1"])
            pe.wait_ge(row[2], 8)
            for i in range(NT // 2):
                pe.wait_ge(col[2], 2 * (i // 2) + 2)
                if i >= 4:
                    pe.wait_ge(S["s_upr"], i - 3)
                for t in range(2):
                    for k in range(2):
                        mm = pe.matmul(ps[:, 4 + i % 4, t * D + k * P:t * D + (k + 1) * P],
                                       YT[:, k, (2 * i + t) * P:(2 * i + t + 1) * P], bu[:, k, :], start=True, stop=True)
                mm.then_inc(S["s_up"], 1)
            pe.wait_ge(S["s_wc"], 2)
            pe.wait_ge(col[2], 8)
            for t in range(NT):
                if t >= 2:
                    pe.wait_ge(S["s_k1s"], t - 1)
                for h in range(2):
                    for k in range(2):
                        mm = pe.matmul(ps[:, 2 * (t % 2) + h, :], YT[:, k, t * P:(t + 1) * P],
                                       wkv1[:, k, h * 512:(h + 1) * 512], start=(k == 0), stop=(k == 1))
                mm.then_inc(S["s_kv1"], 1)
            pe.wait_ge(S["s_upr"], 8)
            for g in range(4):
                for t in range(NT):
                    pe.wait_ge(S["s_v1n"], t + 1)
                    r = P if t < NT - 1 else LAST
                    KVf = KV1[0:r, t, :, :].rearrange("p g c -> p (g c)")
                    mm = pe.matmul(ps[:, 4, g * P:(g + 1) * P], KVf[:, 512 + g * P:512 + (g + 1) * P],
                                   KVf[:, g * P:(g + 1) * P], start=(t == 0), stop=(t == NT - 1))
            mm.then_inc(S["s_kvt1"], 1)
            pe.wait_ge(S["s_kvm1"], 1)
            for g in range(4):
                mm = pe.matmul(ps[:, 5 + g // 2, (g % 2) * D:(g % 2 + 1) * D], KVM1[:, g, :], woT[:, g, :],
                               start=True, stop=True)
            mm.then_inc(S["s_A1"], 1)
            pe.wait_ge(S["s_Am1"], 2)
            for c in range(2):
                for g in range(4):
                    mm = pe.matmul(ps[:, 7, c * D:(c + 1) * D], wq1[:, g, c * P:(c + 1) * P], AM1[:, g, :],
                                   start=(g == 0), stop=(g == 3))
            mm.then_inc(S["s_G1"], 1)
            pe.wait_ge(S["s_Gm1"], 1)
            for i in range(8):
                c, o = divmod(i, 2)
                if i >= 4:
                    pe.wait_ge(S["s_xt3"], i - 3)
                for k in range(2):
                    mm = pe.matmul(ps[:, i % 4, :], GM1[:, k, o * P:(o + 1) * P], YT[:, k, 512 * c:512 * c + 512],
                                   start=(k == 0), stop=(k == 1))
                mm.then_inc(S["s_y1"], 1)

            pe.wait_ge(S["s_xt3"], 8)
            pe.wait_ge(S["s_utab"], 32)
            pe.wait_ge(S["s_acc1"], 1)
            pe.sem_inc(S["s_mlp"], 6)
            pe.sem_inc(S["s_T"], BODY)
            pe.sem_inc(S["s_seg1"], BODY)

            def layer(w, src_, rows_, after):
                pe.wait_ge(*after)
                for b in range(2):
                    mm = pe.matmul(ps[:, b, 0:GE // 2], w[0:rows_, :], src_[0:rows_, b * (GE // 2):(b + 1) * (GE // 2)],
                                   start=True, stop=True)
                mm.then_inc(S["s_mlp"], 1)

            mp = MP

            def weights(j, i, k):
                h = k // GR % 2
                if k % GR == 0:
                    pe.wait_ge(S["s_split"], j * SPL + 2 * i + k // GR + 2)
                pe.wait_ge(S["s_prod"], j * ET + i * BODY + k + BODY - 3)
                for m in range(2):
                    mm = pe.matmul(weights_of(k), RS[:, h, (k % GR) * P:(k % GR + 1) * P], m4s[:, m, :],
                                   start=(m == 0), stop=(m == 1))
                mm.then_inc(S["s_T"], 1)

            def segment(j, i, u, k):
                T = j * ET + i * BODY + k
                pe.wait_ge(S["s_prod"], T + BODY + 1)
                pe.wait_ge(S["s_rmw1"], j * (ET + AHEAD) + i * BODY + k + 2)
                o = sums(u * BODY + k)
                S5k = S5[:, k // GR, k % GR, :, :]
                for pair, (a, y0, y1) in enumerate(((0, 1, 5), (4, 1, 2), (5, 0, 2))):
                    mm = pe.matmul(o[:, a:a + y1 - y0, :], PP[:, k, 2 * pair:2 * pair + 2, :], S5k[:, y0:y1, :],
                                   start=True, stop=True)
                mm.then_inc(S["s_seg1"], 1)

            with pe.Fori(0, npass) as j:
                def first(par, n_loaded, c):
                    pe.wait_ge(rbl[par], n_loaded)
                    layer(m1, RBF[:, par, :], 32, (S["s_silu"], c))

                pe.wait_ge(rbl[0], (j * ((ITERS + 2) // 2) + 1) * 16)
                for b in range(2):
                    mm = pe.matmul(ps[:, b, 0:GE // 2], m1[0:32, :], RBF[0:32, 0, b * (GE // 2):(b + 1) * (GE // 2)],
                                   start=True, stop=True)
                mm.then_inc(S["s_mlp"], 1)
                layer(m2, R1, P, (S["s_silu"], j * mp + 1))
                layer(m3, R2, P, (S["s_silu"], j * mp + 2))
                for k in range(AHEAD):
                    weights(j, 0, k)
                with pe.Fori(0, ITERS // 2) as i2:
                    for u in range(2):
                        i = 2 * i2 + u
                        for k in range(BODY):
                            if k == 0:
                                first(1 - u, (j * ((ITERS + 2) // 2) + i2 + 1 + u) * 16, j * mp + 3 * i + 3)
                            if k == 2:
                                layer(m2, R1, P, (S["s_silu"], j * mp + 3 * i + 4))
                            if k == 4:
                                layer(m3, R2, P, (S["s_silu"], j * mp + 3 * i + 5))
                            weights(j, 2 * i2, u * BODY + k + AHEAD)
                            segment(j, i, u, k)
                pe.wait_ge(S["s_silu"], (j + 1) * mp)
                pe.wait_ge(rbl[1], (j + 1) * ((ITERS + 2) // 2) * 16)
            pe.wait_ge(S["s_base1"], 1)
            pe.wait_ge(S["s_w4"], 16 * NLOAD["s_w4"])
            for i in range(NT // 2):
                if i >= 4:
                    pe.wait_ge(S["s_are"], i - 3)
                for t in range(2):
                    for h in range(NA):
                        mm = pe.matmul(ps[:, 4 + i % 4, t * D:(t + 1) * D], acc1[:, h, (2 * i + t) * P:(2 * i + t + 1) * P],
                                       wl[:, h, :], start=(h == 0), stop=(h == NA - 1))
                mm.then_inc(S["s_ar"], 1)
            pe.wait_ge(S["s_b"], 1)
            for i in range(NT // 2):
                c, k = divmod(i, 2)
                if i >= 4:
                    pe.wait_ge(S["s_bte"], i - 3)
                for t in range(4):
                    tr = pe.transpose(ps[:, i % 4, t * P:(t + 1) * P],
                                      BR[:, 4 * c + t, 2 * k:2 * k + 2, :].rearrange("p b c -> p (b c)"), ident)
                tr.then_inc(S["s_bt"], 1)
            pe.wait_ge(S["s_are"], 8)
            for i in range(8):
                c, k = divmod(i, 2)
                pe.wait_ge(S["s_bte"], i + 1)
                if i >= 4:
                    pe.wait_ge(S["s_oe"], i - 3)
                pe.matmul(ps[:, 4 + i % 4, :], bdb[:, k, :], BT[:, k, 512 * c:512 * c + 512], start=True, stop=False)
                pe.matmul(ps[:, 4 + i % 4, :], bds[:, k, :], YT[:, k, 512 * c:512 * c + 512], start=False,
                          stop=True).then_inc(S["s_o"], 1)
            pe.wait_ge(S["s_nr"], 1)
            for o in range(2):
                for k in range(2):
                    mm = pe.matmul(ps[:, 0, o:o + 1], pat[:, k, o, :], ss[:, k:k + 1], start=(k == 0), stop=(k == 1))
            mm.then_inc(S["s_nre"], 1)
            to_rows(3)
            to_cols(3)
            pe.wait_ge(row[3], 8)
            pe.wait_ge(S["s_fw1"], 16)
            for c in range(4):
                pe.wait_ge(col[3], 2 * c + 2)
                for k in range(2):
                    mm = pe.matmul(ps[:, 4 + c, :], wrb[:, k, :], YT[:, k, 512 * c:512 * c + 512],
                                   start=(k == 0), stop=(k == 1))
                mm.then_inc(S["s_wb"], 1)
            for i in range(4):
                pe.wait_ge(S["s_wbe"], 4)
                for t in range(4):
                    tr = pe.transpose(ps[:, 4 + i, t * P:(t + 1) * P], WB[:, (4 * i + t) * P:(4 * i + t + 1) * P], ident)
                tr.then_inc(S["s_wct"], 1)
            for i in range(32):
                c, m = divmod(i, 8)
                if i >= 4:
                    pe.wait_ge(S["s_he"], i - 3)
                for k in range(2):
                    mm = pe.matmul(ps[:, i % 4, :], fw1[:, k, m * P:(m + 1) * P], YT[:, k, 512 * c:512 * c + 512],
                                   start=(k == 0), stop=(k == 1))
                mm.then_inc(S["s_hh"], 1)
            pe.wait_ge(S["s_wcol"], 4)
            for t in range(NT):
                pe.wait_ge(S["s_he"], 8 * (t // 4) + 8)
                if t >= 4:
                    pe.wait_ge(S["s_out"], t - 3)
                for m in range(8):
                    mm = pe.matmul(ps[:, 4 + t % 4, 0:D], HT[:, m, t * P:(t + 1) * P], fw2[:, m, :],
                                   start=(m == 0), stop=(m == 7))
                mm.then_inc(S["s_yy"], 1)

        @block.vector
        def _(dve):
            n = [0]

            def link(ins):
                n[0] += 1
                ins.then_inc(S["s_dve"], 1)
                dve.wait_ge(S["s_dve"], n[0])

            def layer_norm(v):
                for t in range(NT):
                    if v:
                        dve.wait_ge(row[v], t // 2 + 1)
                    ins = dve.bn_stats(st[:, t, :], ROW[:, t, :])
                link(ins)
                for t in range(NT):
                    ins = dve.bn_aggr(mv[:, t, :], st[:, t, :])
                link(ins)
                dve.tensor_scalar(var, mv[:, :, 1], EPS, None, ALU.add).then_inc(lnvar[v], 1)
                dve.wait_ge(lnstd[v], 1)
                link(dve.reciprocal(rs, std))
                for t in range(NT):
                    dve.tensor_scalar(YROW[:, t, :], ROW[:, t, :], mv[:, t, 0:1], rs[:, t:t + 1],
                                      ALU.subtract, ALU.mult).then_inc(lny[v], 1)

            dve.memset(ROW[:, NT - 1, :], 0.0).then_inc(S["s_zero"], 1)
            dve.memset(XT[:, :, N:NPAD], 0.0).then_inc(S["s_zero"], 1)
            dve.memset(vacc[:, :], 0.0)
            dve.memset(ewt[:, ET:], 0.0)
            dve.memset(dloc[:, ET:], -1.0)
            dve.memset(baseI[:, 0:GR], 0)
            dve.wait_ge(S["s_idx"], 32)
            dve.tensor_copy(dstF[:, :], dstI)
            link(dve.tensor_copy(dr, drI))
            dve.memset(MR[:, :, H:H + 1], 1.0)
            drv = dr.rearrange("p (q e) -> p q e", q=4)
            dve.tensor_reduce(lohi[0:125, 0:4], drv, AX.X, ALU.min)
            link(dve.tensor_reduce(lohi[0:125, 4:8], drv, AX.X, ALU.max))
            link(dve.tensor_tensor(cnt3[0:125, 0, 0:4], lohi[0:125, 4:8], lohi[0:125, 0:4], ALU.subtract))
            dve.tensor_reduce(span[0:125, 0:1], cnt3[0:125, 0, 0:4], AX.X, ALU.max).then_inc(S["s_span"], 1)
            dve.wait_ge(S["s_span"], 2)
            link(dve.tensor_reduce(span[0:1, 1:2], ps[0:1, 7, 0:125], AX.X, ALU.max))
            link(dve.tensor_copy(npassI[0:1, 1:2], span[0:1, 1:2]))
            link(dve.tensor_scalar(npassI[0:1, 1:2], npassI[0:1, 1:2], 3, None, ALU.arith_shift_right))
            dve.tensor_scalar(npassI[0:1, 0:1], npassI[0:1, 1:2], 1, None, ALU.add).then_inc(S["s_npass"], 1)
            dve.wait_ge(S["s_const"], 16 * NLOAD["s_const"])
            dve.tensor_scalar(bnt, bnv[:, 3, :], EPS, None, ALU.add).then_inc(S["s_bnvar"], 1)
            dve.wait_ge(S["s_bnstd"], 1)
            link(dve.reciprocal(bns, bns))
            link(dve.tensor_tensor(bns, bns, bnv[:, 0, :], ALU.mult))
            link(dve.tensor_tensor(bnb, bnv[:, 4, :], bnv[:, 2, :], ALU.subtract))
            link(dve.tensor_tensor(bnb, bnb, bns, ALU.mult))
            dve.tensor_tensor(bnb, bnb, bnv[:, 1, :], ALU.add).then_inc(S["s_bn"], 1)
            dve.wait_ge(S["s_x"], 32)
            layer_norm(0)
            for i in range(2):
                dve.wait_ge(S["s_mtr"], i + 1)
                dve.tensor_copy(MROW[:, 8 * i:8 * i + 8, :].rearrange("p t h -> p (t h)"),
                                ps[:, 4 + i, :]).then_inc(S["s_mrow"], 1)

            def centre(w, g, c):
                wv = w.rearrange("p (g c) -> p g c", c=c)
                m = wmean[0:w.shape[0], 0:g]
                link(dve.tensor_reduce(m, wv, AX.X, ALU.add))
                link(dve.tensor_scalar(m, m, 1.0 / c, None, ALU.mult))
                link(dve.tensor_tensor(wv, wv, m.unsqueeze(2).broadcast_to([w.shape[0], g, c]), ALU.subtract))

            dve.wait_ge(S["s_w0"], 16 * NLOAD["s_w0"])
            for k in range(2):
                centre(wkv[:, k, :], 16, 32)
            centre(bkvr, 16, 32)
            dve.sem_inc(S["s_wc"], 1)
            for t in range(NT):
                dve.wait_ge(S["s_kvr"], t + 1)
                dve.tensor_reduce(VS[:, t * 16:(t + 1) * 16], SQ[:, t % 2, :].rearrange("p (g c) -> p g c", c=32),
                                  AX.X, ALU.add).then_inc(S["s_vs"], 1)
            dve.wait_ge(S["s_vs"], NT)
            dve.tensor_scalar(VS, VS, 1.0 / 32, EPS, ALU.mult, ALU.add).then_inc(S["s_vs"], 1)
            dve.wait_ge(S["s_vstd"], 1)
            link(dve.reciprocal(VS, VS))
            for t in range(NT):
                dve.wait_ge(S["s_kvc"], t + 1)
                ins = dve.tensor_tensor(KC[:, t, :, :], KC[:, t, :, :],
                                        VS[:, t * 16:(t + 1) * 16].unsqueeze(2).broadcast_to([P, 16, 32]), ALU.mult)
            link(ins)
            for t in range(NT):
                ins = dve.tensor_tensor(KC[:, t, :, :], KC[:, t, :, :], gkv.rearrange("p (g c) -> p g c", c=32), ALU.mult)
            link(ins)
            for t in range(NT):
                dve.tensor_tensor(KC[:, t, :, :], KC[:, t, :, :], bkv.rearrange("p (g c) -> p g c", c=32),
                                  ALU.add).then_inc(S["s_kvn"], 1)
            dve.wait_ge(S["s_kvt"], 1)
            dve.tensor_tensor(KVM, ps[:, 6, 0:256].rearrange("p (g c) -> p g c", g=2),
                              mask32.unsqueeze(1).broadcast_to([P, 2, P]), ALU.mult).then_inc(S["s_kvm"], 1)
            dve.wait_ge(S["s_A"], 1)
            dve.tensor_copy(AM.rearrange("p g c -> p (g c)"), ps[:, 4, :]).then_inc(S["s_Am"], 1)
            dve.wait_ge(S["s_G"], 1)
            dve.tensor_tensor(GM.rearrange("p g c -> p (g c)"), ps[:, 5, :], w1p.rearrange("p g c -> p (g c)"),
                              ALU.add).then_inc(S["s_Gm"], 1)
            dve.wait_ge(S["s_bv"], 1)
            dve.tensor_tensor(bvec, ps[:, 7, 0:2], b1c, ALU.add).then_inc(S["s_bvm"], 1)
            for i in range(8):
                c, o = divmod(i, 2)
                dve.wait_ge(S["s_mo"], i + 1)
                xc = XT[:, o, 512 * c:512 * c + 512]
                dve.scalar_tensor_tensor(xc, ps[:, 4 + i % 4, :], b2c[:, o:o + 1], xc, ALU.add,
                                         ALU.add).then_inc(S["s_xt0"], 1)
            dve.wait_ge(S["s_xt0"], 8)
            for i in range(8):
                c, o = divmod(i, 2)
                xc = XT[:, o, 512 * c:512 * c + 512]
                dve.tensor_tensor(xc, xc, YT[:, o, 512 * c:512 * c + 512], ALU.add).then_inc(S["s_xt0"], 1)
            dve.wait_ge(S["s_xt0"], 16)
            dve.memset(arena[:, 0:20000], 0.0)
            dve.wait_ge(S["s_lo"], 16)
            link(dve.tensor_copy(base[:, :], LO[:, :]))
            dve.wait_ge(S["s_acc0p"], 1)
            npass = vload(dve)

            regs = [dve.alloc_register(name=f"start{k}") for k in range(GR)]

            def window_starts(t):
                dve.load(regs, baseI[0:1, bass.ds(GR + t, GR)])
                return [dve.snap(x, min_val=0, max_val=N) for x in regs]

            def windows(done):
                dve.tensor_tensor(dloc[:, 0:ET], dstF[:, :], base[:, :], ALU.subtract)
                dve.tensor_copy(baseI[:, GR:], base[0:1, :]).then_inc(S["s_oh"], 1)
                dve.wait_ge(S["s_oh"], done)

            def next_windows(done):
                dve.tensor_scalar(base[:, :], base[:, :], float(WIN), float(N), ALU.add,
                                  ALU.min).then_inc(S["s_oh"], 1)
                dve.wait_ge(S["s_oh"], done)

            def onehot(out_, t0, count, sem_):
                dve.tensor_tensor(out_, iota8.unsqueeze(1).broadcast_to([P, GR, WIN]),
                                  dloc[:, bass.ds(t0, GR)].unsqueeze(2).broadcast_to([P, GR, WIN]),
                                  ALU.is_equal).then_inc(sem_, 1)
                dve.wait_ge(sem_, count)

            for w_, w2_, w3_ in ((kw1, k2, k3), (kb1r[0:1, :], kb2[0:1, :], kb3[0:1, :])):
                link(dve.tensor_tensor(w2_, w_, top(w_), ALU.subtract))
                link(dve.tensor_tensor(w3_, w2_, top(w2_), ALU.subtract))
            dve.sem_inc(S["s_rmw"], 1)
            dve.sem_inc(S["s_ea"], 1)
            with dve.Fori(0, npass) as j:
                per = 2 + 2 * NG
                dve.memset(ps[:, 4:6, 0:3 * (P + WIN)], 0.0)
                windows(j * per + 1)

                def masks(i, g, step):
                    n = 2 * i + g
                    c = j * per + 1 + 2 * n
                    t0 = i * BODY + g * GR
                    ready = j * NG + n + 1
                    g = g % 2
                    if step == 0:
                        dve.wait_ge(S["s_seg"], j * 2 * ITERS + n + 1)
                        dve.tensor_tensor(SW[:, g, :, :], iota8.unsqueeze(1).broadcast_to([P, GR, WIN]),
                                          dloc[:, bass.ds(t0, GR)].unsqueeze(2).broadcast_to([P, GR, WIN]),
                                          ALU.is_equal).then_inc(S["s_oh"], 1)
                    elif step == 1:
                        dve.wait_ge(S["s_oh"], c + 1)
                        dve.tensor_tensor(SW[:, g, :, :], SW[:, g, :, :],
                                          ewt[:, bass.ds(t0, GR)].unsqueeze(2).broadcast_to([P, GR, WIN]),
                                          ALU.mult).then_inc(S["s_oh"], 1)
                    else:
                        h = step - 2
                        if h == 0:
                            dve.wait_ge(S["s_oh"], c + 2)
                            dve.wait_ge(S["s_rready"], ready)
                        ins = dve.tensor_tensor(
                            RM[:, g, :, h * P:(h + 1) * P].rearrange("p t (w q) -> p t w q", q=16),
                            MR[:, g * GR:(g + 1) * GR, H + 1 + 16 * h:H + 17 + 16 * h].unsqueeze(2).broadcast_to([P, GR, WIN, 16]),
                            SW[:, g, :, :].unsqueeze(3).broadcast_to([P, GR, WIN, 16]), ALU.mult)
                        if h == 1:
                            ins.then_inc(S["s_mask"], 1)

                def rest(loaded, n, par, step):
                    if step == 0:
                        dve.wait_ge(eal[par], loaded)
                        dve.wait_ge(S["s_er"], j * NG + n + 1)
                        dve.tensor_tensor(EA2[:, par, :], EA[:, par, :], top(EA[:, par, :]),
                                          ALU.subtract).then_inc(S["s_rest"], 1)
                    else:
                        dve.wait_ge(S["s_rest"], j * (NG + 1) + n + 1)
                        dve.tensor_tensor(EA3[:, par, :], EA2[:, par, :], top(EA2[:, par, :]),
                                          ALU.subtract).then_inc(S["s_ea"], 1)

                def add(i, g, t, first):
                    if t == 0:
                        dve.wait_ge(S["s_seg"], j * 2 * ITERS + 2 * i + g + 2)
                    a = acc[:, bass.ds(first[t], WIN), :]
                    v = vacc[:, bass.ds(first[t], WIN)]
                    slot = (1 - g) * GR + t
                    dve.wait_ge(S["s_rmw"], j * (ET + GR) + i * BODY + g * GR + t + 1)
                    dve.tensor_tensor(a, a, outer(slot).rearrange("p (n q) -> p n q", q=16), ALU.add)
                    dve.tensor_tensor(v, v, affine(slot), ALU.add).then_inc(S["s_rmw"], 1)

                for step in range(2):
                    for g in range(2):
                        rest((j * (ITERS + 1) + 1) * 16, g, g, step)
                for step in range(4):
                    masks(0, 0, step)
                with dve.Fori(0, ITERS) as i:
                    for slot in range(BODY):
                        g, pos = divmod(slot, GR)
                        if pos < 4:
                            masks(i, g + 1, pos)
                        if pos == 0:
                            first = window_starts(i * BODY + slot - GR)
                        add(i, g, pos, first)
                        if pos in (2, 3):
                            rest((j * (ITERS + 1) + i + 2) * 16, 2 * i + g + 2, g, pos - 2)
                first = window_starts(ET - GR)
                for t in range(GR):
                    add(ITERS, 0, t, first)
                next_windows(j * per + per)
            dve.drain().then_inc(S["s_base"], 1)
            for i in range(8):
                c, o = divmod(i, 2)
                dve.wait_ge(S["s_mo"], 8 + i + 1)
                xc = XT[:, o, NCH * c:NCH * (c + 1)]
                dve.scalar_tensor_tensor(xc, ps[:, 4 + i % 4, 0:NCH], bns[:, 4 + o:5 + o], xc, ALU.mult,
                                         ALU.add).then_inc(S["s_o0"], 1)
            dve.wait_ge(S["s_o0"], 8)
            for o in range(2):
                ins = dve.tensor_scalar(XT[:, o, 0:N], XT[:, o, 0:N], bnb[:, 4 + o:5 + o], None, ALU.add)
            ins.then_inc(xtd[1], 1)
            layer_norm(1)
            for i in range(8):
                c, o = divmod(i, 2)
                dve.wait_ge(S["s_mo"], 16 + i + 1)
                xc = XT[:, o, 512 * c:512 * c + 512]
                ins = dve.scalar_tensor_tensor(xc, ps[:, 4 + i % 4, :], bfc[:, o:o + 1], xc, ALU.add, ALU.add)
                ins.then_inc(S["s_ff"], 1)
            dve.wait_ge(S["s_ff"], 8)
            dve.sem_inc(xtd[2], 1)
            layer_norm(2)
            dve.wait_ge(S["s_w1"], 16 * NLOAD["s_w1"])
            for k in range(2):
                centre(wkv1[:, k, :], 16, 64)
            dve.sem_inc(S["s_wc"], 1)
            link(dve.tensor_scalar(m4[:, 192:256], m4[:, 192:256], 3.0 ** -0.5, None, ALU.mult))
            for t in range(NT):
                dve.wait_ge(S["s_k1s"], t + 1)
                dve.tensor_reduce(VS1[:, t * 16:(t + 1) * 16], SQ1.rearrange("p (g c) -> p g c", c=64),
                                  AX.X, ALU.add).then_inc(S["s_v1r"], 1)
            dve.wait_ge(S["s_v1r"], NT)
            dve.tensor_scalar(VS1, VS1, 1.0 / 64, EPS, ALU.mult, ALU.add).then_inc(S["s_v1r"], 1)
            dve.wait_ge(S["s_v1std"], 1)
            link(dve.reciprocal(VS1, VS1))
            vsv = VS1.rearrange("p (t u h) -> p t u h", t=NT, u=2)
            link(dve.tensor_tensor(RK1.rearrange("p (t h) -> p t h", h=8), vsv[:, :, 0, :], vsv[:, :, 1, :], ALU.mult))
            for t in range(NT):
                dve.tensor_tensor(KV1[:, t, 8:16, :], KV1[:, t, 8:16, :],
                                  RK1[:, t * 8:(t + 1) * 8].unsqueeze(2).broadcast_to([P, 8, 64]),
                                  ALU.mult).then_inc(S["s_v1n"], 1)
            dve.wait_ge(S["s_kvt1"], 1)
            dve.tensor_tensor(KVM1, ps[:, 4, :].rearrange("p (g c) -> p g c", g=4),
                              mask64.unsqueeze(1).broadcast_to([P, 4, P]), ALU.mult).then_inc(S["s_kvm1"], 1)
            dve.wait_ge(S["s_A1"], 1)
            for h in range(2):
                dve.tensor_copy(AM1[:, 2 * h:2 * h + 2, :].rearrange("p g c -> p (g c)"),
                                ps[:, 5 + h, :]).then_inc(S["s_Am1"], 1)
            dve.wait_ge(S["s_G1"], 1)
            dve.tensor_copy(GM1.rearrange("p g c -> p (g c)"), ps[:, 7, :]).then_inc(S["s_Gm1"], 1)
            for i in range(8):
                c, o = divmod(i, 2)
                dve.wait_ge(S["s_y1"], i + 1)
                xc = XT[:, o, 512 * c:512 * c + 512]
                dve.scalar_tensor_tensor(xc, ps[:, i % 4, :], boc[:, o:o + 1], xc, ALU.add,
                                         ALU.add).then_inc(S["s_xt3"], 1)
            dve.wait_ge(S["s_kvt1"], 1)
            dve.memset(acc1, 0.0).then_inc(S["s_acc1"], 1)
            dve.wait_ge(S["s_acc1"], 1)
            link(dve.tensor_copy(base[:, :], LO[:, :]))
            dve.wait_ge(S["s_utab"], 32)
            dve.sem_inc(S["s_prod"], BODY)
            dve.sem_inc(S["s_rmw1"], 1)
            dve.sem_inc(S["s_split"], 1)

            def upper(dst, a):
                return dve.tensor_scalar(dst.bitcast(I32), a.bitcast(I32), HIGH, None, ALU.bitwise_and)

            link(upper(UP12[:, 0:D], m4))
            link(dve.tensor_tensor(m4s[:, 1, :], m4, UP12[:, 0:D], ALU.subtract))
            link(dve.tensor_copy(m4s[:, 0, :], UP12[:, 0:D]))

            with dve.Fori(0, npass) as j:
                per = 2 + 5 * NG
                b0 = npass * (2 + 2 * NG)
                dve.memset(ps[:, 6:8, 0:NA * WIN], 0.0)
                windows(b0 + j * per + 1)
                dve.sem_inc(S["s_pass1"], 1)

                def split_half(c, h):
                    if h == 0:
                        dve.wait_ge(S["s_silu"], j * MP + 3 * c + 3)
                        upper(UP12, R3).then_inc(S["s_half"], 1)
                    dve.wait_ge(S["s_half"], j * (ITERS + 1) + c + 1)
                    dve.wait_ge(S["s_T"], j * ET2 + c * BODY + GR * (h + 1))
                    hi, lo = slice(h * H, (h + 1) * H), slice((1 - h) * H, (2 - h) * H)
                    dve.tensor_copy(RS[hi, h, :], UP12[hi, :])
                    dve.tensor_tensor(RS[lo, h, :], R3[hi, :], UP12[hi, :],
                                      ALU.subtract).then_inc(S["s_split"], 1)

                def prepare(i, g, step):
                    c = b0 + j * per + 1 + 5 * (2 * i + g)
                    t0 = i * BODY + g * GR
                    i, g = i + g // 2, g % 2
                    if step == 0:
                        dve.wait_ge(S["s_seg1"], j * ET + t0 + GR)
                        dve.tensor_tensor(S5[:, g, :, 0, :], iota8.unsqueeze(1).broadcast_to([P, GR, WIN]),
                                          dloc[:, bass.ds(t0, GR)].unsqueeze(2).broadcast_to([P, GR, WIN]),
                                          ALU.is_equal).then_inc(S["s_oh"], 1)
                    elif step == 1:
                        dve.wait_ge(S["s_oh"], c + 1)
                        dve.tensor_tensor(
                            S5[:, g, :, 1:5, :], S5[:, g, :, 0:1, :].broadcast_to([P, GR, 4, WIN]),
                            shv[:, bass.ds(t0, GR), :].unsqueeze(3).broadcast_to([P, GR, 4, WIN]),
                            ALU.mult).then_inc(S["s_oh"], 1)
                    elif step == 2:
                        for slot in range(g * GR, (g + 1) * GR):
                            dve.wait_ge(gath[slot], (npass * ITERS + j * (ITERS + 1 - g) + i + 1) * 16)
                        dve.tensor_tensor(
                            XS, G1[:, g * GR:(g + 1) * GR, H:].rearrange("p t (x c) -> p t x c", x=3),
                            shv[:, bass.ds(t0, GR), 1:4].unsqueeze(3).broadcast_to([P, GR, 3, H]),
                            ALU.mult).then_inc(S["s_oh"], 1)
                    else:
                        dve.wait_ge(S["s_oh"], c + step)
                        dve.tensor_tensor(XU[:, g, :, :], XS[:, :, 0, :] if step == 3 else XU[:, g, :, :],
                                          XS[:, :, step - 2, :], ALU.add).then_inc(S["s_oh"], 1)

                def products(i, u, slot):
                    T = j * ET + i * BODY + slot
                    if slot % GR == 0:
                        dve.wait_ge(S["s_oh"], b0 + j * per + 1 + 5 * (2 * i + slot // GR + 1))
                    dve.wait_ge(S["s_T"], j * ET2 + i * BODY + slot + BODY + 1)
                    dve.wait_ge(S["s_seg1"], T + 1)
                    tp = weights_of(u * BODY + slot).rearrange("p (b c) -> p b c", b=4)
                    x = G1[:, slot, :].rearrange("p (b c) -> p b c", b=4)
                    dve.tensor_tensor(PP[:, slot, 0:2, :], tp[:, 0:2, :], x[:, 0:1, :].broadcast_to([P, 2, H]), ALU.mult)
                    dve.tensor_tensor(PP[:, slot, 2:5, :], tp[:, 2:3, :].broadcast_to([P, 3, H]), x[:, 1:4, :], ALU.mult)
                    dve.tensor_tensor(PP[:, slot, 5, :], tp[:, 3, :], XU[:, slot // GR, slot % GR, :],
                                      ALU.mult).then_inc(S["s_prod"], 1)

                def add1(i, T):
                    n = i * BODY + T
                    b = dve.value_load(baseI[0:1, bass.ds(GR - AHEAD + n, 1)], min_val=0, max_val=N)
                    dve.wait_ge(S["s_seg1"], j * ET + n - AHEAD + BODY + 1)
                    dve.wait_ge(S["s_rmw1"], j * (ET + AHEAD) + n + 1)
                    a = acc1[:, :, bass.ds(b, WIN)]
                    dve.tensor_tensor(a, a, sums(T), ALU.add).then_inc(S["s_rmw1"], 1)

                split_half(0, 0)
                for step in range(5):
                    prepare(0, 0, step)
                with dve.Fori(0, ITERS // 2) as i2:
                    for T in range(2 * BODY):
                        u, slot = divmod(T, BODY)
                        i = 2 * i2 + u
                        g, pos = divmod(slot, GR)
                        if pos == 4:
                            prepare(i, g + 1, 3)
                        products(i, u, slot)
                        if pos == 4:
                            prepare(i, g + 1, 4)
                        add1(2 * i2, T)
                        if slot == 0:
                            split_half(i, 1)
                        if slot == 6:
                            split_half(i + 1, 0)
                        if pos == 2:
                            prepare(i, g + 1, 0)
                        if pos == 3:
                            prepare(i, g + 1, 1)
                            prepare(i, g + 1, 2)
                for T in range(AHEAD):
                    add1(ITERS, T)
                next_windows(b0 + j * per + per)
            dve.drain().then_inc(S["s_base1"], 1)
            dve.wait_ge(S["s_are"], 8)
            dve.wait_ge(S["s_w4"], 16 * NLOAD["s_w4"])
            A0 = AR[:, :, 0, :]
            t0, t1, t2, t3 = TMP

            def W(v):
                return wc[:, v, :].unsqueeze(1).broadcast_to([P, NT, 64])

            def tt(o, a, b, op):
                link(dve.tensor_tensor(o, a, b, op))
            tt(t0, AR[:, :, 1, :], AR[:, :, 1, :], ALU.mult)
            tt(t1, AR[:, :, 2, :], AR[:, :, 2, :], ALU.mult)
            tt(t0, t0, t1, ALU.add)
            tt(t1, AR[:, :, 3, :], AR[:, :, 3, :], ALU.mult)
            tt(t0, t0, t1, ALU.add)
            tt(t1, A0, A0, ALU.mult)
            tt(t2, A0, W(1), ALU.mult)
            tt(t2, t2, W(0), ALU.add)
            tt(t3, t1, W(3), ALU.mult)
            tt(t2, t2, t3, ALU.add)
            tt(t3, t0, W(4), ALU.mult)
            tt(t2, t2, t3, ALU.add)
            tt(t2, t2, A0, ALU.mult)
            tt(t3, t0, W(2), ALU.mult)
            tt(BR[:, :, 0, :], t2, t3, ALU.add)
            tt(t2, A0, W(6), ALU.mult)
            tt(t2, t2, W(5), ALU.add)
            tt(t3, t1, W(7), ALU.mult)
            tt(t2, t2, t3, ALU.add)
            tt(t3, t0, W(8), ALU.mult)
            tt(t2, t2, t3, ALU.add)
            for x in range(3):
                ins = dve.tensor_tensor(BR[:, :, 1 + x, :], AR[:, :, 1 + x, :], t2, ALU.mult)
            ins.then_inc(S["s_b"], 1)
            dve.wait_ge(S["s_oe"], 8)
            for k in range(2):
                for c in range(4):
                    ins = dve.bn_stats(sto[:, k, c, :], OT[:, k, c * NCH:(c + 1) * NCH])
            link(ins)
            for k in range(2):
                ins = dve.bn_aggr(mvo[:, k, :], sto[:, k, :, :].rearrange("p c s -> p (c s)"))
            link(ins)
            link(dve.tensor_tensor(ss, mvo[:, :, 0], mvo[:, :, 0], ALU.mult))
            dve.tensor_tensor(ss, ss, mvo[:, :, 1], ALU.add).then_inc(S["s_nr"], 1)
            dve.wait_ge(S["s_nre"], 1)
            link(dve.tensor_copy(nrm, ps[:, 0, 0:2]))
            link(dve.tensor_copy(nrm[0:H, 0:1], mvo[0:H, 0, 1:2]))
            dve.tensor_scalar(nrm, nrm, EPS, None, ALU.add).then_inc(S["s_nvar"], 1)
            dve.wait_ge(S["s_nstd"], 1)
            link(dve.reciprocal(osc, nrm))
            link(dve.tensor_tensor(osc, osc, l1v[:, 0, :], ALU.mult))
            link(dve.tensor_tensor(obi, mvo[:, :, 0], osc, ALU.mult))
            link(dve.tensor_tensor(obi, obi, l1v[:, 2, :], ALU.mult))
            link(dve.tensor_tensor(obi, l1v[:, 1, :], obi, ALU.subtract))
            for k in range(2):
                ins = dve.scalar_tensor_tensor(XT[:, k, :], OT[:, k, :], osc[:, k:k + 1], XT[:, k, :], ALU.mult, ALU.add)
            link(ins)
            for k in range(2):
                ins = dve.tensor_scalar(XT[:, k, :], XT[:, k, :], obi[:, k:k + 1], None, ALU.add)
            link(ins)
            link(dve.tensor_copy(wrb, wr.unsqueeze(2).broadcast_to([P, 2, P])))
            dve.sem_inc(xtd[3], 1)
            layer_norm(3)
            for i in range(4):
                dve.wait_ge(S["s_wct"], i + 1)
                dve.tensor_copy(wcol[:, 4 * i:4 * i + 4],
                                ps[:, 4 + i, :].rearrange("p (t c) -> p t c", c=P)[:, :, 0]).then_inc(S["s_wcol"], 1)
            dve.wait_ge(S["s_wcol"], 4)
            link(dve.memset(cnt3[:, 0, 0:1], 0.0))
            for t in range(NT):
                w = wcol[:, t:t + 1]
                if t:
                    link(dve.tensor_scalar(junk[:, 0:t * P], WB[:, 0:t * P], w, 0.0, ALU.is_ge, ALU.add,
                                           accum_out=cnt3[:, 0, t:t + 1]))
                link(dve.tensor_scalar(junk[:, t * P:N], WB[:, t * P:N], w, 0.0, ALU.is_gt, ALU.add,
                                       accum_out=cnt3[:, 1, t:t + 1]))
                link(dve.scalar_tensor_tensor(junk[:, 0:P], WB[:, t * P:(t + 1) * P], w, ltm, ALU.is_equal, ALU.mult,
                                              accum_out=cnt3[:, 2, t:t + 1]))
            link(dve.tensor_tensor(mw, cnt3[:, 0, :], cnt3[:, 1, :], ALU.add))
            link(dve.tensor_tensor(mw, mw, cnt3[:, 2, :], ALU.add))
            link(dve.tensor_scalar(mw, mw, float(SEL), None, ALU.is_lt))
            link(dve.tensor_tensor(mw, mw, wcol, ALU.mult))
            for t in range(NT):
                dve.wait_ge(S["s_yy"], t + 1)
                o = OUTR[:, t, :]
                link(dve.tensor_tensor(o, ps[:, 4 + t % 4, 0:D], fb2, ALU.add))
                link(dve.scalar_tensor_tensor(o, o, mw[:, t:t + 1], ROW[:, t, :], ALU.mult, ALU.add))
                dve.tensor_tensor(o, o, YROW[:, t, :], ALU.add).then_inc(S["s_out"], 1)


def kernel(**inputs):
    import numpy as np
    import concourse.bacc as _bacc
    from concourse.bass_utils import run_bass_kernel_spmd as _run

    I = {k: np.asarray(v) for k, v in inputs.items()}
    perm = np.concatenate([np.arange(64)] + [64 + 3 * np.arange(64) + x for x in range(3)])

    def kt(a):
        k = a.shape[0] // 128
        return np.ascontiguousarray(a.reshape(k, 128, -1).transpose(1, 0, 2).reshape(128, -1))

    def colv(v):
        return np.ascontiguousarray(v.reshape(-1, 128).T)

    def pad64(v):
        return np.concatenate([v, np.zeros(64, np.float32)])

    def blocks(parts):
        a = np.zeros((128, 2, 128), np.float32)
        for n, b in enumerate(parts):
            r = 64 * (n % 2)
            a[r:r + 64, n // 2, r:r + 64] = b
        return a.reshape(128, 256)

    A = {}
    x = I["x"][:, perm]
    A["x"] = np.ascontiguousarray(x)
    A["xT"] = np.ascontiguousarray(x.T)
    A["src_l"] = np.zeros((P, ET + GR), np.int32)
    A["src_l"][:, :ET] = I["src"].reshape(ET, P).T
    A["dst_l"] = np.ascontiguousarray(I["dst"].reshape(ET, P).T)
    A["dst_r"] = np.ascontiguousarray(I["dst"].reshape(125, 4 * P))
    A["ew"] = np.ascontiguousarray(I["edge_weight"].reshape(ET, P).T)
    A["sh"] = np.zeros((P, (ET + GR) * 4), np.float32)
    A["sh"][:, :ET * 4] = I["edge_attr_4"].reshape(ET, P, 4).transpose(1, 0, 2).reshape(P, ET * 4)
    ea = np.zeros((P, (2 * ITERS + 2) * GE), np.float32)
    ea[:, :E] = I["edge_attr_128"].T
    A["eaT"] = ea
    rb = np.zeros(((ITERS + 2) * 2 * GE, 16), np.float32)
    rb[:E] = I["edge_attr_16"]
    A["rbf"] = np.ascontiguousarray(rb.reshape(ITERS + 2, 2, GE, 16).transpose(0, 1, 3, 2).reshape(-1, GE))
    A["ident"] = np.eye(128, dtype=np.float32)
    A["iota8"] = np.tile(np.arange(WIN, dtype=np.float32), (128, 1))
    A["ones"] = np.ones((128, 128), np.float32)
    A["mask32"] = np.kron(np.eye(4), np.ones((32, 32))).astype(np.float32) / np.float32(N)
    A["mask64"] = np.kron(np.eye(2), np.ones((64, 64))).astype(np.float32) / np.float32(N)
    A["ltm"] = np.tril(np.ones((128, 128), np.float32), -1)
    pat = np.zeros((2, 128, 2, 128), np.float32)
    for k in range(2):
        for o in range(2):
            for a in range(2):
                for b in range(2):
                    if (k, a) != (0, 0) and (o, b) != (0, 0):
                        pat[k, 64 * a:64 * a + 64, o, 64 * b:64 * b + 64] = np.eye(64) / 3
    A["pat"] = np.ascontiguousarray(pat.transpose(1, 0, 2, 3).reshape(128, 512))
    g = lambda n: I["L0_gnn_" + n]
    vec = []
    for a in ("g", "be", "m", "v"):
        vec.append(np.concatenate([colv(g(a + "_in")[perm]), colv(pad64(g(a + "_msg"))), colv(pad64(g(a + "_upd"))),
                                   colv(g(a + "_out")[perm])], 1))
    z2 = np.zeros((128, 2), np.float32)
    vec.append(np.concatenate([z2, colv(pad64(g("b1"))), z2[:, :1], colv(g("b2")[perm])], 1))
    A["bnv"] = np.concatenate(vec, 1)
    A["w1g"] = kt(g("w1")[perm])
    A["kw1"] = g("kw1")
    A["kb1r"] = g("kb1")[None]
    A["w2g"] = np.ascontiguousarray(g("w2")[:, perm])
    kw2 = g("kw2").reshape(KH, H + 1, H)
    kb2 = g("kb2").reshape(H + 1, H)
    A["W2S"] = np.ascontiguousarray(kw2[:, 1:, :].reshape(2, 16, H, H).transpose(0, 3, 1, 2).reshape(128, 16 * H))
    A["wV"] = np.concatenate([np.zeros((31, H), np.float32), kb2[:1], kw2[:, 0, :], kb2[1:].T], 0)
    m = lambda n: I["L0_mix_" + n]
    wq = m("w_qkv")[perm].reshape(D, 8, 3, 32)
    bq = m("b_qkv").reshape(8, 3, 32)
    A["wqT"] = kt(np.ascontiguousarray(wq[:, :, 0].reshape(D, D).T))
    A["bq"] = colv(bq[:, 0].reshape(-1))
    A["wkv"] = kt(np.concatenate([wq[:, :, 1].reshape(D, D), wq[:, :, 2].reshape(D, D)], 1))
    A["bkvr"] = np.concatenate([bq[:, 1].reshape(-1), bq[:, 2].reshape(-1)])[None]
    A["gkv"] = np.tile(np.concatenate([np.tile(m("kln_g"), 8), np.tile(m("vln_g"), 8)]), (128, 1))
    A["bkv"] = np.tile(np.concatenate([np.tile(m("kln_b"), 8), np.tile(m("vln_b"), 8)]), (128, 1))
    A["w1m"] = kt(m("w1"))
    A["w1p"] = kt(m("w1")[perm])
    A["w2m"] = kt(np.ascontiguousarray(m("w2")[:, perm]))
    A["b1c"] = colv(m("b1"))
    A["b2c"] = colv(m("b2")[perm])
    A["wfT"] = kt(np.ascontiguousarray(I["L0_ffn_weight"].T[perm][:, perm]))
    A["bfc"] = colv(I["L0_ffn_bias"][perm])
    g1 = lambda n: I["L1_gnn_" + n]
    A["bu"] = blocks([g1("W_up0")] + [g1("W_up1")] * 3)
    A["bdb"] = blocks([g1("WB0")] + [g1("WB1")] * 3)
    A["bds"] = blocks([g1("Wsc0")] + [g1("Wsc1")] * 3)

    def two(w):
        a = np.zeros((2 * w.shape[0], 128), np.float32)
        a[:w.shape[0], :64] = w
        a[w.shape[0]:, 64:] = w
        return a
    A["m1"], A["m2"], A["m3"] = two(g1("M1")), two(g1("M2")), two(g1("M3"))
    A["m4"] = np.tile(g1("M4"), (2, 1))
    wl = np.zeros((2, 64, NA, 4, 64), np.float32)
    w0, w1 = g1("W_lin0"), g1("W_lin1")
    for half, h in ((0, 0), (1, 5)):
        wl[half, :, h, 0] = w0
    for half, h, c in ((1, 1, 1), (1, 2, 2), (1, 3, 3), (0, 4, 1), (1, 4, 2), (0, 6, 3)):
        wl[half, :, h, c] = w1
    A["wl"] = wl.reshape(128, NA * D)
    A["wc"] = np.tile(np.concatenate([g1("Wc0").T.reshape(-1), g1("Wc1").T.reshape(-1)]), (128, 1))
    gam = np.concatenate([g1("gamma0")] + [g1("gamma1")] * 3)
    bet = np.concatenate([g1("beta0"), np.zeros(192, np.float32)])
    is0 = np.concatenate([np.ones(64, np.float32), np.zeros(192, np.float32)])
    A["l1v"] = np.concatenate([colv(gam), colv(bet), colv(is0)], 1)
    Wqkv = I["L1_mix_Wqkv"][:, perm]
    A["wq1"] = kt(Wqkv[0:512])
    A["wkv1"] = kt(np.ascontiguousarray(Wqkv[512:].T))
    A["woT"] = kt(np.ascontiguousarray(I["L1_mix_Wout"][perm].T))
    A["boc"] = colv(I["L1_mix_bout"][perm])
    f = lambda n: I["L1_ffn_" + n]
    A["wr"] = colv(f("wr")[perm, 0])
    A["brc"] = np.tile(f("br"), (128, 1))
    A["fw1"] = kt(f("w1")[perm])
    A["fb1"] = colv(f("b1"))
    A["fw2"] = kt(np.ascontiguousarray(f("w2")[:, perm]))
    A["fb2"] = np.tile(f("b2")[perm], (128, 1))

    nc = _bacc.Bacc("TRN2", target_bir_lowering=False, num_devices=1)
    arrays, aps = {}, {}
    for name, a in A.items():
        a = np.ascontiguousarray(a)
        assert a.dtype in (np.float32, np.int32), (name, a.dtype)
        arrays["in_" + name] = a
        aps[name] = nc.dram_tensor("in_" + name, a.shape, mybir.dt.from_np(a.dtype), kind="ExternalInput").ap()
    out = nc.dram_tensor("out_0", (N, D), F32, kind="ExternalOutput").ap()
    build(nc, aps, out)
    r = _run(nc, [arrays], core_ids=[0])
    got = r.results[0]["out_0"]
    inv = np.argsort(perm)
    return np.ascontiguousarray(got[:, inv])
```

```python
from contextlib import ExitStack

import concourse.bass as bass
from concourse import mybir

F32 = mybir.dt.float32
I32 = mybir.dt.int32
F32R = mybir.dt.float32r
BF16 = mybir.dt.bfloat16
ALU = mybir.AluOpType
ACT = mybir.ActivationFunctionType
AX = mybir.AxisListType

P = 128
N, D, E = 2000, 256, 64000
NT = (N + P - 1) // P
NPAD = NT * P
LAST = N - (NT - 1) * P
ET = E // P
WIN = 8
NW = N + WIN
H = 64
KH = 32
GR = 5
BODY = 2 * GR
ITERS = ET // BODY
NG = 2 * ITERS + 1
MP = 6 * (ITERS + 1) + 2
SPL = 2 * ITERS + 1
PT = ET // 2
BP = BODY // 2
AHEAD = 2
HIGH = -4096
GE = GR * P
NCH = 500
EPS = 1e-5
SMALL = 1720
NA = 6
ARENA = 32256
RING = 7744
SEL = N // 2 - 1


class Area:

    def __init__(self, tensor, start, end):
        self.tensor, self.at, self.end = tensor, start, end

    def take(self, n):
        a = self.at
        self.at += n
        assert self.at <= self.end, (self.at, self.end)
        return self.tensor[:, a:a + n]


def build(nc, A, out):
    ctx = ExitStack()
    with ctx:
        def sb(name, cols, dt=F32, parts=P):
            return ctx.enter_context(nc.sbuf_tensor(name, [parts, cols], dt))

        def sem(name):
            return ctx.enter_context(nc.semaphore(name))

        arena = sb("arena", ARENA)
        ring = sb("ring", RING)
        XT = sb("XT", 2 * NPAD)[:, :].rearrange("p (k n) -> p k n", k=2)
        src = sb("src", ET + GR, I32)
        dstF = sb("dstF", ET)
        ewt = sb("ewt", ET + GR)
        LO = sb("LO", ET)
        base = sb("base", ET)
        dloc = sb("dloc", ET + GR)
        baseI = sb("baseI", GR + ET, I32, 1)
        vacc = sb("vacc", NW)
        curI = sb("curI", 2 * GR, I32)
        small = sb("small", SMALL)
        npassI = sb("npassI", 2, I32, 1)
        with ExitStack() as first:
            W2S = first.enter_context(nc.sbuf_tensor("W2S", [P, 16 * H], F32))[:, :].rearrange("p (q j) -> p q j", q=16)
            wfT = first.enter_context(nc.sbuf_tensor("wfT", [P, 512], F32))[:, :].rearrange("p (k c) -> p k c", k=2)
        RS = sb("RS", 2 * GE, F32R)[:, :].rearrange("p (h e) -> p h e", h=2)
        m4s = sb("m4s", 2 * D, F32R)[:, :].rearrange("p (h c) -> p h c", h=2)
        ps = ctx.enter_context(nc.psum_tensor("ps", [P, 8, 512], F32))

        sm = Area(small, 0, SMALL)
        ident = sm.take(P)
        iota8 = sm.take(WIN)
        st = sm.take(NT * 6).rearrange("p (t s) -> p t s", s=6)
        mv = sm.take(NT * 2).rearrange("p (t s) -> p t s", s=2)
        var = sm.take(NT)
        std = sm.take(NT)
        rs = sm.take(NT)
        bnv = sm.take(30).rearrange("p (v c) -> p v c", v=5)
        bns = sm.take(6)
        bnb = sm.take(6)
        bnt = sm.take(6)
        ones = sm.take(P)
        w1g = sm.take(2 * H).rearrange("p (k h) -> p k h", k=2)
        kw1 = sm.take(KH)
        kb1r = sm.take(KH)
        k2 = sm.take(KH)
        kb2 = sm.take(KH)
        k3 = sm.take(KH // 2).bitcast(BF16)
        kb3 = sm.take(KH // 2).bitcast(BF16)
        w2g = sm.take(D)
        wV = sm.take(H)
        bq = sm.take(2)
        b1c = sm.take(2)
        b2c = sm.take(2)
        bfc = sm.take(2)
        boc = sm.take(2)
        bvec = sm.take(2)
        l1v = sm.take(6).rearrange("p (v c) -> p v c", v=3)
        mvo = sm.take(4).rearrange("p (k s) -> p k s", k=2)
        sto = sm.take(2 * 4 * 6).rearrange("p (k c s) -> p k c s", k=2, c=4)
        ss = sm.take(2)
        nrm = sm.take(2)
        osc = sm.take(2)
        obi = sm.take(2)
        brc = sm.take(1)
        fb1 = sm.take(8)
        wcol = sm.take(NT)
        cnt3 = sm.take(3 * NT).rearrange("p (c t) -> p c t", c=3)
        mw = sm.take(NT)
        wr = sm.take(2)
        wmean = sm.take(32)

        def rows(off):
            return arena[:, off:off + NT * D].rearrange("p (t d) -> p t d", d=D)

        def cols(off, k=2):
            return arena[:, off:off + k * NPAD].rearrange("p (k n) -> p k n", k=k)

        YT = cols(0)
        ROW = rows(4096)
        YROW = rows(8192)
        LT = cols(12288)
        H1T = LT
        MT = arena[0:H, 16384:16384 + NPAD]
        KC = arena[:, 18432:18432 + NT * 512].rearrange("p (t g c) -> p t g c", t=NT, c=32)
        MROW = arena[:, 26624:26624 + NT * H].rearrange("p (t h) -> p t h", h=H)
        SQ = arena[:, 27648:28672].rearrange("p (b c) -> p b c", b=2)
        a1 = Area(arena, 28672, 32256)
        wkv = a1.take(1024).rearrange("p (k c) -> p k c", k=2)
        wqT = a1.take(512).rearrange("p (k c) -> p k c", k=2)
        w1m = a1.take(512).rearrange("p (k c) -> p k c", k=2)
        w1p = a1.take(512).rearrange("p (k c) -> p k c", k=2)
        w2m = a1.take(512).rearrange("p (k c) -> p k c", k=2)
        mask32 = a1.take(P)
        VS = a1.take(NT * 16)
        r0 = Area(ring, 0, RING)
        MR = r0.take(BODY * (H + 1 + KH)).rearrange("p (s c) -> p s c", s=BODY)
        RM = r0.take(2 * GR * WIN * (KH + 1)).rearrange("p (g t c) -> p g t c", g=2, t=GR)
        SW = RM[:, :, :, WIN * KH:]
        EA = r0.take(2 * GE).rearrange("p (g e) -> p g e", g=2)
        ru = r0.at
        U = ring[:, ru:ru + NPAD]
        re = Area(ring, ru, RING)
        EA2 = re.take(2 * GE).rearrange("p (g e) -> p g e", g=2)
        EA3 = re.take(GE).bitcast(BF16).rearrange("p (g e) -> p g e", g=2)
        gkv = r0.take(512)
        bkvr = r0.take(512)[0:1, :]
        bkv = r0.take(512)
        KVM = r0.take(2 * P).rearrange("p (g c) -> p g c", g=2)
        AM = r0.take(512).rearrange("p (g c) -> p g c", g=2)
        GM = r0.take(512).rearrange("p (g c) -> p g c", g=2)
        dr = arena[0:125, 0:512]
        drI = ring[0:125, 0:512].bitcast(I32)
        dstI = ring[:, 512:512 + ET].bitcast(I32)
        lohi = sm.take(8)
        span = sm.take(2)

        acc = arena[:, 0:NW * 16].rearrange("p (n q) -> p n q", q=16)

        KV1 = arena[:, 4096:4096 + NT * 1024].rearrange("p (t g c) -> p t g c", t=NT, c=64)
        a2 = Area(arena, 20480, 26752)
        wkv1 = a2.take(2048).rearrange("p (k c) -> p k c", k=2)
        wq1 = a2.take(1024).rearrange("p (k c) -> p k c", k=4)
        woT = a2.take(1024).rearrange("p (k c) -> p k c", k=4)
        bu = a2.take(256).rearrange("p (k c) -> p k c", k=2)
        mask64 = a2.take(P)
        a2.at = 26112
        m1 = a2.take(P)
        m2 = a2.take(P)
        m3 = a2.take(P)
        m4 = a2.take(D)
        UPR = rows(26752)
        SQ1 = arena[:, 30848:31872]
        r1a = Area(ring, 0, RING)
        KVM1 = r1a.take(4 * P).rearrange("p (g c) -> p g c", g=4)
        AM1 = r1a.take(1024).rearrange("p (g c) -> p g c", g=4)
        GM1 = r1a.take(512).rearrange("p (g c) -> p g c", g=2)
        VS1 = r1a.take(NT * 16)
        RK1 = r1a.take(NT * 8)

        acc1 = arena[:, 4096:4096 + NA * NPAD].rearrange("p (h n) -> p h n", h=NA)
        a3 = Area(arena, 4096 + NA * NPAD, 26112)
        G1 = a3.take(BODY * D).rearrange("p (s c) -> p s c", s=BODY)
        pp = a3.take(BODY * 5 * H)
        PP = pp.rearrange("p (s b c) -> p s b c", s=BODY, b=5)
        PPT = pp.bitcast(BF16).rearrange("p (s b c t) -> p s b c t", s=BODY, b=5, t=2)[:, :, :, :, 1]
        p2 = a3.take(BODY * P)
        P2 = p2.rearrange("p (s c) -> p s c", s=BODY)
        P2T = p2.bitcast(BF16).rearrange("p (s c t) -> p s c t", s=BODY, t=2)[:, :, :, 1]
        XS = a3.take(BODY * 4 * H).rearrange("p (s b c) -> p s b c", s=BODY, b=4)
        a3b = Area(arena, 26752, ARENA)
        R1 = a3b.take(GE)
        R2 = a3b.take(GE)
        R3 = a3b.take(GE)
        RBF = a3b.take(GE * 2).rearrange("p (g e) -> p g e", g=2)
        s5 = a3b.take(BODY * 5 * WIN)
        S5 = s5.rearrange("p (s k w) -> p s k w", s=BODY, k=5)
        S5T = s5.bitcast(BF16).rearrange("p (s k w t) -> p s k w t", s=BODY, k=5, t=2)[:, :, :, :, 1]
        s2 = a3b.take(BODY * WIN)
        S2 = s2.rearrange("p (s w) -> p s w", s=BODY)
        S2T = s2.bitcast(BF16).rearrange("p (s w t) -> p s w t", s=BODY, t=2)[:, :, :, 1]
        S3 = a3b.take(BODY * WIN // 2).bitcast(BF16).rearrange("p (s w) -> p s w", s=BODY)
        P3 = a3b.take(BODY * H).bitcast(BF16).rearrange("p (s c) -> p s c", s=BODY)
        TU = a3b.take(2 * P).rearrange("p (s b c) -> p s b c", s=2, b=2)
        SHC = a3b.take(BODY * 4).rearrange("p (s k) -> p s k", s=BODY)
        r3 = Area(ring, 0, 2432)
        shv = r3.take((ET + GR) * 4).rearrange("p (t k) -> p t k", k=4)
        UP12 = ring[:, RING - GE:]

        AR = arena[:, 18432:22528].rearrange("p (t b c) -> p t b c", b=4, c=64)
        BR = arena[:, 26752:30848].rearrange("p (t b c) -> p t b c", b=4, c=64)
        TMP = [arena[:, 22528 + 512 * i:23040 + 512 * i].rearrange("p (t c) -> p t c", c=64) for i in range(4)]
        BT = cols(12320)
        OT = cols(18432)
        HT = cols(12320, 8)
        WB = arena[:, 28704:28704 + NPAD]
        r4 = Area(ring, 2432, RING)
        wl = vacc[:, 0:NA * D].rearrange("p (h c) -> p h c", h=NA)
        bdb = r4.take(256).rearrange("p (k c) -> p k c", k=2)
        bds = r4.take(256).rearrange("p (k c) -> p k c", k=2)
        wc = r4.take(9 * 64).rearrange("p (v c) -> p v c", v=9)
        pat = r4.take(512).rearrange("p (a b c) -> p a b c", a=2, b=2)
        wrb = r4.take(256).rearrange("p (k c) -> p k c", k=2)
        ltm = r4.take(P)
        fb2 = r4.take(256)
        fw1 = ring[:, 0:2048].rearrange("p (k c) -> p k c", k=2)
        fw2 = r4.take(2048).rearrange("p (m c) -> p m c", m=8)
        OUTR = XT.rearrange("p k n -> p (k n)").rearrange("p (t d) -> p t d", d=D)
        junk = XT[:, 0, 0:N]

        mtab = nc.dram_tensor("mtab", [NPAD, H], F32, kind="Internal").ap()
        utab = nc.dram_tensor("utab", [NPAD, D], F32, kind="Internal").ap()
        lod = nc.dram_tensor("lod", [ET], F32, kind="Internal").ap()

        S = {n: sem(n) for n in (
            "s_zero", "s_idx", "s_const", "s_x", "s_w0", "s_lod", "s_lo", "s_npass", "s_dve", "s_span",
            "s_bnvar", "s_bnstd", "s_bn", "s_lt", "s_msg", "s_mt", "s_mtr", "s_mrow", "s_mtab",
            "s_wc", "s_kv", "s_kvc", "s_kvr", "s_vs", "s_vstd", "s_kvn", "s_kvt", "s_kvm", "s_A", "s_Am",
            "s_G", "s_Gm", "s_bv", "s_bvm", "s_h1", "s_h1e", "s_mo", "s_xt0",
            "s_acc0p",
            "s_er", "s_ea", "s_rest", "s_rready", "s_mask", "s_seg", "s_rmw", "s_curI", "s_step", "s_base",
            "s_u", "s_ue", "s_o0", "s_w1", "s_ff", "s_up", "s_upr", "s_utab", "s_w4", "s_fw1",
            "s_kv1", "s_k1c", "s_k1s", "s_v1r", "s_v1std", "s_v1n", "s_kvt1", "s_kvm1", "s_A1", "s_Am1", "s_G1", "s_Gm1",
            "s_y1", "s_xt3", "s_acc1", "s_mlp", "s_silu", "s_T", "s_prod", "s_seg1", "s_rmw1", "s_curI1", "s_oh",
            "s_shc", "s_xs", "s_split", "s_half", "s_part",
            "s_ar", "s_are", "s_b", "s_bt", "s_bte", "s_o", "s_oe", "s_nr", "s_nre", "s_nvar", "s_nstd",
            "s_wb", "s_wbe", "s_wct", "s_wcol", "s_hh", "s_he", "s_yy", "s_out", "s_store", "s_base1")}
        lnr = [[sem(f"{w}{n}") for n in range(4)] for w in ("rowT", "row", "lnvar", "lnstd", "lny", "colT", "col", "xt")]
        rowT, row, lnvar, lnstd, lny, colT, col, xtd = lnr
        gath = [sem(f"gath{k}") for k in range(BODY)]
        eal = [sem(f"eal{k}") for k in range(2)]
        rbl = [sem(f"rbl{k}") for k in range(2)]

        block = ctx.enter_context(nc.Block())
        NLOAD = {}

        def top(a):
            return a.bitcast(BF16).rearrange("p (n b) -> p n b", b=2)[:, :, 1]

        def place(slot):
            g, pos = divmod(slot, GR)
            return 2 + 2 * g + pos // 3, pos % 3 * (P + WIN)

        def outer(slot):
            b, c = place(slot)
            return ps[:, b, c:c + P]

        def affine(slot):
            b, c = place(slot)
            return ps[:, b, c + P:c + P + WIN]

        def sums(T):
            return ps[:, 4 + T // 2 % 2, T % 2 * H:T % 2 * H + NA * WIN].rearrange("p (h w) -> p h w", h=NA)

        def weights_of(pair):
            return ps[:, 2 + pair % 2, :]

        def half_of(c):
            return slice(c % 2 * H, (c % 2 + 1) * H)

        def vload(eng):
            eng.wait_ge(S["s_npass"], 1)
            return eng.value_load(npassI[0:1, 0:1], min_val=1, max_val=N // WIN + 1)

        @block.sync
        def _(sp):
            def ld(dst, a, s):
                NLOAD[s] = NLOAD.get(s, 0) + 1
                return sp.dma_start(dst, a).then_inc(S[s], 16)

            ld(drI, A["dst_r"], "s_idx")
            ld(dstI, A["dst_l"], "s_idx")
            sp.wait_ge(S["s_zero"], 2)
            ld(ROW[:, 0:NT - 1, :], A["x"][0:(NT - 1) * P, :].rearrange("(t p) d -> p t d", p=P), "s_x")
            ld(ROW[0:LAST, NT - 1, :], A["x"][(NT - 1) * P:N, :], "s_x")
            ld(ident, A["ident"], "s_const")
            ld(iota8, A["iota8"], "s_const")
            ld(bnv.rearrange("p v c -> p (v c)"), A["bnv"], "s_const")
            ld(ones, A["ones"], "s_const")
            ld(src[:, :], A["src_l"], "s_const")
            ld(ewt[:, 0:ET], A["ew"], "s_const")
            ld(mask32, A["mask32"], "s_const")
            ld(w1g.rearrange("p k h -> p (k h)"), A["w1g"], "s_const")
            for d_, n_ in ((kw1, "kw1"), (kb1r[0:1, :], "kb1r"), (w2g, "w2g"), (wV, "wV"),
                           (bq, "bq"), (b1c, "b1c"), (b2c, "b2c"), (bfc, "bfc"), (boc, "boc"),
                           (l1v.rearrange("p v c -> p (v c)"), "l1v"), (brc, "brc"), (fb1, "fb1"), (wr, "wr"),
                           (bkvr, "bkvr"), (gkv, "gkv"), (bkv, "bkv"),
                           (wkv.rearrange("p k c -> p (k c)"), "wkv"), (wqT.rearrange("p k c -> p (k c)"), "wqT"),
                           (w1m.rearrange("p k c -> p (k c)"), "w1m"), (w1p.rearrange("p k c -> p (k c)"), "w1p"),
                           (w2m.rearrange("p k c -> p (k c)"), "w2m"), (W2S.rearrange("p q j -> p (q j)"), "W2S"),
                           (wfT.rearrange("p k c -> p (k c)"), "wfT")):
                ld(d_, A[n_], "s_w0")
            for k in range(2):
                ld(XT[:, k, 0:N], A["xT"][k * P:(k + 1) * P, :], "s_w0")
            sp.wait_ge(S["s_span"], 1)
            sp.dma_start(lod.rearrange("(p q) -> p q", q=4), lohi[0:125, 0:4]).then_inc(S["s_lod"], 16)
            sp.wait_ge(S["s_lod"], 16)
            sp.dma_start(LO[:, :], lod.rearrange("(a n) -> a n", a=1).broadcast_to([P, ET])).then_inc(S["s_lo"], 16)
            sp.wait_ge(S["s_mrow"], 2)
            sp.dma_start(mtab.rearrange("(t p) h -> p t h", p=P), MROW).then_inc(S["s_mtab"], 16)

            npass = vload(sp)

            def load_ea(count, group, par):
                sp.wait_ge(S["s_er"], count)
                sp.dma_start(EA[:, par, :], A["eaT"][:, bass.ds(group * GE, GE)]).then_inc(eal[par], 16)

            with sp.Fori(0, npass) as j:
                sp.wait_ge(S["s_er"], j * NG + 2)
                sp.sem_inc(S["s_step"], 1)
                sp.wait_ge(S["s_ea"], j * (NG + 1) + 1)
                sp.sem_inc(S["s_step"], 1)
                with sp.Fori(0, ITERS + 1) as i:
                    for g in range(2):
                        load_ea(j * NG + 2 * i + g + 1, 2 * i + g, g)
                sp.wait_ge(eal[1], (j + 1) * (ITERS + 1) * 16)
                sp.sem_inc(S["s_step"], 1)
            sp.wait_ge(S["s_ue"], 4)
            for d_, n_ in ((wkv1.rearrange("p k c -> p (k c)"), "wkv1"), (wq1.rearrange("p k c -> p (k c)"), "wq1"),
                           (woT.rearrange("p k c -> p (k c)"), "woT"), (bu.rearrange("p k c -> p (k c)"), "bu"),
                           (m1[0:32, :], "m1"), (m2, "m2"), (m3, "m3"), (m4, "m4"), (mask64, "mask64")):
                ld(d_, A[n_], "s_w1")
            sp.wait_ge(S["s_o0"], 8)
            for d_, n_ in ((wl.rearrange("p k c -> p (k c)"), "wl"), (bdb.rearrange("p k c -> p (k c)"), "bdb"),
                           (bds.rearrange("p k c -> p (k c)"), "bds"), (wc.rearrange("p k c -> p (k c)"), "wc"),
                           (pat.rearrange("p a b c -> p (a b c)"), "pat"), (ltm, "ltm"), (fb2, "fb2"),
                           (fw2.rearrange("p m c -> p (m c)"), "fw2")):
                ld(d_, A[n_], "s_w4")
            sp.wait_ge(S["s_upr"], 8)
            sp.dma_start(utab.rearrange("(t p) h -> p t h", p=P), UPR).then_inc(S["s_utab"], 16)
            sp.wait_ge(S["s_xt3"], 8)
            sp.wait_ge(S["s_utab"], 16)
            sp.dma_start(shv.rearrange("p t k -> p (t k)"), A["sh"]).then_inc(S["s_utab"], 16)
            with sp.Fori(0, npass) as j:
                sp.wait_ge(S["s_mlp"], j * MP + 12)
                sp.sem_inc(S["s_step"], 1)
                with sp.Fori(0, (ITERS + 2) // 2) as i:
                    for g in range(2):
                        sp.wait_ge(S["s_mlp"], j * MP + 6 * (2 * i + g) + 2)
                        sp.dma_start(RBF[0:32, g, :],
                                     A["rbf"][bass.ds((2 * i + g) * 32, 32), :]).then_inc(rbl[g], 16)
                sp.wait_ge(rbl[1], (j + 1) * ((ITERS + 2) // 2) * 16)
                sp.sem_inc(S["s_step"], 1)
            sp.wait_ge(S["s_base1"], 1)
            sp.wait_ge(S["s_xs"], npass * (PT + 1) + 1)
            sp.sem_inc(S["s_step"], 1)
            ld(fw1.rearrange("p k c -> p (k c)"), A["fw1"], "s_fw1")
            for t in range(NT):
                sp.wait_ge(S["s_out"], t + 1)
                n = P if t < NT - 1 else LAST
                sp.dma_start(out[t * P:t * P + n, :], OUTR[0:n, t, :]).then_inc(S["s_store"], 16)
            sp.wait_ge(S["s_store"], 16 * NT)

        @block.gpsimd
        def _(pool):
            npass = vload(pool)

            def gather(free, n, t0, s0, count, table, width, ring_, used, copied):
                pool.wait_ge(used, free)
                pool.sem_inc(S["s_step"], 1)
                pool.tensor_copy(curI[:, s0:s0 + count], src[:, bass.ds(t0, count)]).then_inc(copied, 1)
                pool.wait_ge(copied, n)
                pool.sem_inc(S["s_step"], 1)
                for slot in range(s0, s0 + count):
                    pool.indirect_dma_start(ring_[:, slot, 0:width], None, table,
                                            bass.IndirectOffsetOnAxis(ap=curI[:, slot:slot + 1], axis=0)
                                            ).then_inc(gath[slot], 16)

            pool.wait_ge(S["s_mtab"], 16)
            with pool.Fori(0, npass) as j:
                with pool.Fori(0, ITERS) as i:
                    for h in range(2):
                        gather(j * 2 * ITERS + 2 * i + h + 1, j * 2 * ITERS + 2 * i + h + 1,
                               i * BODY + h * GR, h * GR, GR, mtab, H, MR, S["s_seg"], S["s_curI"])
            pool.wait_ge(S["s_utab"], 32)
            pool.wait_ge(S["s_xt3"], 8)
            with pool.Fori(0, npass) as j:
                pool.wait_ge(S["s_xs"], j * (PT + 1) + 1)
                pool.sem_inc(S["s_step"], 1)
                with pool.Fori(0, ITERS) as i:
                    for p in range(BP):
                        gather(j * PT + i * BP + p + 1, j * (PT + 1) + i * BP + p + 1, i * BODY + 2 * p, 2 * p, 2,
                               utab, D, G1, S["s_prod"], S["s_curI1"])
                gather((j + 1) * PT + 1, (j + 1) * (PT + 1), ET, 0, 2, utab, D, G1, S["s_prod"], S["s_curI1"])

        @block.scalar
        def _(act):
            def rows_and_std(v):
                if v:
                    for i in range(NT // 2):
                        act.wait_ge(rowT[v], i + 1)
                        act.activation(ROW[:, 2 * i:2 * i + 2, :].rearrange("p t d -> p (t d)"),
                                       ps[:, 4 + i % 4, :], ACT.Copy).then_inc(row[v], 1)
                act.wait_ge(lnvar[v], 1)
                act.activation(std, var, ACT.Sqrt).then_inc(lnstd[v], 1)

            def cols_out(v):
                for i in range(NT // 2):
                    c, k = divmod(i, 2)
                    act.wait_ge(colT[v], i + 1)
                    act.activation(YT[:, k, 512 * c:512 * c + 512], ps[:, i % 4, :], ACT.Copy).then_inc(col[v], 1)

            act.wait_ge(S["s_bnvar"], 1)
            act.activation(bns, bnt, ACT.Sqrt).then_inc(S["s_bnstd"], 1)
            rows_and_std(0)
            cols_out(0)
            act.wait_ge(col[0], 8)
            act.wait_ge(S["s_bn"], 1)
            for k in range(2):
                act.activation(LT[:, k, :], YT[:, k, :], ACT.Relu, bias=bnb[:, k:k + 1],
                               scale=bns[:, k:k + 1]).then_inc(S["s_lt"], 1)
            for c in range(4):
                act.wait_ge(S["s_msg"], c + 1)
                act.activation(MT[:, 512 * c:512 * c + 512], ps[0:H, c, :], ACT.Relu, bias=bnb[0:H, 2:3],
                               scale=bns[0:H, 2:3]).then_inc(S["s_mt"], 1)
            for t in range(NT):
                act.wait_ge(S["s_kv"], t + 1)
                act.activation(KC[:, t, :, :].rearrange("p g c -> p (g c)"), ps[:, t % 4, :],
                               ACT.Copy).then_inc(S["s_kvc"], 1)
                if t >= 2:
                    act.wait_ge(S["s_vs"], t - 1)
                act.activation(SQ[:, t % 2, :], ps[:, t % 4, :], ACT.Square).then_inc(S["s_kvr"], 1)
            act.wait_ge(S["s_vs"], NT + 1)
            act.activation(VS, VS, ACT.Sqrt).then_inc(S["s_vstd"], 1)
            for i in range(8):
                c, o = divmod(i, 2)
                act.wait_ge(S["s_h1"], i + 1)
                if i == 0:
                    act.wait_ge(S["s_bvm"], 1)
                act.activation(H1T[:, o, 512 * c:512 * c + 512], ps[:, i % 4, :], ACT.Gelu,
                               bias=bvec[:, o:o + 1]).then_inc(S["s_h1e"], 1)
            act.wait_ge(S["s_xt0"], 16)
            act.wait_ge(S["s_mtab"], 16)
            act.memzero(arena[:, 20000:NW * 16]).then_inc(S["s_acc0p"], 1)

            npass = vload(act)
            def relu(par, lead, free):
                act.wait_ge(S["s_er"], lead)
                act.wait_ge(S["s_seg"], free)
                act.activation(MR[:, par * GR:(par + 1) * GR, H + 1:],
                               ps[:, par, 0:GR * KH].rearrange("p (t q) -> p t q", t=GR),
                               ACT.Relu).then_inc(S["s_rready"], 1)

            with act.Fori(0, npass) as j:
                relu(0, j * NG + 3, j * 2 * ITERS + 1)
                with act.Fori(0, ITERS) as i:
                    for g in range(2):
                        relu(1 - g, j * NG + 2 * i + g + 4, (j * ITERS + i) * 2 + g + 2)
            for c in range(4):
                act.wait_ge(S["s_u"], c + 1)
                act.activation(U[half_of(c), NCH * c:NCH * (c + 1)], ps[half_of(c), c, 0:NCH], ACT.Relu,
                               bias=bnb[half_of(c), 3:4], scale=bns[half_of(c), 3:4]).then_inc(S["s_ue"], 1)
            rows_and_std(1)
            cols_out(1)
            rows_and_std(2)
            cols_out(2)
            for i in range(NT // 2):
                act.wait_ge(S["s_up"], i + 1)
                act.activation(UPR[:, 2 * i:2 * i + 2, :].rearrange("p t d -> p (t d)"), ps[:, 4 + i % 4, :],
                               ACT.Copy).then_inc(S["s_upr"], 1)
            for t in range(NT):
                act.wait_ge(S["s_kv1"], t + 1)
                b = 2 * (t % 2)
                act.activation(KV1[:, t, :, :].rearrange("p g c -> p (g c)"),
                               ps[:, b:b + 2, :].rearrange("p b c -> p (b c)"), ACT.Copy).then_inc(S["s_k1c"], 1)
                if t >= 1:
                    act.wait_ge(S["s_v1r"], t)
                act.activation(SQ1, ps[:, b:b + 2, :].rearrange("p b c -> p (b c)"),
                               ACT.Square).then_inc(S["s_k1s"], 1)
            act.wait_ge(S["s_v1r"], NT + 1)
            act.activation(VS1, VS1, ACT.Sqrt).then_inc(S["s_v1std"], 1)
            def silu(j, c, layer_, half, free=None):
                act.wait_ge(S["s_mlp"], j * MP + 6 * c + 2 * layer_ + half + 13)
                if free is not None:
                    act.wait_ge(*free)
                act.activation((R1, R2, R3)[layer_][:, half * GE // 2:(half + 1) * GE // 2], ps[:, half, 0:GE // 2],
                               ACT.Silu).then_inc(S["s_silu"], 1)

            def scale(j, i, p):
                n = j * (PT + 1) + i * BP + p
                t0 = i * BODY + 2 * p
                i, p = i + p // BP, p % BP
                for slot in (2 * p, 2 * p + 1):
                    act.wait_ge(gath[slot], (npass * ITERS + j * (ITERS + (p == 0)) + i + 1) * 16)
                act.activation(SHC[:, 2 * p:2 * p + 2, :], shv[:, bass.ds(t0, 2), :], ACT.Copy).then_inc(S["s_shc"], 1)
                act.wait_ge(S["s_shc"], n + 1)
                for s_ in range(2):
                    for x in range(4):
                        ins = act.activation(XS[:, 2 * p + s_, x, :], G1[:, 2 * p + s_, x * H:(x + 1) * H], ACT.Copy,
                                             scale=SHC[:, 2 * p + s_, (x - 1) % 4:(x - 1) % 4 + 1])
                ins.then_inc(S["s_xs"], 1)

            act.wait_ge(S["s_kvt1"], 1)
            act.memzero(acc1[:, 3:NA, :]).then_inc(S["s_acc1"], 1)
            act.sem_inc(S["s_xs"], 1)
            with act.Fori(0, npass) as j:
                for n in range(6):
                    silu(j, 0, n // 2, n % 2, (S["s_split"], j * SPL + 1) if n == 4 else None)
                for half in range(2):
                    silu(j, 1, 0, half)
                scale(j, 0, 0)
                with act.Fori(0, ITERS) as i:
                    scale(j, i, 1)
                    silu(j, i + 1, 1, 0)
                    scale(j, i, 2)
                    silu(j, i + 1, 1, 1)
                    silu(j, i + 1, 2, 0, (S["s_split"], j * SPL + 2 * i + 3))
                    scale(j, i, 3)
                    silu(j, i + 1, 2, 1)
                    scale(j, i, 4)
                    silu(j, i + 2, 0, 0)
                    scale(j, i, 5)
                    silu(j, i + 2, 0, 1)
            for i in range(NT // 2):
                act.wait_ge(S["s_ar"], i + 1)
                act.activation(AR[:, 2 * i:2 * i + 2, :, :].rearrange("p t b c -> p (t b c)"), ps[:, 4 + i % 4, :],
                               ACT.Copy).then_inc(S["s_are"], 1)
            for i in range(NT // 2):
                c, k = divmod(i, 2)
                act.wait_ge(S["s_bt"], i + 1)
                act.activation(BT[:, k, 512 * c:512 * c + 512], ps[:, i % 4, :], ACT.Copy).then_inc(S["s_bte"], 1)
            for i in range(8):
                c, k = divmod(i, 2)
                act.wait_ge(S["s_o"], i + 1)
                act.activation(OT[:, k, 512 * c:512 * c + 512], ps[:, 4 + i % 4, :], ACT.Copy).then_inc(S["s_oe"], 1)
            act.wait_ge(S["s_nvar"], 1)
            act.activation(nrm, nrm, ACT.Sqrt).then_inc(S["s_nstd"], 1)
            rows_and_std(3)
            cols_out(3)
            for c in range(4):
                act.wait_ge(S["s_wb"], c + 1)
                act.activation(WB[:, 512 * c:512 * c + 512], ps[:, 4 + c, :], ACT.Identity,
                               bias=brc[:, 0:1]).then_inc(S["s_wbe"], 1)
            for i in range(32):
                c, m = divmod(i, 8)
                act.wait_ge(S["s_hh"], i + 1)
                act.activation(HT[:, m, 512 * c:512 * c + 512], ps[:, i % 4, :], ACT.Gelu_apprx_tanh,
                               bias=fb1[:, m:m + 1]).then_inc(S["s_he"], 1)

        @block.tensor
        def _(pe):
            def to_rows(v):
                pe.wait_ge(xtd[v], 1)
                for i in range(NT // 2):
                    if v == 3:
                        pe.wait_ge(xtd[v], i // 2 + 1)
                    if i >= 4:
                        pe.wait_ge(row[v], i - 3)
                    for t in range(2):
                        for k in range(2):
                            tr = pe.transpose(ps[:, 4 + i % 4, t * D + k * P:t * D + (k + 1) * P],
                                              XT[:, k, (2 * i + t) * P:(2 * i + t + 1) * P], ident)
                    tr.then_inc(rowT[v], 1)

            def to_cols(v):
                for i in range(NT // 2):
                    c, k = divmod(i, 2)
                    pe.wait_ge(lny[v], 4 * c + 4)
                    if i >= 4:
                        pe.wait_ge(col[v], i - 3)
                    for t in range(4):
                        tr = pe.transpose(ps[:, i % 4, t * P:(t + 1) * P], YROW[:, 4 * c + t, k * P:(k + 1) * P], ident)
                    tr.then_inc(colT[v], 1)

            pe.wait_ge(S["s_const"], 16 * NLOAD["s_const"])
            pe.wait_ge(S["s_idx"], 32)
            pe.wait_ge(S["s_span"], 1)
            pe.transpose(ps[0:1, 7, 0:125], span[0:125, 0:1], ident[0:125, 0:125]).then_inc(S["s_span"], 1)
            to_cols(0)
            for c in range(4):
                pe.wait_ge(S["s_lt"], 2)
                for k in range(2):
                    mm = pe.matmul(ps[0:H, c, :], w1g[:, k, :], LT[:, k, 512 * c:512 * c + 512],
                                   start=(k == 0), stop=(k == 1))
                mm.then_inc(S["s_msg"], 1)
            for i in range(2):
                pe.wait_ge(S["s_mt"], 2 * i + 2)
                for t in range(8):
                    n = 8 * i + t
                    tr = pe.transpose(ps[:, 4 + i, t * H:(t + 1) * H], MT[:, n * P:(n + 1) * P], ident[0:H, 0:H])
                tr.then_inc(S["s_mtr"], 1)
            pe.wait_ge(S["s_w0"], 16 * NLOAD["s_w0"])
            pe.wait_ge(S["s_wc"], 1)
            pe.wait_ge(S["s_mt"], 4)
            for t in range(NT):
                if t >= 4:
                    pe.wait_ge(S["s_kvr"], t - 3)
                b = ps[:, t % 4, :]
                for k in range(2):
                    pe.matmul(b, YT[:, k, t * P:(t + 1) * P], wkv[:, k, :], start=(k == 0), stop=False)
                pe.matmul(b, ones[0:1, :], bkvr, start=False, stop=True).then_inc(S["s_kv"], 1)
            for g in range(2):
                for t in range(NT):
                    pe.wait_ge(S["s_kvn"], t + 1)
                    r = P if t < NT - 1 else LAST
                    KCf = KC[0:r, t, :, :].rearrange("p g c -> p (g c)")
                    mm = pe.matmul(ps[:, 6, g * P:(g + 1) * P], KCf[:, 256 + g * P:256 + (g + 1) * P],
                                   KCf[:, g * P:(g + 1) * P], start=(t == 0), stop=(t == NT - 1))
            mm.then_inc(S["s_kvt"], 1)
            pe.wait_ge(S["s_kvm"], 1)
            for g in range(2):
                mm = pe.matmul(ps[:, 4, g * D:(g + 1) * D], KVM[:, g, :], w1m[:, g, :], start=True, stop=True)
            mm.then_inc(S["s_A"], 1)
            pe.wait_ge(S["s_Am"], 1)
            for c in range(2):
                for g in range(2):
                    mm = pe.matmul(ps[:, 5, c * D:(c + 1) * D], wqT[:, g, c * P:(c + 1) * P], AM[:, g, :],
                                   start=(g == 0), stop=(g == 1))
            mm.then_inc(S["s_G"], 1)
            for o in range(2):
                for g in range(2):
                    mm = pe.matmul(ps[:, 7, o:o + 1], AM[:, g, o * P:(o + 1) * P], bq[:, g:g + 1],
                                   start=(g == 0), stop=(g == 1))
            mm.then_inc(S["s_bv"], 1)
            pe.wait_ge(S["s_Gm"], 1)
            pe.wait_ge(S["s_bvm"], 1)
            for i in range(8):
                c, o = divmod(i, 2)
                if i >= 4:
                    pe.wait_ge(S["s_h1e"], i - 3)
                for k in range(2):
                    mm = pe.matmul(ps[:, i % 4, :], GM[:, k, o * P:(o + 1) * P], YT[:, k, 512 * c:512 * c + 512],
                                   start=(k == 0), stop=(k == 1))
                mm.then_inc(S["s_h1"], 1)
            for i in range(8):
                c, o = divmod(i, 2)
                pe.wait_ge(S["s_h1e"], 2 * c + 2)
                if i >= 4:
                    pe.wait_ge(S["s_xt0"], i - 3)
                for k in range(2):
                    mm = pe.matmul(ps[:, 4 + i % 4, :], w2m[:, k, o * P:(o + 1) * P], H1T[:, k, 512 * c:512 * c + 512],
                                   start=(k == 0), stop=(k == 1))
                mm.then_inc(S["s_mo"], 1)

            npass = vload(pe)
            pe.wait_ge(S["s_xt0"], 16)
            pe.sem_inc(S["s_er"], 2)
            pe.sem_inc(S["s_seg"], 2)

            def edge_net(par, ready, free):
                pe.wait_ge(S["s_ea"], ready)
                if free is not None:
                    pe.wait_ge(S["s_rready"], free)
                for t in range(GR):
                    r = ps[:, par, t * KH:(t + 1) * KH]
                    e = slice(t * P, (t + 1) * P)
                    for n, b in enumerate((top(kb1r[0:1, :]), top(kb2[0:1, :]), kb3[0:1, :])):
                        pe.matmul(r, top(ones[0:1, :]), b, start=(n == 0), stop=False)
                    e1, e2, e3 = top(EA[:, par, e]), top(EA2[:, par, e]), EA3[:, par, e]
                    for a_, b in ((e1, top(kw1)), (e1, top(k2)), (e1, k3), (e2, top(kw1)), (e2, top(k2)), (e3, top(kw1))):
                        mm = pe.matmul(r, a_, b, start=False, stop=(a_ is e3))
                mm.then_inc(S["s_er"], 1)

            def segments(j, i, g):
                pe.wait_ge(S["s_mask"], j * NG + 2 * i + g + 1)
                pe.wait_ge(S["s_rmw"], j * (ET + GR) + i * BODY + g * GR + 1)
                for t in range(GR):
                    slot = g * GR + t
                    pe.wait_ge(gath[slot], (j * ITERS + i + 1) * 16)
                    b, c = place(slot)
                    pe.matmul(ps[0:H, b, c:c + P], MR[:, slot, 0:H], RM[:, g, t, 0:P], start=True, stop=True)
                    pe.matmul(ps[H:P, b, c:c + P + WIN], MR[:, slot, 0:H], RM[:, g, t, P:], start=True, stop=True)
                    mm = pe.matmul(affine(slot)[0:H, :], MR[:, slot, KH + 1:], SW[:, g, t, :], start=True, stop=True)
                mm.then_inc(S["s_seg"], 1)

            with pe.Fori(0, npass) as j:
                edge_net(0, j * (NG + 1) + 2, None)
                with pe.Fori(0, ITERS) as i:
                    edge_net(1, j * (NG + 1) + 2 * i + 3, j * (2 * ITERS + 1) + 2 * i + 1)
                    segments(j, i, 0)
                    edge_net(0, j * (NG + 1) + 2 * i + 4, j * (2 * ITERS + 1) + 2 * i + 2)
                    segments(j, i, 1)
                pe.wait_ge(S["s_rready"], (j + 1) * NG)
            pe.wait_ge(S["s_base"], 1)
            for c0 in (0, 2):
                for c in (c0, c0 + 1):
                    pe.matmul(ps[half_of(c), c, 0:NCH], wV, vacc[:, c * NCH:(c + 1) * NCH], start=True, stop=False)
                for q in range(16):
                    for c in (c0, c0 + 1):
                        mm = pe.matmul(ps[half_of(c), c, 0:NCH], W2S[:, q, :], acc[:, c * NCH:(c + 1) * NCH, q],
                                       start=False, stop=(q == 15))
                        if q == 15:
                            mm.then_inc(S["s_u"], 1)
            for i in range(8):
                c, o = divmod(i, 2)
                pe.wait_ge(S["s_ue"], c + 1)
                if i >= 4:
                    pe.wait_ge(S["s_o0"], i - 3)
                pe.matmul(ps[:, 4 + i % 4, 0:NCH], w2g[half_of(c), o * P:(o + 1) * P], U[half_of(c), c * NCH:(c + 1) * NCH],
                          start=True, stop=True).then_inc(S["s_mo"], 1)
            to_rows(1)
            to_cols(1)
            for i in range(8):
                c, o = divmod(i, 2)
                pe.wait_ge(col[1], 2 * c + 2)
                pe.wait_ge(S["s_ff"], i - 3) if i >= 4 else pe.wait_ge(row[1], 8)
                for k in range(2):
                    mm = pe.matmul(ps[:, 4 + i % 4, :], wfT[:, k, o * P:(o + 1) * P], YT[:, k, 512 * c:512 * c + 512],
                                   start=(k == 0), stop=(k == 1))
                mm.then_inc(S["s_mo"], 1)
            to_rows(2)
            to_cols(2)
            pe.wait_ge(S["s_w1"], 16 * NLOAD["s_w1"])
            pe.wait_ge(row[2], 8)
            for i in range(NT // 2):
                pe.wait_ge(col[2], 2 * (i // 2) + 2)
                if i >= 4:
                    pe.wait_ge(S["s_upr"], i - 3)
                for t in range(2):
                    for k in range(2):
                        mm = pe.matmul(ps[:, 4 + i % 4, t * D + k * P:t * D + (k + 1) * P],
                                       YT[:, k, (2 * i + t) * P:(2 * i + t + 1) * P], bu[:, k, :], start=True, stop=True)
                mm.then_inc(S["s_up"], 1)
            pe.wait_ge(S["s_wc"], 2)
            pe.wait_ge(col[2], 8)
            for t in range(NT):
                if t >= 2:
                    pe.wait_ge(S["s_k1s"], t - 1)
                for h in range(2):
                    for k in range(2):
                        mm = pe.matmul(ps[:, 2 * (t % 2) + h, :], YT[:, k, t * P:(t + 1) * P],
                                       wkv1[:, k, h * 512:(h + 1) * 512], start=(k == 0), stop=(k == 1))
                mm.then_inc(S["s_kv1"], 1)
            pe.wait_ge(S["s_upr"], 8)
            for g in range(4):
                for t in range(NT):
                    pe.wait_ge(S["s_v1n"], t + 1)
                    r = P if t < NT - 1 else LAST
                    KVf = KV1[0:r, t, :, :].rearrange("p g c -> p (g c)")
                    mm = pe.matmul(ps[:, 4, g * P:(g + 1) * P], KVf[:, 512 + g * P:512 + (g + 1) * P],
                                   KVf[:, g * P:(g + 1) * P], start=(t == 0), stop=(t == NT - 1))
            mm.then_inc(S["s_kvt1"], 1)
            pe.wait_ge(S["s_kvm1"], 1)
            for g in range(4):
                mm = pe.matmul(ps[:, 5 + g // 2, (g % 2) * D:(g % 2 + 1) * D], KVM1[:, g, :], woT[:, g, :],
                               start=True, stop=True)
            mm.then_inc(S["s_A1"], 1)
            pe.wait_ge(S["s_Am1"], 2)
            for c in range(2):
                for g in range(4):
                    mm = pe.matmul(ps[:, 7, c * D:(c + 1) * D], wq1[:, g, c * P:(c + 1) * P], AM1[:, g, :],
                                   start=(g == 0), stop=(g == 3))
            mm.then_inc(S["s_G1"], 1)
            pe.wait_ge(S["s_Gm1"], 1)
            for i in range(8):
                c, o = divmod(i, 2)
                if i >= 4:
                    pe.wait_ge(S["s_xt3"], i - 3)
                for k in range(2):
                    mm = pe.matmul(ps[:, i % 4, :], GM1[:, k, o * P:(o + 1) * P], YT[:, k, 512 * c:512 * c + 512],
                                   start=(k == 0), stop=(k == 1))
                mm.then_inc(S["s_y1"], 1)

            pe.wait_ge(S["s_xt3"], 8)
            pe.wait_ge(S["s_utab"], 32)
            pe.wait_ge(S["s_acc1"], 2)
            pe.sem_inc(S["s_mlp"], 12)
            pe.sem_inc(S["s_T"], BP)
            pe.sem_inc(S["s_seg1"], BP)

            def layer(layer_, half, par, after):
                w, x = ((m1[0:32, :], RBF[0:32, par, :]), (m2, R1), (m3, R2))[layer_]
                if after is not None:
                    pe.wait_ge(S["s_silu"], after)
                pe.matmul(ps[:, half, 0:GE // 2], w, x[:, half * GE // 2:(half + 1) * GE // 2],
                          start=True, stop=True).then_inc(S["s_mlp"], 1)

            def weights(j, i, q):
                pe.wait_ge(S["s_prod"], j * PT + i * BP + q + 4)
                for k in (2 * q, 2 * q + 1):
                    h = k // GR % 2
                    if k % GR == 0:
                        pe.wait_ge(S["s_split"], j * SPL + 2 * i + k // GR + 2)
                    for m in range(2):
                        mm = pe.matmul(weights_of(q)[:, k % 2 * D:(k % 2 + 1) * D], RS[:, h, (k % GR) * P:(k % GR + 1) * P],
                                       m4s[:, m, :], start=(m == 0), stop=(m == 1))
                mm.then_inc(S["s_T"], 1)

            def segment(j, i, u, p):
                m = i * BP + p
                pe.wait_ge(S["s_prod"], j * PT + m + BP + 1)
                pe.wait_ge(S["s_rmw1"], j * (ET + AHEAD) + m * 2 + 1)
                for s_ in (2 * p, 2 * p + 1):
                    o = sums(u * BODY + s_)
                    pe.matmul(o[:, 0:4, :], PP[:, s_, 0:2, :], S5[:, s_, 0:4, :], start=True, stop=True)
                    pe.matmul(o[0:H, 5, :], PP[:, s_, 4, :], S5[:, s_, 4, :], start=True, stop=True)
                    x1, x2, x3 = PPT[:, s_, 2:4, :], P2T[:, s_, :], P3[:, s_, :]
                    y1, y2, y3 = S5T[:, s_, 4, :], S2T[:, s_, :], S3[:, s_, :]
                    for n, (x, y) in enumerate(((x1, y1), (x1, y2), (x1, y3), (x2, y1), (x2, y2), (x3, y1))):
                        mm = pe.matmul(o[:, 4, :], x, y, start=(n == 0), stop=(n == 5))
                mm.then_inc(S["s_seg1"], 1)

            with pe.Fori(0, npass) as j:
                pe.wait_ge(rbl[0], (j * ((ITERS + 2) // 2) + 1) * 16)
                for n in range(6):
                    layer(n // 2, n % 2, 0, j * MP + n - 1 if n >= 2 else None)
                pe.wait_ge(rbl[1], (j * ((ITERS + 2) // 2) + 1) * 16)
                for half in range(2):
                    layer(0, half, 1, j * MP + 5 + half)
                weights(j, 0, 0)
                with pe.Fori(0, ITERS // 2) as i2:
                    for u in range(2):
                        i = 2 * i2 + u
                        for p in range(BP):
                            if p == 3:
                                pe.wait_ge(rbl[u], (j * ((ITERS + 2) // 2) + i2 + 2) * 16)
                            for n in ((2,), (3, 4), (5,), (6,), (7,))[p]:
                                layer(n // 2 % 3, n % 2, u, j * MP + 6 * i + 5 + n)
                            weights(j, 2 * i2, u * BP + p + 1)
                            segment(j, i, u, p)
                pe.wait_ge(S["s_silu"], (j + 1) * MP)
                pe.wait_ge(rbl[1], (j + 1) * ((ITERS + 2) // 2) * 16)
            pe.wait_ge(S["s_base1"], 1)
            pe.wait_ge(S["s_w4"], 16 * NLOAD["s_w4"])
            for i in range(NT // 2):
                if i >= 4:
                    pe.wait_ge(S["s_are"], i - 3)
                for t in range(2):
                    for x, hs in enumerate(((0,), (1, 4), (2, 4), (3, 5))):
                        for h in hs:
                            o = slice(t * D + x * H, t * D + (x + 1) * H)
                            mm = pe.matmul(ps[:, 4 + i % 4, o], acc1[:, h, (2 * i + t) * P:(2 * i + t + 1) * P],
                                           wl[:, h, x * H:(x + 1) * H], start=(h == hs[0]), stop=(h == hs[-1]))
                mm.then_inc(S["s_ar"], 1)
            for i in range(NT // 2):
                c, k = divmod(i, 2)
                pe.wait_ge(S["s_b"], c // 2 + 1)
                if i >= 4:
                    pe.wait_ge(S["s_bte"], i - 3)
                for t in range(4):
                    tr = pe.transpose(ps[:, i % 4, t * P:(t + 1) * P],
                                      BR[:, 4 * c + t, 2 * k:2 * k + 2, :].rearrange("p b c -> p (b c)"), ident)
                tr.then_inc(S["s_bt"], 1)
            pe.wait_ge(S["s_are"], 8)
            for i in range(8):
                c, k = divmod(i, 2)
                pe.wait_ge(S["s_bte"], i + 1)
                if i >= 4:
                    pe.wait_ge(S["s_oe"], i - 3)
                pe.matmul(ps[:, 4 + i % 4, :], bdb[:, k, :], BT[:, k, 512 * c:512 * c + 512], start=True, stop=False)
                pe.matmul(ps[:, 4 + i % 4, :], bds[:, k, :], YT[:, k, 512 * c:512 * c + 512], start=False,
                          stop=True).then_inc(S["s_o"], 1)
            pe.wait_ge(S["s_nr"], 1)
            for o in range(2):
                for k in range(2):
                    mm = pe.matmul(ps[:, 0, o:o + 1], pat[:, k, o, :], ss[:, k:k + 1], start=(k == 0), stop=(k == 1))
            mm.then_inc(S["s_nre"], 1)
            to_rows(3)
            to_cols(3)
            pe.wait_ge(row[3], 8)
            pe.wait_ge(S["s_fw1"], 16)
            for c in range(4):
                pe.wait_ge(col[3], 2 * c + 2)
                for k in range(2):
                    mm = pe.matmul(ps[:, 4 + c, :], wrb[:, k, :], YT[:, k, 512 * c:512 * c + 512],
                                   start=(k == 0), stop=(k == 1))
                mm.then_inc(S["s_wb"], 1)
            for i in range(4):
                pe.wait_ge(S["s_wbe"], 4)
                for t in range(4):
                    tr = pe.transpose(ps[:, 4 + i, t * P:(t + 1) * P], WB[:, (4 * i + t) * P:(4 * i + t + 1) * P], ident)
                tr.then_inc(S["s_wct"], 1)
            for i in range(32):
                c, m = divmod(i, 8)
                if i >= 4:
                    pe.wait_ge(S["s_he"], i - 3)
                for k in range(2):
                    mm = pe.matmul(ps[:, i % 4, :], fw1[:, k, m * P:(m + 1) * P], YT[:, k, 512 * c:512 * c + 512],
                                   start=(k == 0), stop=(k == 1))
                mm.then_inc(S["s_hh"], 1)
            pe.wait_ge(S["s_wcol"], 4)
            for t in range(NT):
                pe.wait_ge(S["s_he"], 8 * (t // 4) + 8)
                if t >= 4:
                    pe.wait_ge(S["s_out"], t - 3)
                for m in range(8):
                    mm = pe.matmul(ps[:, 4 + t % 4, 0:D], HT[:, m, t * P:(t + 1) * P], fw2[:, m, :],
                                   start=(m == 0), stop=(m == 7))
                mm.then_inc(S["s_yy"], 1)

        @block.vector
        def _(dve):
            n = [0]

            def link(ins):
                n[0] += 1
                ins.then_inc(S["s_dve"], 1)
                dve.wait_ge(S["s_dve"], n[0])

            def layer_norm(v):
                for t in range(NT):
                    if v:
                        dve.wait_ge(row[v], t // 2 + 1)
                    ins = dve.bn_stats(st[:, t, :], ROW[:, t, :])
                link(ins)
                for t in range(NT):
                    ins = dve.bn_aggr(mv[:, t, :], st[:, t, :])
                link(ins)
                dve.tensor_scalar(var, mv[:, :, 1], EPS, None, ALU.add).then_inc(lnvar[v], 1)
                dve.wait_ge(lnstd[v], 1)
                link(dve.reciprocal(rs, std))
                for t in range(NT):
                    dve.tensor_scalar(YROW[:, t, :], ROW[:, t, :], mv[:, t, 0:1], rs[:, t:t + 1],
                                      ALU.subtract, ALU.mult).then_inc(lny[v], 1)

            dve.memset(ROW[:, NT - 1, :], 0.0).then_inc(S["s_zero"], 1)
            dve.memset(XT[:, :, N:NPAD], 0.0).then_inc(S["s_zero"], 1)
            dve.memset(vacc[:, :], 0.0)
            dve.memset(ewt[:, ET:], 0.0)
            dve.memset(dloc[:, ET:], -1.0)
            dve.memset(baseI[:, 0:GR], 0)
            dve.wait_ge(S["s_idx"], 32)
            dve.tensor_copy(dstF[:, :], dstI)
            link(dve.tensor_copy(dr, drI))
            dve.memset(MR[:, :, H:H + 1], 1.0)
            drv = dr.rearrange("p (q e) -> p q e", q=4)
            dve.tensor_reduce(lohi[0:125, 0:4], drv, AX.X, ALU.min)
            link(dve.tensor_reduce(lohi[0:125, 4:8], drv, AX.X, ALU.max))
            link(dve.tensor_tensor(cnt3[0:125, 0, 0:4], lohi[0:125, 4:8], lohi[0:125, 0:4], ALU.subtract))
            dve.tensor_reduce(span[0:125, 0:1], cnt3[0:125, 0, 0:4], AX.X, ALU.max).then_inc(S["s_span"], 1)
            dve.wait_ge(S["s_span"], 2)
            link(dve.tensor_reduce(span[0:1, 1:2], ps[0:1, 7, 0:125], AX.X, ALU.max))
            link(dve.tensor_copy(npassI[0:1, 1:2], span[0:1, 1:2]))
            link(dve.tensor_scalar(npassI[0:1, 1:2], npassI[0:1, 1:2], 3, None, ALU.arith_shift_right))
            dve.tensor_scalar(npassI[0:1, 0:1], npassI[0:1, 1:2], 1, None, ALU.add).then_inc(S["s_npass"], 1)
            dve.wait_ge(S["s_const"], 16 * NLOAD["s_const"])
            dve.tensor_scalar(bnt, bnv[:, 3, :], EPS, None, ALU.add).then_inc(S["s_bnvar"], 1)
            dve.wait_ge(S["s_bnstd"], 1)
            link(dve.reciprocal(bns, bns))
            link(dve.tensor_tensor(bns, bns, bnv[:, 0, :], ALU.mult))
            link(dve.tensor_tensor(bnb, bnv[:, 4, :], bnv[:, 2, :], ALU.subtract))
            link(dve.tensor_tensor(bnb, bnb, bns, ALU.mult))
            dve.tensor_tensor(bnb, bnb, bnv[:, 1, :], ALU.add).then_inc(S["s_bn"], 1)
            dve.wait_ge(S["s_x"], 32)
            layer_norm(0)
            for i in range(2):
                dve.wait_ge(S["s_mtr"], i + 1)
                dve.tensor_copy(MROW[:, 8 * i:8 * i + 8, :].rearrange("p t h -> p (t h)"),
                                ps[:, 4 + i, :]).then_inc(S["s_mrow"], 1)

            def centre(w, g, c):
                wv = w.rearrange("p (g c) -> p g c", c=c)
                m = wmean[0:w.shape[0], 0:g]
                link(dve.tensor_reduce(m, wv, AX.X, ALU.add))
                link(dve.tensor_scalar(m, m, 1.0 / c, None, ALU.mult))
                link(dve.tensor_tensor(wv, wv, m.unsqueeze(2).broadcast_to([w.shape[0], g, c]), ALU.subtract))

            dve.wait_ge(S["s_w0"], 16 * NLOAD["s_w0"])
            for k in range(2):
                centre(wkv[:, k, :], 16, 32)
            centre(bkvr, 16, 32)
            dve.sem_inc(S["s_wc"], 1)
            for t in range(NT):
                dve.wait_ge(S["s_kvr"], t + 1)
                dve.tensor_reduce(VS[:, t * 16:(t + 1) * 16], SQ[:, t % 2, :].rearrange("p (g c) -> p g c", c=32),
                                  AX.X, ALU.add).then_inc(S["s_vs"], 1)
            dve.wait_ge(S["s_vs"], NT)
            dve.tensor_scalar(VS, VS, 1.0 / 32, EPS, ALU.mult, ALU.add).then_inc(S["s_vs"], 1)
            dve.wait_ge(S["s_vstd"], 1)
            link(dve.reciprocal(VS, VS))
            for t in range(NT):
                dve.wait_ge(S["s_kvc"], t + 1)
                ins = dve.tensor_tensor(KC[:, t, :, :], KC[:, t, :, :],
                                        VS[:, t * 16:(t + 1) * 16].unsqueeze(2).broadcast_to([P, 16, 32]), ALU.mult)
            link(ins)
            for t in range(NT):
                ins = dve.tensor_tensor(KC[:, t, :, :], KC[:, t, :, :], gkv.rearrange("p (g c) -> p g c", c=32), ALU.mult)
            link(ins)
            for t in range(NT):
                dve.tensor_tensor(KC[:, t, :, :], KC[:, t, :, :], bkv.rearrange("p (g c) -> p g c", c=32),
                                  ALU.add).then_inc(S["s_kvn"], 1)
            dve.wait_ge(S["s_kvt"], 1)
            dve.tensor_tensor(KVM, ps[:, 6, 0:256].rearrange("p (g c) -> p g c", g=2),
                              mask32.unsqueeze(1).broadcast_to([P, 2, P]), ALU.mult).then_inc(S["s_kvm"], 1)
            dve.wait_ge(S["s_A"], 1)
            dve.tensor_copy(AM.rearrange("p g c -> p (g c)"), ps[:, 4, :]).then_inc(S["s_Am"], 1)
            dve.wait_ge(S["s_G"], 1)
            dve.tensor_tensor(GM.rearrange("p g c -> p (g c)"), ps[:, 5, :], w1p.rearrange("p g c -> p (g c)"),
                              ALU.add).then_inc(S["s_Gm"], 1)
            dve.wait_ge(S["s_bv"], 1)
            dve.tensor_tensor(bvec, ps[:, 7, 0:2], b1c, ALU.add).then_inc(S["s_bvm"], 1)
            for i in range(8):
                c, o = divmod(i, 2)
                dve.wait_ge(S["s_mo"], i + 1)
                xc = XT[:, o, 512 * c:512 * c + 512]
                dve.scalar_tensor_tensor(xc, ps[:, 4 + i % 4, :], b2c[:, o:o + 1], xc, ALU.add,
                                         ALU.add).then_inc(S["s_xt0"], 1)
            dve.wait_ge(S["s_xt0"], 8)
            for i in range(8):
                c, o = divmod(i, 2)
                xc = XT[:, o, 512 * c:512 * c + 512]
                dve.tensor_tensor(xc, xc, YT[:, o, 512 * c:512 * c + 512], ALU.add).then_inc(S["s_xt0"], 1)
            dve.wait_ge(S["s_xt0"], 16)
            dve.memset(arena[:, 0:20000], 0.0)
            dve.wait_ge(S["s_lo"], 16)
            link(dve.tensor_copy(base[:, :], LO[:, :]))
            dve.wait_ge(S["s_acc0p"], 1)
            npass = vload(dve)

            regs = [dve.alloc_register(name=f"start{k}") for k in range(GR)]

            def window_starts(t, n):
                dve.load(regs[0:n], baseI[0:1, bass.ds(GR + t, n)])
                return [dve.snap(x, min_val=0, max_val=N) for x in regs[0:n]]

            def windows(done):
                dve.tensor_tensor(dloc[:, 0:ET], dstF[:, :], base[:, :], ALU.subtract)
                dve.tensor_copy(baseI[:, GR:], base[0:1, :]).then_inc(S["s_oh"], 1)
                dve.wait_ge(S["s_oh"], done)

            def next_windows(done):
                dve.tensor_scalar(base[:, :], base[:, :], float(WIN), float(N), ALU.add,
                                  ALU.min).then_inc(S["s_oh"], 1)
                dve.wait_ge(S["s_oh"], done)

            def onehot(out_, t0, count, sem_):
                dve.tensor_tensor(out_, iota8.unsqueeze(1).broadcast_to([P, GR, WIN]),
                                  dloc[:, bass.ds(t0, GR)].unsqueeze(2).broadcast_to([P, GR, WIN]),
                                  ALU.is_equal).then_inc(sem_, 1)
                dve.wait_ge(sem_, count)

            for w_, w2_, w3_ in ((kw1, k2, k3), (kb1r[0:1, :], kb2[0:1, :], kb3[0:1, :])):
                link(dve.tensor_tensor(w2_, w_, top(w_), ALU.subtract))
                link(dve.tensor_tensor(w3_, w2_, top(w2_), ALU.subtract))
            dve.sem_inc(S["s_rmw"], 1)
            dve.sem_inc(S["s_ea"], 1)
            with dve.Fori(0, npass) as j:
                per = 2 + 2 * NG
                dve.memset(ps[:, 4:6, 0:3 * (P + WIN)], 0.0)
                windows(j * per + 1)

                def masks(i, g, step):
                    n = 2 * i + g
                    c = j * per + 1 + 2 * n
                    t0 = i * BODY + g * GR
                    ready = j * NG + n + 1
                    g = g % 2
                    if step == 0:
                        dve.wait_ge(S["s_seg"], j * 2 * ITERS + n + 1)
                        dve.tensor_tensor(SW[:, g, :, :], iota8.unsqueeze(1).broadcast_to([P, GR, WIN]),
                                          dloc[:, bass.ds(t0, GR)].unsqueeze(2).broadcast_to([P, GR, WIN]),
                                          ALU.is_equal).then_inc(S["s_oh"], 1)
                    elif step == 1:
                        dve.wait_ge(S["s_oh"], c + 1)
                        dve.tensor_tensor(SW[:, g, :, :], SW[:, g, :, :],
                                          ewt[:, bass.ds(t0, GR)].unsqueeze(2).broadcast_to([P, GR, WIN]),
                                          ALU.mult).then_inc(S["s_oh"], 1)
                    else:
                        h = step - 2
                        if h == 0:
                            dve.wait_ge(S["s_oh"], c + 2)
                            dve.wait_ge(S["s_rready"], ready)
                        ins = dve.tensor_tensor(
                            RM[:, g, :, h * P:(h + 1) * P].rearrange("p t (w q) -> p t w q", q=16),
                            MR[:, g * GR:(g + 1) * GR, H + 1 + 16 * h:H + 17 + 16 * h]
                            .unsqueeze(2).broadcast_to([P, GR, WIN, 16]),
                            SW[:, g, :, :].unsqueeze(3).broadcast_to([P, GR, WIN, 16]), ALU.mult)
                        if h == 1:
                            ins.then_inc(S["s_mask"], 1)

                def rest(loaded, n, par, step):
                    if step == 0:
                        dve.wait_ge(eal[par], loaded)
                        dve.wait_ge(S["s_er"], j * NG + n + 1)
                        dve.tensor_tensor(EA2[:, par, :], EA[:, par, :], top(EA[:, par, :]),
                                          ALU.subtract).then_inc(S["s_rest"], 1)
                    else:
                        dve.wait_ge(S["s_rest"], j * (NG + 1) + n + 1)
                        dve.tensor_tensor(EA3[:, par, :], EA2[:, par, :], top(EA2[:, par, :]),
                                          ALU.subtract).then_inc(S["s_ea"], 1)

                def add(i, g, t, first):
                    if t == 0:
                        dve.wait_ge(S["s_seg"], j * 2 * ITERS + 2 * i + g + 2)
                    a = acc[:, bass.ds(first[t], WIN), :]
                    v = vacc[:, bass.ds(first[t], WIN)]
                    slot = (1 - g) * GR + t
                    dve.wait_ge(S["s_rmw"], j * (ET + GR) + i * BODY + g * GR + t + 1)
                    dve.tensor_tensor(a, a, outer(slot).rearrange("p (n q) -> p n q", q=16), ALU.add)
                    dve.tensor_tensor(v, v, affine(slot), ALU.add).then_inc(S["s_rmw"], 1)

                for step in range(2):
                    for g in range(2):
                        rest((j * (ITERS + 1) + 1) * 16, g, g, step)
                for step in range(4):
                    masks(0, 0, step)
                with dve.Fori(0, ITERS) as i:
                    for slot in range(BODY):
                        g, pos = divmod(slot, GR)
                        if pos < 4:
                            masks(i, g + 1, pos)
                        if pos == 0:
                            first = window_starts(i * BODY + slot - GR, GR)
                        add(i, g, pos, first)
                        if pos in (2, 3):
                            rest((j * (ITERS + 1) + i + 2) * 16, 2 * i + g + 2, g, pos - 2)
                first = window_starts(ET - GR, GR)
                for t in range(GR):
                    add(ITERS, 0, t, first)
                next_windows(j * per + per)
            dve.drain().then_inc(S["s_base"], 1)
            for i in range(8):
                c, o = divmod(i, 2)
                dve.wait_ge(S["s_mo"], 8 + i + 1)
                xc = XT[:, o, NCH * c:NCH * (c + 1)]
                dve.scalar_tensor_tensor(xc, ps[:, 4 + i % 4, 0:NCH], bns[:, 4 + o:5 + o], xc, ALU.mult,
                                         ALU.add).then_inc(S["s_o0"], 1)
            dve.wait_ge(S["s_o0"], 8)
            for o in range(2):
                ins = dve.tensor_scalar(XT[:, o, 0:N], XT[:, o, 0:N], bnb[:, 4 + o:5 + o], None, ALU.add)
            ins.then_inc(xtd[1], 1)
            layer_norm(1)
            for i in range(8):
                c, o = divmod(i, 2)
                dve.wait_ge(S["s_mo"], 16 + i + 1)
                xc = XT[:, o, 512 * c:512 * c + 512]
                ins = dve.scalar_tensor_tensor(xc, ps[:, 4 + i % 4, :], bfc[:, o:o + 1], xc, ALU.add, ALU.add)
                ins.then_inc(S["s_ff"], 1)
            dve.wait_ge(S["s_ff"], 8)
            dve.sem_inc(xtd[2], 1)
            layer_norm(2)
            dve.wait_ge(S["s_w1"], 16 * NLOAD["s_w1"])
            for k in range(2):
                centre(wkv1[:, k, :], 16, 64)
            dve.sem_inc(S["s_wc"], 1)
            link(dve.tensor_scalar(m4[:, 192:256], m4[:, 192:256], 3.0 ** -0.5, None, ALU.mult))
            for t in range(NT):
                dve.wait_ge(S["s_k1s"], t + 1)
                dve.tensor_reduce(VS1[:, t * 16:(t + 1) * 16], SQ1.rearrange("p (g c) -> p g c", c=64),
                                  AX.X, ALU.add).then_inc(S["s_v1r"], 1)
            dve.wait_ge(S["s_v1r"], NT)
            dve.tensor_scalar(VS1, VS1, 1.0 / 64, EPS, ALU.mult, ALU.add).then_inc(S["s_v1r"], 1)
            dve.wait_ge(S["s_v1std"], 1)
            link(dve.reciprocal(VS1, VS1))
            vsv = VS1.rearrange("p (t u h) -> p t u h", t=NT, u=2)
            link(dve.tensor_tensor(RK1.rearrange("p (t h) -> p t h", h=8), vsv[:, :, 0, :], vsv[:, :, 1, :], ALU.mult))
            for t in range(NT):
                dve.tensor_tensor(KV1[:, t, 8:16, :], KV1[:, t, 8:16, :],
                                  RK1[:, t * 8:(t + 1) * 8].unsqueeze(2).broadcast_to([P, 8, 64]),
                                  ALU.mult).then_inc(S["s_v1n"], 1)
            dve.wait_ge(S["s_kvt1"], 1)
            dve.tensor_tensor(KVM1, ps[:, 4, :].rearrange("p (g c) -> p g c", g=4),
                              mask64.unsqueeze(1).broadcast_to([P, 4, P]), ALU.mult).then_inc(S["s_kvm1"], 1)
            dve.wait_ge(S["s_A1"], 1)
            for h in range(2):
                dve.tensor_copy(AM1[:, 2 * h:2 * h + 2, :].rearrange("p g c -> p (g c)"),
                                ps[:, 5 + h, :]).then_inc(S["s_Am1"], 1)
            dve.wait_ge(S["s_G1"], 1)
            dve.tensor_copy(GM1.rearrange("p g c -> p (g c)"), ps[:, 7, :]).then_inc(S["s_Gm1"], 1)
            for i in range(8):
                c, o = divmod(i, 2)
                dve.wait_ge(S["s_y1"], i + 1)
                xc = XT[:, o, 512 * c:512 * c + 512]
                dve.scalar_tensor_tensor(xc, ps[:, i % 4, :], boc[:, o:o + 1], xc, ALU.add,
                                         ALU.add).then_inc(S["s_xt3"], 1)
            dve.wait_ge(S["s_kvt1"], 1)
            dve.memset(acc1[:, 0:3, :], 0.0).then_inc(S["s_acc1"], 1)
            dve.wait_ge(S["s_acc1"], 2)
            link(dve.tensor_copy(base[:, :], LO[:, :]))
            dve.wait_ge(S["s_utab"], 32)
            dve.sem_inc(S["s_prod"], BP)
            dve.sem_inc(S["s_rmw1"], 1)
            dve.sem_inc(S["s_split"], 1)

            def upper(dst, a):
                return dve.tensor_scalar(dst.bitcast(I32), a.bitcast(I32), HIGH, None, ALU.bitwise_and)

            link(upper(UP12[:, 0:D], m4))
            link(dve.tensor_tensor(m4s[:, 1, :], m4, UP12[:, 0:D], ALU.subtract))
            link(dve.tensor_copy(m4s[:, 0, :], UP12[:, 0:D]))

            with dve.Fori(0, npass) as j:
                per = 2 + 4 * NG
                b0 = npass * (2 + 2 * NG)
                dve.memset(ps[:, 4:6, 0:P], 0.0)
                windows(b0 + j * per + 1)

                def split_half(c, h):
                    if h == 0:
                        dve.wait_ge(S["s_silu"], j * MP + 6 * c + 6)
                        upper(UP12, R3).then_inc(S["s_half"], 1)
                    dve.wait_ge(S["s_half"], j * (ITERS + 1) + c + 1)
                    dve.wait_ge(S["s_T"], j * (PT + 1) + c * BP + 3 + 2 * h)
                    hi, lo = slice(h * H, (h + 1) * H), slice((1 - h) * H, (2 - h) * H)
                    dve.tensor_copy(RS[hi, h, :], UP12[hi, :])
                    dve.tensor_tensor(RS[lo, h, :], R3[hi, :], UP12[hi, :],
                                      ALU.subtract).then_inc(S["s_split"], 1)

                def prepare(i, g, *steps):
                    c = b0 + j * per + 1 + 4 * (2 * i + g)
                    t0 = i * BODY + g * GR
                    sl = slice(g % 2 * GR, (g % 2 + 1) * GR)
                    for step in steps:
                        if step:
                            dve.wait_ge(S["s_oh"], c + step)
                        if step == 0:
                            ins = dve.tensor_tensor(S5[:, sl, 0, :], iota8.unsqueeze(1).broadcast_to([P, GR, WIN]),
                                                    dloc[:, bass.ds(t0, GR)].unsqueeze(2).broadcast_to([P, GR, WIN]),
                                                    ALU.is_equal)
                        elif step == 1:
                            ins = dve.tensor_tensor(S5[:, sl, 1:5, :], S5[:, sl, 0:1, :].broadcast_to([P, GR, 4, WIN]),
                                                    shv[:, bass.ds(t0, GR), :].unsqueeze(3).broadcast_to([P, GR, 4, WIN]),
                                                    ALU.mult)
                        elif step == 2:
                            ins = dve.tensor_tensor(S2[:, sl, :], S5[:, sl, 4, :], S5T[:, sl, 4, :], ALU.subtract)
                        else:
                            ins = dve.tensor_tensor(S3[:, sl, :], S2[:, sl, :], S2T[:, sl, :], ALU.subtract)
                        ins.then_inc(S["s_oh"], 1)

                def add1(i, q, n, first):
                    if n == 0:
                        dve.wait_ge(S["s_seg1"], j * PT + i * BP + q + BP)
                    T = 2 * q - 2 + n
                    a = acc1[:, :, bass.ds(first[n], WIN)]
                    dve.wait_ge(S["s_rmw1"], j * (ET + AHEAD) + i * BODY + T + 3)
                    dve.tensor_tensor(a, a, sums(T), ALU.add).then_inc(S["s_rmw1"], 1)

                def pair(i2, q):
                    u, p = divmod(q, BP)
                    i = 2 * i2 + u
                    m = i * BP + p
                    c = (j * PT + m) * 6
                    s_ = slice(2 * p, 2 * p + 2)
                    tp = weights_of(q).rearrange("p (s b c) -> p s b c", s=2, b=4)
                    x = G1[:, s_, :].rearrange("p s (b c) -> p s b c", b=4)

                    def step(ins):
                        ins.then_inc(S["s_part"], 1)

                    if p in (0, 2):
                        dve.wait_ge(S["s_oh"], b0 + j * per + 1 + 4 * (2 * i + 1 + p // 2))
                    dve.wait_ge(S["s_xs"], j * (PT + 1) + m + 2)
                    step(dve.tensor_tensor(XS[:, s_, 1, :], XS[:, s_, 1, :], XS[:, s_, 2, :], ALU.add))
                    dve.wait_ge(S["s_T"], j * (PT + 1) + m + BP + 1)
                    step(dve.tensor_tensor(PP[:, s_, 2:5, :], tp[:, :, 2:3, :].broadcast_to([P, 2, 3, H]), x[:, :, 1:4, :],
                                           ALU.mult))
                    first = window_starts(i2 * 2 * BODY + 2 * q - AHEAD, 2)
                    dve.wait_ge(S["s_part"], c + 1)
                    step(dve.tensor_tensor(XS[:, s_, 1, :], XS[:, s_, 1, :], XS[:, s_, 3, :], ALU.add))
                    dve.tensor_tensor(PP[:, s_, 1, :], tp[:, :, 1, :], x[:, :, 0, :], ALU.mult)
                    dve.wait_ge(S["s_part"], c + 2)
                    step(dve.tensor_tensor(P2[:, s_, :].rearrange("p s (b c) -> p s b c", b=2), PP[:, s_, 2:4, :],
                                           PPT[:, s_, 2:4, :], ALU.subtract))
                    dve.wait_ge(S["s_part"], c + 3)
                    step(dve.tensor_tensor(TU, tp[:, :, 0:4:3, :], XS[:, s_, 0:2, :], ALU.mult))
                    add1(2 * i2, q, 0, first)
                    dve.wait_ge(S["s_part"], c + 4)
                    step(dve.tensor_tensor(P3[:, s_, :], P2[:, s_, :], P2T[:, s_, :], ALU.subtract))
                    dve.wait_ge(S["s_part"], c + 5)
                    dve.tensor_tensor(PP[:, s_, 0, :], TU[:, :, 0, :], TU[:, :, 1, :], ALU.add).then_inc(S["s_prod"], 1)
                    add1(2 * i2, q, 1, first)

                split_half(0, 0)
                prepare(0, 0, *range(4))
                with dve.Fori(0, ITERS // 2) as i2:
                    for q in range(2 * BP):
                        u, p = divmod(q, BP)
                        i = 2 * i2 + u
                        if p in (1, 4):
                            prepare(i, (p + 2) // 3, 1)
                        pair(i2, q)
                        if p in (1, 4):
                            prepare(i, (p + 2) // 3, 2)
                        if p in (1, 4):
                            prepare(i, (p + 2) // 3, 3)
                        if p == 0:
                            split_half(i, 1)
                            prepare(i, 1, 0)
                        if p == 3:
                            split_half(i + 1, 0)
                            prepare(i, 2, 0)
                first = window_starts(ET - AHEAD, 2)
                for t in range(2):
                    add1(ITERS, 0, t, first)
                next_windows(b0 + j * per + per)
            dve.drain().then_inc(S["s_base1"], 1)
            dve.wait_ge(S["s_w4"], 16 * NLOAD["s_w4"])
            t0, t1, t2, t3 = TMP

            def W(v):
                return wc[:, v, :].unsqueeze(1).broadcast_to([P, NT // 2, 64])

            def tt(o, a, b, op):
                link(dve.tensor_tensor(o, a, b, op))
            for h in range(2):
                A_ = AR[:, h * NT // 2:(h + 1) * NT // 2, :, :]
                B_ = BR[:, h * NT // 2:(h + 1) * NT // 2, :, :]
                A0 = A_[:, :, 0, :]
                dve.wait_ge(S["s_are"], 4 * h + 4)
                tt(t0, A_[:, :, 1, :], A_[:, :, 1, :], ALU.mult)
                tt(t1, A_[:, :, 2, :], A_[:, :, 2, :], ALU.mult)
                tt(t0, t0, t1, ALU.add)
                tt(t1, A_[:, :, 3, :], A_[:, :, 3, :], ALU.mult)
                tt(t0, t0, t1, ALU.add)
                tt(t1, A0, A0, ALU.mult)
                tt(t2, A0, W(1), ALU.mult)
                tt(t2, t2, W(0), ALU.add)
                tt(t3, t1, W(3), ALU.mult)
                tt(t2, t2, t3, ALU.add)
                tt(t3, t0, W(4), ALU.mult)
                tt(t2, t2, t3, ALU.add)
                tt(t2, t2, A0, ALU.mult)
                tt(t3, t0, W(2), ALU.mult)
                tt(B_[:, :, 0, :], t2, t3, ALU.add)
                tt(t2, A0, W(6), ALU.mult)
                tt(t2, t2, W(5), ALU.add)
                tt(t3, t1, W(7), ALU.mult)
                tt(t2, t2, t3, ALU.add)
                tt(t3, t0, W(8), ALU.mult)
                tt(t2, t2, t3, ALU.add)
                for x in range(3):
                    ins = dve.tensor_tensor(B_[:, :, 1 + x, :], A_[:, :, 1 + x, :], t2, ALU.mult)
                ins.then_inc(S["s_b"], 1)
            dve.wait_ge(S["s_oe"], 8)
            for k in range(2):
                for c in range(4):
                    ins = dve.bn_stats(sto[:, k, c, :], OT[:, k, c * NCH:(c + 1) * NCH])
            link(ins)
            for k in range(2):
                ins = dve.bn_aggr(mvo[:, k, :], sto[:, k, :, :].rearrange("p c s -> p (c s)"))
            link(ins)
            link(dve.tensor_tensor(ss, mvo[:, :, 0], mvo[:, :, 0], ALU.mult))
            dve.tensor_tensor(ss, ss, mvo[:, :, 1], ALU.add).then_inc(S["s_nr"], 1)
            dve.wait_ge(S["s_nre"], 1)
            link(dve.tensor_copy(nrm, ps[:, 0, 0:2]))
            link(dve.tensor_copy(nrm[0:H, 0:1], mvo[0:H, 0, 1:2]))
            dve.tensor_scalar(nrm, nrm, EPS, None, ALU.add).then_inc(S["s_nvar"], 1)
            dve.wait_ge(S["s_nstd"], 1)
            link(dve.reciprocal(osc, nrm))
            link(dve.tensor_tensor(osc, osc, l1v[:, 0, :], ALU.mult))
            link(dve.tensor_tensor(obi, mvo[:, :, 0], osc, ALU.mult))
            link(dve.tensor_tensor(obi, obi, l1v[:, 2, :], ALU.mult))
            link(dve.tensor_tensor(obi, l1v[:, 1, :], obi, ALU.subtract))
            dve.tensor_copy(wrb, wr.unsqueeze(2).broadcast_to([P, 2, P]))
            for c in range(4):
                for k in range(2):
                    xc = XT[:, k, 512 * c:512 * c + 512]
                    ins = dve.scalar_tensor_tensor(xc, OT[:, k, 512 * c:512 * c + 512], osc[:, k:k + 1], xc, ALU.mult,
                                                   ALU.add)
                n[0] += 1
                ins.then_inc(S["s_dve"], 1)
            for c in range(4):
                dve.wait_ge(S["s_dve"], n[0] - 3 + c)
                for k in range(2):
                    xc = XT[:, k, 512 * c:512 * c + 512]
                    ins = dve.tensor_scalar(xc, xc, obi[:, k:k + 1], None, ALU.add)
                ins.then_inc(xtd[3], 1)
            layer_norm(3)
            for i in range(4):
                dve.wait_ge(S["s_wct"], i + 1)
                dve.tensor_copy(wcol[:, 4 * i:4 * i + 4],
                                ps[:, 4 + i, :].rearrange("p (t c) -> p t c", c=P)[:, :, 0]).then_inc(S["s_wcol"], 1)
            dve.wait_ge(S["s_wcol"], 4)
            link(dve.memset(cnt3[:, 0, 0:1], 0.0))
            for t in range(NT):
                w = wcol[:, t:t + 1]
                if t:
                    link(dve.tensor_scalar(junk[:, 0:t * P], WB[:, 0:t * P], w, 0.0, ALU.is_ge, ALU.add,
                                           accum_out=cnt3[:, 0, t:t + 1]))
                link(dve.tensor_scalar(junk[:, t * P:N], WB[:, t * P:N], w, 0.0, ALU.is_gt, ALU.add,
                                       accum_out=cnt3[:, 1, t:t + 1]))
                link(dve.scalar_tensor_tensor(junk[:, 0:P], WB[:, t * P:(t + 1) * P], w, ltm, ALU.is_equal, ALU.mult,
                                              accum_out=cnt3[:, 2, t:t + 1]))
            link(dve.tensor_tensor(mw, cnt3[:, 0, :], cnt3[:, 1, :], ALU.add))
            link(dve.tensor_tensor(mw, mw, cnt3[:, 2, :], ALU.add))
            link(dve.tensor_scalar(mw, mw, float(SEL), None, ALU.is_lt))
            link(dve.tensor_tensor(mw, mw, wcol, ALU.mult))
            for t in range(NT):
                dve.wait_ge(S["s_yy"], t + 1)
                o = OUTR[:, t, :]
                link(dve.tensor_tensor(o, ps[:, 4 + t % 4, 0:D], fb2, ALU.add))
                link(dve.scalar_tensor_tensor(o, o, mw[:, t:t + 1], ROW[:, t, :], ALU.mult, ALU.add))
                dve.tensor_tensor(o, o, YROW[:, t, :], ALU.add).then_inc(S["s_out"], 1)


def kernel(**inputs):
    import numpy as np
    import concourse.bacc as _bacc
    from concourse.bass_utils import run_bass_kernel_spmd as _run

    I = {k: np.asarray(v) for k, v in inputs.items()}
    perm = np.concatenate([np.arange(64)] + [64 + 3 * np.arange(64) + x for x in range(3)])

    def kt(a):
        k = a.shape[0] // 128
        return np.ascontiguousarray(a.reshape(k, 128, -1).transpose(1, 0, 2).reshape(128, -1))

    def colv(v):
        return np.ascontiguousarray(v.reshape(-1, 128).T)

    def twice(v):
        return np.concatenate([v, v])

    def blocks(parts):
        a = np.zeros((128, 2, 128), np.float32)
        for n, b in enumerate(parts):
            r = 64 * (n % 2)
            a[r:r + 64, n // 2, r:r + 64] = b
        return a.reshape(128, 256)

    A = {}
    x = I["x"][:, perm]
    A["x"] = np.ascontiguousarray(x)
    A["xT"] = np.ascontiguousarray(x.T)
    A["src_l"] = np.zeros((P, ET + GR), np.int32)
    A["src_l"][:, :ET] = I["src"].reshape(ET, P).T
    A["dst_l"] = np.ascontiguousarray(I["dst"].reshape(ET, P).T)
    A["dst_r"] = np.ascontiguousarray(I["dst"].reshape(125, 4 * P))
    A["ew"] = np.ascontiguousarray(I["edge_weight"].reshape(ET, P).T)
    A["sh"] = np.zeros((P, (ET + GR) * 4), np.float32)
    A["sh"][:, :ET * 4] = I["edge_attr_4"][:, [1, 2, 3, 0]].reshape(ET, P, 4).transpose(1, 0, 2).reshape(P, ET * 4)
    ea = np.zeros((P, (2 * ITERS + 2) * GE), np.float32)
    ea[:, :E] = I["edge_attr_128"].T
    A["eaT"] = ea
    rb = np.zeros(((ITERS + 2) * 2 * GE, 16), np.float32)
    rb[:E] = I["edge_attr_16"]
    A["rbf"] = np.ascontiguousarray(rb.reshape(ITERS + 2, 2, GE, 16).transpose(0, 1, 3, 2).reshape(-1, GE))
    A["ident"] = np.eye(128, dtype=np.float32)
    A["iota8"] = np.tile(np.arange(WIN, dtype=np.float32), (128, 1))
    A["ones"] = np.ones((128, 128), np.float32)
    A["mask32"] = np.kron(np.eye(4), np.ones((32, 32))).astype(np.float32) / np.float32(N)
    A["mask64"] = np.kron(np.eye(2), np.ones((64, 64))).astype(np.float32) / np.float32(N)
    A["ltm"] = np.tril(np.ones((128, 128), np.float32), -1)
    pat = np.zeros((2, 128, 2, 128), np.float32)
    for k in range(2):
        for o in range(2):
            for a in range(2):
                for b in range(2):
                    if (k, a) != (0, 0) and (o, b) != (0, 0):
                        pat[k, 64 * a:64 * a + 64, o, 64 * b:64 * b + 64] = np.eye(64) / 3
    A["pat"] = np.ascontiguousarray(pat.transpose(1, 0, 2, 3).reshape(128, 512))
    g = lambda n: I["L0_gnn_" + n]
    vec = []
    for a in ("g", "be", "m", "v"):
        vec.append(np.concatenate([colv(g(a + "_in")[perm]), colv(twice(g(a + "_msg"))), colv(twice(g(a + "_upd"))),
                                   colv(g(a + "_out")[perm])], 1))
    z2 = np.zeros((128, 2), np.float32)
    vec.append(np.concatenate([z2, colv(twice(g("b1"))), z2[:, :1], colv(g("b2")[perm])], 1))
    A["bnv"] = np.concatenate(vec, 1)
    A["w1g"] = kt(g("w1")[perm])
    A["kw1"] = g("kw1")
    A["kb1r"] = g("kb1")[None]
    A["w2g"] = np.tile(g("w2")[:, perm], (2, 1))
    kw2 = g("kw2").reshape(KH, H + 1, H)
    kb2 = g("kb2").reshape(H + 1, H)
    A["W2S"] = np.ascontiguousarray(kw2[:, 1:, :].reshape(2, 16, H, H).transpose(0, 3, 1, 2).reshape(128, 16 * H))
    A["wV"] = np.concatenate([np.zeros((31, H), np.float32), kb2[:1], kw2[:, 0, :], kb2[1:].T], 0)
    m = lambda n: I["L0_mix_" + n]
    wq = m("w_qkv")[perm].reshape(D, 8, 3, 32)
    bq = m("b_qkv").reshape(8, 3, 32)
    A["wqT"] = kt(np.ascontiguousarray(wq[:, :, 0].reshape(D, D).T))
    A["bq"] = colv(bq[:, 0].reshape(-1))
    A["wkv"] = kt(np.concatenate([wq[:, :, 1].reshape(D, D), wq[:, :, 2].reshape(D, D)], 1))
    A["bkvr"] = np.concatenate([bq[:, 1].reshape(-1), bq[:, 2].reshape(-1)])[None]
    A["gkv"] = np.tile(np.concatenate([np.tile(m("kln_g"), 8), np.tile(m("vln_g"), 8)]), (128, 1))
    A["bkv"] = np.tile(np.concatenate([np.tile(m("kln_b"), 8), np.tile(m("vln_b"), 8)]), (128, 1))
    A["w1m"] = kt(m("w1"))
    A["w1p"] = kt(m("w1")[perm])
    A["w2m"] = kt(np.ascontiguousarray(m("w2")[:, perm]))
    A["b1c"] = colv(m("b1"))
    A["b2c"] = colv(m("b2")[perm])
    A["wfT"] = kt(np.ascontiguousarray(I["L0_ffn_weight"].T[perm][:, perm]))
    A["bfc"] = colv(I["L0_ffn_bias"][perm])
    g1 = lambda n: I["L1_gnn_" + n]
    A["bu"] = blocks([g1("W_up0")] + [g1("W_up1")] * 3)
    A["bdb"] = blocks([g1("WB0")] + [g1("WB1")] * 3)
    A["bds"] = blocks([g1("Wsc0")] + [g1("Wsc1")] * 3)

    def two(w):
        a = np.zeros((2 * w.shape[0], 128), np.float32)
        a[:w.shape[0], :64] = w
        a[w.shape[0]:, 64:] = w
        return a
    A["m1"], A["m2"], A["m3"] = two(g1("M1")), two(g1("M2")), two(g1("M3"))
    A["m4"] = np.tile(g1("M4"), (2, 1))
    wl = np.zeros((2, 64, NA, 4, 64), np.float32)
    w0, w1 = g1("W_lin0"), g1("W_lin1")
    wl[0, :, 0, 0] = w0
    for half, h, c in ((1, 1, 1), (1, 2, 2), (1, 3, 3), (0, 4, 1), (1, 4, 2), (0, 5, 3)):
        wl[half, :, h, c] = w1
    A["wl"] = wl.reshape(128, NA * D)
    A["wc"] = np.tile(np.concatenate([g1("Wc0").T.reshape(-1), g1("Wc1").T.reshape(-1)]), (128, 1))
    gam = np.concatenate([g1("gamma0")] + [g1("gamma1")] * 3)
    bet = np.concatenate([g1("beta0"), np.zeros(192, np.float32)])
    is0 = np.concatenate([np.ones(64, np.float32), np.zeros(192, np.float32)])
    A["l1v"] = np.concatenate([colv(gam), colv(bet), colv(is0)], 1)
    Wqkv = I["L1_mix_Wqkv"][:, perm]
    A["wq1"] = kt(Wqkv[0:512])
    A["wkv1"] = kt(np.ascontiguousarray(Wqkv[512:].T))
    A["woT"] = kt(np.ascontiguousarray(I["L1_mix_Wout"][perm].T))
    A["boc"] = colv(I["L1_mix_bout"][perm])
    f = lambda n: I["L1_ffn_" + n]
    A["wr"] = colv(f("wr")[perm, 0])
    A["brc"] = np.tile(f("br"), (128, 1))
    A["fw1"] = kt(f("w1")[perm])
    A["fb1"] = colv(f("b1"))
    A["fw2"] = kt(np.ascontiguousarray(f("w2")[:, perm]))
    A["fb2"] = np.tile(f("b2")[perm], (128, 1))

    nc = _bacc.Bacc("TRN2", target_bir_lowering=False, num_devices=1)
    arrays, aps = {}, {}
    for name, a in A.items():
        a = np.ascontiguousarray(a)
        assert a.dtype in (np.float32, np.int32), (name, a.dtype)
        arrays["in_" + name] = a
        aps[name] = nc.dram_tensor("in_" + name, a.shape, mybir.dt.from_np(a.dtype), kind="ExternalInput").ap()
    out = nc.dram_tensor("out_0", (N, D), F32, kind="ExternalOutput").ap()
    build(nc, aps, out)
    r = _run(nc, [arrays], core_ids=[0])
    got = r.results[0]["out_0"]
    inv = np.argsort(perm)
    return np.ascontiguousarray(got[:, inv])
```
